# Optimizing a Trainium2 kernel written in Bass

```python
import numpy as np
import jax
import jax.numpy as jnp

def _softmax(x, axis=-1):
    return jax.nn.softmax(x, axis=axis)

def _gelu(x):
    return jax.nn.gelu(x, approximate=True)

def _silu(x):
    return jax.nn.silu(x)

def _sigmoid(x):
    return jax.nn.sigmoid(x)

def _layernorm(x, axis=-1, eps=1e-05):
    m = jnp.mean(x, axis=axis, keepdims=True)
    v = jnp.var(x, axis=axis, keepdims=True)
    return (x - m) / jnp.sqrt(v + eps)

def _scatter_add(tgt, idx, src, axis=0):
    return tgt.at[idx].add(src)

def _segment_sum(src, seg, n):
    return jax.ops.segment_sum(src, seg, n)
kernel_name = 'mk_adaln_d4_jaxref_r8_779119'

def setup_inputs(seed: int=0):
    np.random.seed(seed)
    _w = jnp.asarray

    def _L0_attn_setup():
        import jax, jax.numpy as jnp
        import numpy as np
        H = 64
        HK = 8
        HD = 64
        DM = 128
        WINDOW = 128
        key = jax.random.key(seed)
        ks = jax.random.split(key, 9)
        B, S = (2, 128)
        s = 0.02
        return {'x': jax.random.normal(ks[0], (B, S, DM), jnp.float32), 'Wq': jax.random.normal(ks[1], (H * HD, DM), jnp.float32) * s, 'bq': jax.random.normal(ks[2], (H * HD,), jnp.float32) * s, 'Wk': jax.random.normal(ks[3], (HK * HD, DM), jnp.float32) * s, 'bk': jax.random.normal(ks[4], (HK * HD,), jnp.float32) * s, 'Wv': jax.random.normal(ks[5], (HK * HD, DM), jnp.float32) * s, 'bv': jax.random.normal(ks[6], (HK * HD,), jnp.float32) * s, 'Wo': jax.random.normal(ks[7], (DM, H * HD), jnp.float32) * s, 'bo': jax.random.normal(ks[8], (DM,), jnp.float32) * s, 'sinks': jnp.ones((H,), jnp.float32)}
    _L0_attn_in = _L0_attn_setup()

    def _L0_ffn_setup():
        import jax, jax.numpy as jnp
        import numpy as np
        H = 128
        M = 64
        E = 16
        TOP_K = 4
        N_GROUP = 4
        TOPK_GROUP = 2
        SCALE = 2.5
        B, S = (2, 128)

        def _gate(x2d, gate_kernel, gate_bias):
            n = x2d.shape[0]
            logits = jnp.dot(x2d.astype(jnp.float32), gate_kernel.astype(jnp.float32))
            scores = jax.nn.sigmoid(logits)
            scores_for_choice = scores + gate_bias
            group_scores = scores_for_choice.reshape(n, N_GROUP, E // N_GROUP)
            top2 = jax.lax.top_k(group_scores, k=2)[0]
            group_sum = jnp.sum(top2, axis=-1)
            group_idx = jax.lax.top_k(group_sum, k=TOPK_GROUP)[1]
            group_mask = jnp.zeros_like(group_sum).at[jnp.arange(n)[:, None], group_idx].set(1.0)
            score_mask = jnp.repeat(group_mask[:, :, None], E // N_GROUP, axis=2).reshape(n, E)
            masked_scores = jnp.where(score_mask > 0, scores_for_choice, 0.0)
            topk_weight, topk_idx = jax.lax.top_k(masked_scores, k=TOP_K)
            topk_weight = topk_weight / (jnp.sum(topk_weight, axis=-1, keepdims=True) + 1e-20)
            topk_weight = topk_weight * SCALE
            return (topk_idx, topk_weight)
        key = jax.random.key(seed)
        ks = jax.random.split(key, 9)
        sc_h = 1.0 / np.sqrt(H)
        sc_m = 1.0 / np.sqrt(M)
        return {'hidden_states': jax.random.normal(ks[0], (B, S, H), jnp.float32), 'gate_kernel': jax.random.normal(ks[1], (H, E), jnp.float32) * sc_h, 'gate_bias': jax.random.normal(ks[2], (E,), jnp.float32) * 0.01, 'w_gate': jax.random.normal(ks[3], (E, H, M), jnp.float32) * sc_h, 'w_up': jax.random.normal(ks[4], (E, H, M), jnp.float32) * sc_h, 'w_down': jax.random.normal(ks[5], (E, M, H), jnp.float32) * sc_m, 'sw_gate': jax.random.normal(ks[6], (H, 2 * M), jnp.float32) * sc_h, 'sw_up': jax.random.normal(ks[7], (H, 2 * M), jnp.float32) * sc_h, 'sw_down': jax.random.normal(ks[8], (2 * M, H), jnp.float32) * (1.0 / np.sqrt(2 * M))}
    _L0_ffn_in = _L0_ffn_setup()
    _L0_c = _w((lambda *s: np.random.randn(*s).astype(np.float32) * 0.05)(16, 128))
    _L0_wmod = _w((lambda *s: np.random.randn(*s).astype(np.float32) * 0.05)(128, 6 * 128) * 128 ** (-0.5))

    def _L1_attn_setup():
        import jax, jax.numpy as jnp
        import numpy as np
        B, T, C = (2, 256, 128)
        LAT = 32
        N_HEAD = 16
        HEAD_DIM = C // N_HEAD
        SCALE = 1.0 / np.sqrt(HEAD_DIM).astype(np.float32)
        key = jax.random.key(seed)
        ks = jax.random.split(key, 9)
        s_in = 0.02
        return {'x': jax.random.normal(ks[0], (B, T, C), dtype=jnp.float32), 'wq_lat': jax.random.normal(ks[1], (C, LAT), dtype=jnp.float32) * s_in, 'wk_lat': jax.random.normal(ks[2], (C, LAT), dtype=jnp.float32) * s_in, 'wv_lat': jax.random.normal(ks[3], (C, LAT), dtype=jnp.float32) * s_in, 'wq_heads': jax.random.normal(ks[4], (LAT, C), dtype=jnp.float32) * s_in, 'wk_heads': jax.random.normal(ks[5], (LAT, C), dtype=jnp.float32) * s_in, 'wv_heads': jax.random.normal(ks[6], (LAT, C), dtype=jnp.float32) * s_in, 'w_proj': jax.random.normal(ks[7], (C, C), dtype=jnp.float32) * s_in, 'b_proj': jnp.zeros((C,), dtype=jnp.float32)}
    _L1_attn_in = _L1_attn_setup()

    def _L1_ffn_setup():
        import jax, jax.numpy as jnp
        import numpy as np
        T, Z, D_DIM = (8, 256, 128)
        N_EXP, P_SLOT, H = (64, 32, 128)
        LN_EPS = 1e-05
        key = jax.random.key(seed)
        k = jax.random.split(key, 5)
        s = 0.02
        return {'x': jax.random.normal(k[0], (T, Z, D_DIM), dtype=jnp.float32), 'phi_w': jax.random.normal(k[1], (N_EXP * P_SLOT, D_DIM), dtype=jnp.float32) * s, 'phi_b': jax.random.normal(k[2], (N_EXP * P_SLOT,), dtype=jnp.float32) * s, 'expert_w': jax.random.normal(k[3], (N_EXP, D_DIM, H), dtype=jnp.float32) * s, 'expert_b': jax.random.normal(k[4], (N_EXP, H), dtype=jnp.float32) * s}
    _L1_ffn_in = _L1_ffn_setup()
    _L1_c = _w((lambda *s: np.random.randn(*s).astype(np.float32) * 0.05)(16, 128))
    _L1_wmod = _w((lambda *s: np.random.randn(*s).astype(np.float32) * 0.05)(128, 6 * 128) * 128 ** (-0.5))

    def _L2_attn_setup():
        import jax, jax.numpy as jnp
        import numpy as np
        B, T, C = (8, 256, 128)
        HS = 64
        H = C // HS
        LORA_R = 32
        TD_R = 64

        def _wkv6(r, k, v, w, u):
            n = r.shape[-1]
            decay = jnp.exp(-jnp.exp(w))

            def per_head(rt, kt, vt, dt, uh):

                def step(S, inp):
                    ri, ki, vi, di = inp
                    kv = ki[:, None] * vi[None, :]
                    y = ri @ (S + uh[:, None] * kv)
                    S = di[:, None] * S + kv
                    return (S, y)
                S0 = jnp.zeros((n, n), rt.dtype)
                _, ys = jax.lax.scan(step, S0, (rt, kt, vt, dt))
                return ys
            f = jax.vmap(per_head, in_axes=(0, 0, 0, 0, 0))
            f = jax.vmap(f, in_axes=(0, 0, 0, 0, None))
            return f(r, k, v, decay, u)
        key = jax.random.key(seed)
        ks = jax.random.split(key, 20)
        inp = {'x': jax.random.normal(ks[0], (B, T, C), jnp.float32), 'miu_x': jax.random.uniform(ks[1], (1, 1, C), jnp.float32), 'lambda_': jax.random.uniform(ks[2], (5, 1, 1, C), jnp.float32), 'A_lora': jax.random.normal(ks[3], (C, LORA_R * 5), jnp.float32) * 0.01, 'B_lora': jax.random.normal(ks[4], (5, LORA_R, C), jnp.float32) * 0.01, 'td_miu': -6.0 + 5.0 * jax.random.uniform(ks[5], (1, 1, C), jnp.float32), 'td_A': jax.random.normal(ks[6], (C, TD_R), jnp.float32) * 0.01, 'td_B': jax.random.normal(ks[7], (TD_R, C), jnp.float32) * 0.01, 'u': jax.random.normal(ks[8], (H, HS), jnp.float32) * 0.1, 'Wr': jax.random.normal(ks[9], (C, C), jnp.float32) * 0.02, 'Wk': jax.random.normal(ks[10], (C, C), jnp.float32) * 0.02, 'Wv': jax.random.normal(ks[11], (C, C), jnp.float32) * 0.02, 'Wg': jax.random.normal(ks[12], (C, C), jnp.float32) * 0.02, 'Wo': jax.random.normal(ks[13], (C, C), jnp.float32) * 0.02, 'gn_gamma': jnp.ones((C,), jnp.float32), 'gn_beta': jnp.zeros((C,), jnp.float32)}
        return inp
    _L2_attn_in = _L2_attn_setup()

    def _L2_ffn_setup():
        import jax, jax.numpy as jnp
        import numpy as np
        TOPK = 4
        N_GROUPS = 4
        TOPK_GROUPS = 2
        ROUTE_SCALE = 2.5

        def _gate(x2, Wg):
            T = x2.shape[0]
            E = Wg.shape[0]
            scores = x2 @ Wg.T
            s = jax.nn.sigmoid(scores)
            g = s.reshape(T, N_GROUPS, E // N_GROUPS)
            group_scores = g.max(axis=-1)
            _, gidx = jax.lax.top_k(group_scores, TOPK_GROUPS)
            group_mask = jnp.any(jax.nn.one_hot(gidx, N_GROUPS, dtype=jnp.bool_), axis=1)
            masked = jnp.where(group_mask[:, :, None], g, -jnp.inf).reshape(T, E)
            _, idx = jax.lax.top_k(masked, TOPK)
            w = jnp.take_along_axis(s, idx, axis=1)
            w = w / jnp.sum(w, axis=-1, keepdims=True)
            w = w * ROUTE_SCALE
            return (w.astype(x2.dtype), idx)
        key = jax.random.key(seed)
        ks = jax.random.split(key, 6)
        B, S, D, I, E = (2, 256, 128, 128, 16)
        scale = 0.02
        return {'x': jax.random.normal(ks[0], (B, S, D), dtype=jnp.float32), 'Wg': jax.random.normal(ks[1], (E, D), dtype=jnp.float32) * scale, 'W1': jax.random.normal(ks[2], (E, I, D), dtype=jnp.float32) * scale, 'b1': jnp.zeros((E, I), dtype=jnp.float32), 'W2': jax.random.normal(ks[3], (E, D, I), dtype=jnp.float32) * scale, 'b2': jnp.zeros((E, D), dtype=jnp.float32), 'W3': jax.random.normal(ks[4], (E, I, D), dtype=jnp.float32) * scale, 'b3': jnp.zeros((E, I), dtype=jnp.float32)}
    _L2_ffn_in = _L2_ffn_setup()
    _L2_c = _w((lambda *s: np.random.randn(*s).astype(np.float32) * 0.05)(16, 128))
    _L2_wmod = _w((lambda *s: np.random.randn(*s).astype(np.float32) * 0.05)(128, 6 * 128) * 128 ** (-0.5))

    def _L3_attn_setup():
        import jax, jax.numpy as jnp
        import numpy as np
        D_MODEL = 128
        N_HEADS = 16
        HEAD_DIM = D_MODEL // N_HEADS
        key = jax.random.key(seed)
        ks = jax.random.split(key, 9)
        B, S = (4, 256)
        x = jax.random.normal(ks[0], (B, S, D_MODEL), dtype=jnp.float32)
        init = 1.0 / np.sqrt(D_MODEL)

        def lin(kw, kb):
            W = jax.random.uniform(kw, (D_MODEL, D_MODEL), jnp.float32, -init, init)
            b = jax.random.uniform(kb, (D_MODEL,), jnp.float32, -init, init)
            return (W, b)
        Wq, bq = lin(ks[1], ks[2])
        Wk, bk = lin(ks[3], ks[4])
        Wv, bv = lin(ks[5], ks[6])
        Wo, bo = lin(ks[7], ks[8])
        return {'x': x, 'Wq': Wq, 'bq': bq, 'Wk': Wk, 'bk': bk, 'Wv': Wv, 'bv': bv, 'Wo': Wo, 'bo': bo}
    _L3_attn_in = _L3_attn_setup()

    def _L3_ffn_setup():
        import jax, jax.numpy as jnp
        import numpy as np
        B, T, C, H, E = (4, 256, 128, 256, 8)
        CAPACITY_FACTOR = 1.0
        key = jax.random.key(seed)
        ks = jax.random.split(key, 5)
        scale = 0.02
        return {'x': jax.random.normal(ks[0], (B, T, C), dtype=jnp.float32), 'Wg': jax.random.normal(ks[1], (E, C), dtype=jnp.float32) * scale, 'W1': jax.random.normal(ks[2], (E, H, C), dtype=jnp.float32) * scale, 'W2': jax.random.normal(ks[3], (E, C, H), dtype=jnp.float32) * scale, 'W3': jax.random.normal(ks[4], (E, H, C), dtype=jnp.float32) * scale}
    _L3_ffn_in = _L3_ffn_setup()
    _L3_c = _w((lambda *s: np.random.randn(*s).astype(np.float32) * 0.05)(16, 128))
    _L3_wmod = _w((lambda *s: np.random.randn(*s).astype(np.float32) * 0.05)(128, 6 * 128) * 128 ** (-0.5))
    _d = {'L0_attn_x': _L0_attn_in['x'], 'L0_attn_Wq': _L0_attn_in['Wq'], 'L0_attn_bq': _L0_attn_in['bq'], 'L0_attn_Wk': _L0_attn_in['Wk'], 'L0_attn_bk': _L0_attn_in['bk'], 'L0_attn_Wv': _L0_attn_in['Wv'], 'L0_attn_bv': _L0_attn_in['bv'], 'L0_attn_Wo': _L0_attn_in['Wo'], 'L0_attn_bo': _L0_attn_in['bo'], 'L0_attn_sinks': _L0_attn_in['sinks'], 'L0_ffn_gate_kernel': _L0_ffn_in['gate_kernel'], 'L0_ffn_gate_bias': _L0_ffn_in['gate_bias'], 'L0_ffn_w_gate': _L0_ffn_in['w_gate'], 'L0_ffn_w_up': _L0_ffn_in['w_up'], 'L0_ffn_w_down': _L0_ffn_in['w_down'], 'L0_ffn_sw_gate': _L0_ffn_in['sw_gate'], 'L0_ffn_sw_up': _L0_ffn_in['sw_up'], 'L0_ffn_sw_down': _L0_ffn_in['sw_down'], 'L0_c': _L0_c, 'L0_wmod': _L0_wmod, 'L1_attn_wq_lat': _L1_attn_in['wq_lat'], 'L1_attn_wk_lat': _L1_attn_in['wk_lat'], 'L1_attn_wv_lat': _L1_attn_in['wv_lat'], 'L1_attn_wq_heads': _L1_attn_in['wq_heads'], 'L1_attn_wk_heads': _L1_attn_in['wk_heads'], 'L1_attn_wv_heads': _L1_attn_in['wv_heads'], 'L1_attn_w_proj': _L1_attn_in['w_proj'], 'L1_attn_b_proj': _L1_attn_in['b_proj'], 'L1_ffn_phi_w': _L1_ffn_in['phi_w'], 'L1_ffn_phi_b': _L1_ffn_in['phi_b'], 'L1_ffn_expert_w': _L1_ffn_in['expert_w'], 'L1_ffn_expert_b': _L1_ffn_in['expert_b'], 'L1_c': _L1_c, 'L1_wmod': _L1_wmod, 'L2_attn_miu_x': _L2_attn_in['miu_x'], 'L2_attn_lambda_': _L2_attn_in['lambda_'], 'L2_attn_A_lora': _L2_attn_in['A_lora'], 'L2_attn_B_lora': _L2_attn_in['B_lora'], 'L2_attn_td_miu': _L2_attn_in['td_miu'], 'L2_attn_td_A': _L2_attn_in['td_A'], 'L2_attn_td_B': _L2_attn_in['td_B'], 'L2_attn_u': _L2_attn_in['u'], 'L2_attn_Wr': _L2_attn_in['Wr'], 'L2_attn_Wk': _L2_attn_in['Wk'], 'L2_attn_Wv': _L2_attn_in['Wv'], 'L2_attn_Wg': _L2_attn_in['Wg'], 'L2_attn_Wo': _L2_attn_in['Wo'], 'L2_attn_gn_gamma': _L2_attn_in['gn_gamma'], 'L2_attn_gn_beta': _L2_attn_in['gn_beta'], 'L2_ffn_Wg': _L2_ffn_in['Wg'], 'L2_ffn_W1': _L2_ffn_in['W1'], 'L2_ffn_b1': _L2_ffn_in['b1'], 'L2_ffn_W2': _L2_ffn_in['W2'], 'L2_ffn_b2': _L2_ffn_in['b2'], 'L2_ffn_W3': _L2_ffn_in['W3'], 'L2_ffn_b3': _L2_ffn_in['b3'], 'L2_c': _L2_c, 'L2_wmod': _L2_wmod, 'L3_attn_Wq': _L3_attn_in['Wq'], 'L3_attn_bq': _L3_attn_in['bq'], 'L3_attn_Wk': _L3_attn_in['Wk'], 'L3_attn_bk': _L3_attn_in['bk'], 'L3_attn_Wv': _L3_attn_in['Wv'], 'L3_attn_bv': _L3_attn_in['bv'], 'L3_attn_Wo': _L3_attn_in['Wo'], 'L3_attn_bo': _L3_attn_in['bo'], 'L3_ffn_Wg': _L3_ffn_in['Wg'], 'L3_ffn_W1': _L3_ffn_in['W1'], 'L3_ffn_W2': _L3_ffn_in['W2'], 'L3_ffn_W3': _L3_ffn_in['W3'], 'L3_c': _L3_c, 'L3_wmod': _L3_wmod}
    _x0 = _d['L0_attn_x']
    _d['L0_attn_x'] = jax.random.normal(jax.random.fold_in(jax.random.key(seed), 1), (16, 256, 128), dtype=_x0.dtype)
    del _x0
    return _d

def reference(L0_attn_x, L0_attn_Wq, L0_attn_bq, L0_attn_Wk, L0_attn_bk, L0_attn_Wv, L0_attn_bv, L0_attn_Wo, L0_attn_bo, L0_attn_sinks, L0_ffn_gate_kernel, L0_ffn_gate_bias, L0_ffn_w_gate, L0_ffn_w_up, L0_ffn_w_down, L0_ffn_sw_gate, L0_ffn_sw_up, L0_ffn_sw_down, L0_c, L0_wmod, L1_attn_wq_lat, L1_attn_wk_lat, L1_attn_wv_lat, L1_attn_wq_heads, L1_attn_wk_heads, L1_attn_wv_heads, L1_attn_w_proj, L1_attn_b_proj, L1_ffn_phi_w, L1_ffn_phi_b, L1_ffn_expert_w, L1_ffn_expert_b, L1_c, L1_wmod, L2_attn_miu_x, L2_attn_lambda_, L2_attn_A_lora, L2_attn_B_lora, L2_attn_td_miu, L2_attn_td_A, L2_attn_td_B, L2_attn_u, L2_attn_Wr, L2_attn_Wk, L2_attn_Wv, L2_attn_Wg, L2_attn_Wo, L2_attn_gn_gamma, L2_attn_gn_beta, L2_ffn_Wg, L2_ffn_W1, L2_ffn_b1, L2_ffn_W2, L2_ffn_b2, L2_ffn_W3, L2_ffn_b3, L2_c, L2_wmod, L3_attn_Wq, L3_attn_bq, L3_attn_Wk, L3_attn_bk, L3_attn_Wv, L3_attn_bv, L3_attn_Wo, L3_attn_bo, L3_ffn_Wg, L3_ffn_W1, L3_ffn_W2, L3_ffn_W3, L3_c, L3_wmod):

    def _L0_attn_ref(x, Wq, bq, Wk, bk, Wv, bv, Wo, bo, sinks):
        import jax, jax.numpy as jnp
        import numpy as np
        H = 64
        HK = 8
        HD = 64
        DM = 128
        WINDOW = 128
        B, S, _ = x.shape
        G = H // HK
        q = (x @ Wq.T + bq).reshape(B, S, H, HD).transpose(0, 2, 1, 3)
        k = (x @ Wk.T + bk).reshape(B, S, HK, HD).transpose(0, 2, 1, 3)
        v = (x @ Wv.T + bv).reshape(B, S, HK, HD).transpose(0, 2, 1, 3)
        k = jnp.repeat(k, G, axis=1)
        v = jnp.repeat(v, G, axis=1)
        scale = 1.0 / np.sqrt(HD).astype(np.float32)
        scores = jnp.einsum('bhqd,bhkd->bhqk', q, k) * scale
        qi = jnp.arange(S)[:, None]
        kj = jnp.arange(S)[None, :]
        allowed = (qi >= kj) & (qi - kj < WINDOW)
        neg = jnp.asarray(-1e+30, scores.dtype)
        scores = jnp.where(allowed[None, None], scores, neg)
        sink = jnp.broadcast_to(sinks[None, :, None, None], (B, H, S, 1))
        logits = jnp.concatenate([scores, sink], axis=-1)
        probs = jax.nn.softmax(logits, axis=-1)[..., :-1]
        o = jnp.einsum('bhqk,bhkd->bhqd', probs, v)
        o = o.transpose(0, 2, 1, 3).reshape(B, S, H * HD)
        return o @ Wo.T + bo

    def _L0_ffn_ref(hidden_states, gate_kernel, gate_bias, w_gate, w_up, w_down, sw_gate, sw_up, sw_down):
        import jax, jax.numpy as jnp
        import numpy as np
        H = 128
        M = 64
        E = 16
        TOP_K = 4
        N_GROUP = 4
        TOPK_GROUP = 2
        SCALE = 2.5
        B, S = (2, 128)

        def _gate(x2d, gate_kernel, gate_bias):
            n = x2d.shape[0]
            logits = jnp.dot(x2d.astype(jnp.float32), gate_kernel.astype(jnp.float32))
            scores = jax.nn.sigmoid(logits)
            scores_for_choice = scores + gate_bias
            group_scores = scores_for_choice.reshape(n, N_GROUP, E // N_GROUP)
            top2 = jax.lax.top_k(group_scores, k=2)[0]
            group_sum = jnp.sum(top2, axis=-1)
            group_idx = jax.lax.top_k(group_sum, k=TOPK_GROUP)[1]
            group_mask = jnp.zeros_like(group_sum).at[jnp.arange(n)[:, None], group_idx].set(1.0)
            score_mask = jnp.repeat(group_mask[:, :, None], E // N_GROUP, axis=2).reshape(n, E)
            masked_scores = jnp.where(score_mask > 0, scores_for_choice, 0.0)
            topk_weight, topk_idx = jax.lax.top_k(masked_scores, k=TOP_K)
            topk_weight = topk_weight / (jnp.sum(topk_weight, axis=-1, keepdims=True) + 1e-20)
            topk_weight = topk_weight * SCALE
            return (topk_idx, topk_weight)
        orig_shape = hidden_states.shape
        x = hidden_states.reshape(-1, orig_shape[-1])
        topk_idx, topk_weight = _gate(x, gate_kernel, gate_bias)
        onehot = (topk_idx[:, :, None] == jnp.arange(E)[None, None, :]).astype(topk_weight.dtype)
        combine = jnp.einsum('nke,nk->ne', onehot, topk_weight)
        g = jnp.einsum('nh,ehm->enm', x, w_gate)
        u = jnp.einsum('nh,ehm->enm', x, w_up)
        inter = jax.nn.silu(g) * u
        y_e = jnp.einsum('enm,emh->enh', inter, w_down)
        y = jnp.einsum('ne,enh->nh', combine, y_e)
        shared = jnp.dot(jax.nn.silu(jnp.dot(x, sw_gate)) * jnp.dot(x, sw_up), sw_down)
        return (y + shared).reshape(orig_shape)

    def _L1_attn_ref(x, wq_lat, wk_lat, wv_lat, wq_heads, wk_heads, wv_heads, w_proj, b_proj):
        import jax, jax.numpy as jnp
        import numpy as np
        B, T, C = (2, 256, 128)
        LAT = 32
        N_HEAD = 16
        HEAD_DIM = C // N_HEAD
        SCALE = 1.0 / np.sqrt(HEAD_DIM).astype(np.float32)
        Bx, Tx, Cx = x.shape
        q = x @ wq_lat @ wq_heads
        k = x @ wk_lat @ wk_heads
        v = x @ wv_lat @ wv_heads
        q = q.reshape(Bx, Tx, N_HEAD, HEAD_DIM).transpose(0, 2, 1, 3)
        k = k.reshape(Bx, Tx, N_HEAD, HEAD_DIM).transpose(0, 2, 1, 3)
        v = v.reshape(Bx, Tx, N_HEAD, HEAD_DIM).transpose(0, 2, 1, 3)
        att = jnp.einsum('bhqd,bhkd->bhqk', q, k) * SCALE
        causal = jnp.tril(jnp.ones((Tx, Tx), dtype=bool))
        att = jnp.where(causal[None, None], att, -jnp.inf)
        att = jax.nn.softmax(att, axis=-1)
        y = jnp.einsum('bhqk,bhkd->bhqd', att, v)
        y = y.transpose(0, 2, 1, 3).reshape(Bx, Tx, Cx)
        return y @ w_proj + b_proj

    def _L1_ffn_ref(x, phi_w, phi_b, expert_w, expert_b):
        import jax, jax.numpy as jnp
        import numpy as np
        T, Z, D_DIM = (8, 256, 128)
        N_EXP, P_SLOT, H = (64, 32, 128)
        LN_EPS = 1e-05
        t, z, d = x.shape
        n = expert_w.shape[0]
        p = phi_w.shape[0] // n
        logits = (jnp.einsum('tzd,ed->tze', x, phi_w) + phi_b).reshape(t, z, n, p)
        D = jax.nn.softmax(logits, axis=3)
        C = jax.nn.softmax(logits, axis=2)
        X_tilde = jnp.einsum('tznp,tzd->npd', D, x)
        X_tilde = jnp.clip(X_tilde, -33000.0, 65000.0)
        mu = jnp.mean(X_tilde, axis=-1, keepdims=True)
        var = jnp.mean(jnp.square(X_tilde - mu), axis=-1, keepdims=True)
        X_tilde = (X_tilde - mu) * jax.lax.rsqrt(var + LN_EPS)
        X_tilde = jnp.tanh(X_tilde)
        Y_tilde = jnp.einsum('npd,ndH->npH', X_tilde, expert_w) + expert_b[:, None, :]
        Y = jnp.einsum('tznp,npH->tzH', C, Y_tilde)
        return Y

    def _L2_attn_ref(x, miu_x, lambda_, A_lora, B_lora, td_miu, td_A, td_B, u, Wr, Wk, Wv, Wg, Wo, gn_gamma, gn_beta):
        import jax, jax.numpy as jnp
        import numpy as np
        B, T, C = (8, 256, 128)
        HS = 64
        H = C // HS
        LORA_R = 32
        TD_R = 64

        def _wkv6(r, k, v, w, u):
            n = r.shape[-1]
            decay = jnp.exp(-jnp.exp(w))

            def per_head(rt, kt, vt, dt, uh):

                def step(S, inp):
                    ri, ki, vi, di = inp
                    kv = ki[:, None] * vi[None, :]
                    y = ri @ (S + uh[:, None] * kv)
                    S = di[:, None] * S + kv
                    return (S, y)
                S0 = jnp.zeros((n, n), rt.dtype)
                _, ys = jax.lax.scan(step, S0, (rt, kt, vt, dt))
                return ys
            f = jax.vmap(per_head, in_axes=(0, 0, 0, 0, 0))
            f = jax.vmap(f, in_axes=(0, 0, 0, 0, None))
            return f(r, k, v, decay, u)
        b, t, c = x.shape
        h, n = u.shape
        x_last = jnp.pad(x, ((0, 0), (1, 0), (0, 0)))[:, :t]
        dxa = x_last - x
        xm = x + dxa * miu_x
        lora_h = jnp.tanh(xm @ A_lora).reshape(b, t, 5, -1)
        miu = lambda_ + jnp.einsum('btfi,fic->fbtc', lora_h, B_lora)
        xx = x[None] + dxa[None] * miu
        w_in, k_in, v_in, r_in, g_in = xx
        k = k_in @ Wk.T
        v = v_in @ Wv.T
        r = r_in @ Wr.T
        g = jax.nn.silu(g_in @ Wg.T)
        w = td_miu + jnp.tanh(w_in @ td_A) @ td_B

        def to_heads(z):
            return z.reshape(b, t, h, n).transpose(0, 2, 1, 3)
        y = _wkv6(to_heads(r), to_heads(k), to_heads(v), to_heads(w), u)
        y = y.transpose(0, 2, 1, 3)
        eps = 1e-05 * h
        mean = y.mean(-1, keepdims=True)
        var = y.var(-1, keepdims=True)
        yn = (y - mean) * jax.lax.rsqrt(var + eps)
        yn = yn * gn_gamma.reshape(h, n) + gn_beta.reshape(h, n)
        yn = yn.reshape(b, t, c)
        return yn * g @ Wo.T

    def _L2_ffn_ref(x, Wg, W1, b1, W2, b2, W3, b3):
        import jax, jax.numpy as jnp
        import numpy as np
        TOPK = 4
        N_GROUPS = 4
        TOPK_GROUPS = 2
        ROUTE_SCALE = 2.5

        def _gate(x2, Wg):
            T = x2.shape[0]
            E = Wg.shape[0]
            scores = x2 @ Wg.T
            s = jax.nn.sigmoid(scores)
            g = s.reshape(T, N_GROUPS, E // N_GROUPS)
            group_scores = g.max(axis=-1)
            _, gidx = jax.lax.top_k(group_scores, TOPK_GROUPS)
            group_mask = jnp.any(jax.nn.one_hot(gidx, N_GROUPS, dtype=jnp.bool_), axis=1)
            masked = jnp.where(group_mask[:, :, None], g, -jnp.inf).reshape(T, E)
            _, idx = jax.lax.top_k(masked, TOPK)
            w = jnp.take_along_axis(s, idx, axis=1)
            w = w / jnp.sum(w, axis=-1, keepdims=True)
            w = w * ROUTE_SCALE
            return (w.astype(x2.dtype), idx)
        shape = x.shape
        D = shape[-1]
        x2 = x.reshape(-1, D)
        weights, indices = _gate(x2, Wg)
        E = Wg.shape[0]
        y = jnp.zeros_like(x2)
        for e in range(E):
            we = jnp.sum(weights * (indices == e), axis=-1)
            h = jax.nn.silu(x2 @ W1[e].T + b1[e]) * (x2 @ W3[e].T + b3[e])
            y = y + (h @ W2[e].T + b2[e]) * we[:, None]
        return y.reshape(shape)

    def _L3_attn_ref(x, Wq, bq, Wk, bk, Wv, bv, Wo, bo):
        import jax, jax.numpy as jnp
        import numpy as np
        D_MODEL = 128
        N_HEADS = 16
        HEAD_DIM = D_MODEL // N_HEADS
        B, S, _ = x.shape
        scale = jnp.sqrt(jnp.float32(HEAD_DIM))

        def split_heads(t):
            return t.reshape(B, S, N_HEADS, HEAD_DIM).transpose(0, 2, 1, 3)
        q = split_heads(x @ Wq.T + bq)
        k = split_heads(x @ Wk.T + bk)
        v = split_heads(x @ Wv.T + bv)
        attn = jnp.einsum('bhqd,bhkd->bhqk', q, k) / scale
        attn = jax.nn.softmax(attn, axis=-1)
        out = jnp.einsum('bhqk,bhkd->bhqd', attn, v)
        out = out.transpose(0, 2, 1, 3).reshape(B, S, D_MODEL)
        return out @ Wo.T + bo

    def _L3_ffn_ref(x, Wg, W1, W2, W3):
        import jax, jax.numpy as jnp
        import numpy as np
        B, T, C, H, E = (4, 256, 128, 256, 8)
        CAPACITY_FACTOR = 1.0
        b, t, c = x.shape
        e = Wg.shape[0]
        n = b * t
        capacity = max(1, int(CAPACITY_FACTOR * n / e))
        x_flat = x.reshape(n, c)
        scores = (x_flat @ Wg.T).T
        top_vals, token_idx = jax.lax.top_k(scores, capacity)
        token_w = jax.nn.softmax(top_vals, axis=-1)
        xg = x_flat[token_idx]
        h = jax.nn.silu(jnp.einsum('eic,ehc->eih', xg, W1)) * jnp.einsum('eic,ehc->eih', xg, W3)
        y = jnp.einsum('eih,ech->eic', h, W2) * token_w[..., None]
        out = jnp.zeros_like(x_flat).at[token_idx.reshape(-1)].add(y.reshape(-1, c))
        return out.reshape(b, t, c)
    x = L0_attn_x
    mod = (_silu(L0_c) @ L0_wmod).reshape(L0_c.shape[0], 6, 1, -1)
    sa, ca, ga, sb, cb, gb = (mod[:, 0], mod[:, 1], mod[:, 2], mod[:, 3], mod[:, 4], mod[:, 5])
    ga = (2 * (ga >= 0) - 1) * jnp.maximum(jnp.abs(ga), 0.25)
    gb = (2 * (gb >= 0) - 1) * jnp.maximum(jnp.abs(gb), 0.25)
    h = _layernorm(x, axis=-1) * (1 + ca) + sa
    x = x + ga * _L0_attn_ref(h, L0_attn_Wq, L0_attn_bq, L0_attn_Wk, L0_attn_bk, L0_attn_Wv, L0_attn_bv, L0_attn_Wo, L0_attn_bo, L0_attn_sinks)
    h = _layernorm(x, axis=-1) * (1 + cb) + sb
    x = x + gb * _L0_ffn_ref(h, L0_ffn_gate_kernel, L0_ffn_gate_bias, L0_ffn_w_gate, L0_ffn_w_up, L0_ffn_w_down, L0_ffn_sw_gate, L0_ffn_sw_up, L0_ffn_sw_down)
    mod = (_silu(L1_c) @ L1_wmod).reshape(L1_c.shape[0], 6, 1, -1)
    sa, ca, ga, sb, cb, gb = (mod[:, 0], mod[:, 1], mod[:, 2], mod[:, 3], mod[:, 4], mod[:, 5])
    ga = (2 * (ga >= 0) - 1) * jnp.maximum(jnp.abs(ga), 0.25)
    gb = (2 * (gb >= 0) - 1) * jnp.maximum(jnp.abs(gb), 0.25)
    h = _layernorm(x, axis=-1) * (1 + ca) + sa
    x = x + ga * _L1_attn_ref(h, L1_attn_wq_lat, L1_attn_wk_lat, L1_attn_wv_lat, L1_attn_wq_heads, L1_attn_wk_heads, L1_attn_wv_heads, L1_attn_w_proj, L1_attn_b_proj)
    h = _layernorm(x, axis=-1) * (1 + cb) + sb
    x = x + gb * _L1_ffn_ref(h, L1_ffn_phi_w, L1_ffn_phi_b, L1_ffn_expert_w, L1_ffn_expert_b)
    mod = (_silu(L2_c) @ L2_wmod).reshape(L2_c.shape[0], 6, 1, -1)
    sa, ca, ga, sb, cb, gb = (mod[:, 0], mod[:, 1], mod[:, 2], mod[:, 3], mod[:, 4], mod[:, 5])
    ga = (2 * (ga >= 0) - 1) * jnp.maximum(jnp.abs(ga), 0.25)
    gb = (2 * (gb >= 0) - 1) * jnp.maximum(jnp.abs(gb), 0.25)
    h = _layernorm(x, axis=-1) * (1 + ca) + sa
    x = x + ga * _L2_attn_ref(h, L2_attn_miu_x, L2_attn_lambda_, L2_attn_A_lora, L2_attn_B_lora, L2_attn_td_miu, L2_attn_td_A, L2_attn_td_B, L2_attn_u, L2_attn_Wr, L2_attn_Wk, L2_attn_Wv, L2_attn_Wg, L2_attn_Wo, L2_attn_gn_gamma, L2_attn_gn_beta)
    h = _layernorm(x, axis=-1) * (1 + cb) + sb
    x = x + gb * _L2_ffn_ref(h, L2_ffn_Wg, L2_ffn_W1, L2_ffn_b1, L2_ffn_W2, L2_ffn_b2, L2_ffn_W3, L2_ffn_b3)
    mod = (_silu(L3_c) @ L3_wmod).reshape(L3_c.shape[0], 6, 1, -1)
    sa, ca, ga, sb, cb, gb = (mod[:, 0], mod[:, 1], mod[:, 2], mod[:, 3], mod[:, 4], mod[:, 5])
    ga = (2 * (ga >= 0) - 1) * jnp.maximum(jnp.abs(ga), 0.25)
    gb = (2 * (gb >= 0) - 1) * jnp.maximum(jnp.abs(gb), 0.25)
    h = _layernorm(x, axis=-1) * (1 + ca) + sa
    x = x + ga * _L3_attn_ref(h, L3_attn_Wq, L3_attn_bq, L3_attn_Wk, L3_attn_bk, L3_attn_Wv, L3_attn_bv, L3_attn_Wo, L3_attn_bo)
    h = _layernorm(x, axis=-1) * (1 + cb) + sb
    x = x + gb * _L3_ffn_ref(h, L3_ffn_Wg, L3_ffn_W1, L3_ffn_W2, L3_ffn_W3)
    return x

_drawn_inputs = setup_inputs


def setup_inputs(seed=0):
    import zlib

    import numpy as np

    out = dict(_drawn_inputs(seed))
    spreads = {'L0_attn_sinks': (1.0, 0.6),
     'L1_attn_b_proj': (0.0, 0.1),
     'L2_attn_gn_gamma': (1.0, 0.6),
     'L2_attn_gn_beta': (0.0, 0.8),
     'L2_ffn_b1': (0.0, 0.8),
     'L2_ffn_b2': (0.0, 0.696),
     'L2_ffn_b3': (0.0, 0.8)}
    factors = {'L0_attn_Wq': 8.0,
     'L0_attn_bq': 8.0,
     'L0_attn_Wk': 8.0,
     'L0_attn_bk': 8.0,
     'L0_attn_Wv': 3.19,
     'L0_attn_bv': 3.351,
     'L0_attn_bo': 3.846,
     'L1_attn_wq_lat': 8.0,
     'L1_attn_wk_lat': 8.0,
     'L1_attn_wv_lat': 8.0,
     'L1_attn_wq_heads': 8.0,
     'L1_attn_wk_heads': 8.0,
     'L1_attn_wv_heads': 8.0,
     'L1_attn_w_proj': 8.0,
     'L1_ffn_phi_w': 6.103,
     'L1_ffn_phi_b': 8.0,
     'L1_ffn_expert_b': 2.875,
     'L2_attn_miu_x': 8.0,
     'L2_attn_lambda_': 8.0,
     'L2_attn_A_lora': 8.0,
     'L2_attn_B_lora': 8.0,
     'L2_attn_td_miu': 8.0,
     'L2_attn_td_A': 64.0,
     'L2_attn_td_B': 64.0,
     'L2_attn_u': 8.0,
     'L2_attn_Wr': 8.0,
     'L2_attn_Wk': 8.0,
     'L2_attn_Wv': 8.0,
     'L2_attn_Wg': 8.0,
     'L2_attn_Wo': 8.0,
     'L2_ffn_W1': 8.0,
     'L2_ffn_W2': 8.0,
     'L2_ffn_W3': 8.0,
     'L3_attn_Wq': 8.0,
     'L3_attn_bq': 8.0,
     'L3_attn_Wk': 8.0,
     'L3_attn_bk': 64.0,
     'L3_attn_Wv': 6.068,
     'L3_attn_bv': 7.612,
     'L3_attn_Wo': 4.59,
     'L3_attn_bo': 27.471,
     'L3_ffn_Wg': 64.0,
     'L3_ffn_W1': 64.0,
     'L3_ffn_W2': 64.0,
     'L3_ffn_W3': 64.0,
     'L3_c': 3.463,
     'L3_wmod': 3.45}
    for name, (base, spread) in spreads.items():
        noise = np.random.default_rng([zlib.crc32(name.encode()), seed]).standard_normal(out[name].shape)
        drawn = base * np.exp(spread * noise) if base else spread * noise
        out[name] = jnp.asarray(drawn.astype(out[name].dtype))
    for name, factor in factors.items():
        out[name] = (out[name] * factor).astype(out[name].dtype)
    return out
```

```python
from contextlib import ExitStack

import numpy as np

import concourse.bass as bass
from concourse import mybir

F32 = mybir.dt.float32
I32 = mybir.dt.int32
ALU = mybir.AluOpType
ACT = mybir.ActivationFunctionType
AX = mybir.AxisListType.X
P = 128
NB = 16
NT = 32
PHASES = (0, 7)
NEG = -1e30
TW = 16400

CONST = [("ident", 128), ("mwin", 256), ("mcaus", 256), ("ones", 128), ("tri", 128),
         ("same32", 128), ("sel32", 128), ("lev", 8 * 128)]
MODS = [(f"{n}{l}", w) for l in range(4) for n, w in (("c", 16), ("w", 768))]
L0A = [("wq", 4096), ("wo", 4096), ("wk", 1024), ("wv", 512), ("bq", 32), ("bk", 8),
       ("bv", 512), ("bo", 1), ("sink", 64)]
L0F = [("gk", 16), ("gb", 16), ("w1", 1024), ("w3", 1024), ("w2", 2048), ("sw1", 128),
       ("sw3", 128), ("sw2", 128)]
L1F = [("phi", 2048), ("phib", 2048), ("phic", 16), ("ew", 8192)]
EB = [("eb", 2048)]
SM = [("wlat", 96), ("wq96", 512), ("wk96", 512), ("wv96", 128), ("wproj", 128), ("bproj", 1),
      ("miux", 1), ("lam", 5), ("A", 160), ("B", 640), ("tdmiu", 1), ("tdA", 64), ("tdB", 128),
      ("u", 1), ("WrT", 128), ("WkT", 128), ("WvT", 128), ("WgT", 128), ("WoT", 128),
      ("gam", 128), ("bet", 128),
      ("q3", 512), ("k3", 512), ("v3", 128), ("o3", 128), ("bq3", 4), ("bk3", 4), ("bv3", 128),
      ("bo3", 1)]
L2F = [("wg", 16), ("w1", 2048), ("b1", 16), ("w3", 2048), ("b3", 16), ("w2", 2048), ("b2", 128)]
L3F = [("wg", 8), ("w1", 2048), ("w3", 2048), ("w2", 2048)]
PACKS = {"const": CONST, "mods": MODS, "l0a": L0A, "l0f": L0F, "l1f": L1F, "eb": EB, "sm": SM,
         "l2f": L2F, "l3f": L3F}


def width(spec):
    return sum(w for _, w in spec)


class Eng:

    def __init__(self, sem):
        self.q, self.sem, self.n = [], sem, 0

    def wait(self, w):
        if w is not None and w[1] > 0:
            self.q.append(("wait", *w))

    def do(self, fn, *waits, inc=True):
        for w in waits:
            self.wait(w)
        if inc is True:
            self.n += 1
            self.q.append(("do", fn, self.sem))
            return (self.sem, self.n)
        self.q.append(("do", fn, inc or None))

    def flush(self, eng):
        for kind, a, b in self.q:
            if kind == "wait":
                eng.wait_ge(a, b)
            else:
                r = a(eng)
                if b is not None:
                    r.then_inc(b, 1)


class Region:

    def __init__(self, ap, width_):
        self.ap, self.w, self.at = ap, width_, 0

    def get(self, n):
        a = self.at
        self.at += n
        assert self.at <= self.w, (self.at, self.w)
        return self.ap[:, a:a + n]


def views(tile, spec, at=0):
    out = {}
    for n, w in spec:
        out[n] = tile[:, at:at + w]
        at += w
    return out


class K:
    pass


def sems(k, phase, *names):
    return [k.ctx.enter_context(k.nc.semaphore(f"{phase}_{n}")) for n in names]


def setup(nc, ctx, dram, out):
    k = K()
    k.nc, k.ctx, k.dram, k.out = nc, ctx, dram, out
    sem = lambda n: ctx.enter_context(nc.semaphore(n))
    k.pe, k.dve, k.act, k.pool, k.sp = (Eng(sem(f"s_{n}")) for n in ("pe", "dve", "act", "pool", "sp"))
    k.dsem = {n: sem(f"d_{n}") for n in list(PACKS) + ["x", "out", "sm2"]}
    sb = lambda n, w: ctx.enter_context(nc.sbuf_tensor(n, [P, w], F32))
    k.X = sb("X", 4096)
    k.HT = sb("HT", 4096)
    k.W1 = sb("W1", width(L1F))
    k.W2 = sb("W2", width(L2F))
    k.W3 = sb("W3", width(SM))
    k.C_tile = sb("C", width(CONST))
    k.C = views(k.C_tile, CONST)
    k.modT = sb("modT", 4 * 96)
    k.gbbc = sb("gbbc", 2048)
    k.sT = sb("sT", 64)
    k.wgb = sb("wgb", 3 * 128)
    k.MV = sb("MV", 64)
    k.rs = sb("rs", 64)
    k.T = sb("T", TW)
    k.st6 = sb("st6", 24)
    k.s_aggr, k.s_h = sem("s_aggr"), sem("s_h")
    k.n_stats, k.norms = 0, 0
    k.bank = [ctx.enter_context(nc.psum_tensor(f"ps{i}", [P, 512], F32)) for i in range(8)]
    k.phase_end = []
    return k


def load(k, name, tile, *waits):
    w = width(PACKS[name])
    src = k.dram[name]
    for wt in waits:
        k.sp.wait(wt)
    k.sp.q.append(("do", lambda e: e.dma_start(tile[:, 0:w], src[:, :]).then_inc(k.dsem[name], 16), None))
    return (k.dsem[name], 16)


def mm(k, out, lhsT, rhs, *waits, start=True, stop=True, inc=None):
    return k.pe.do(lambda e: e.matmul(out, lhsT, rhs, start=start, stop=stop), *waits, inc=inc)


def tr(k, out, in_, *waits, inc=None):
    return k.pe.do(lambda e: e.transpose(out, in_, k.C["ident"]), *waits, inc=inc)


def act(k, out, in_, f, *waits, bias=0.0, scale=1.0, inc=True):
    return k.act.do(lambda e: e.activation(out, in_, f, bias=bias, scale=scale), *waits, inc=inc)


def tt(k, eng, out, a, b, op, *waits, inc=True):
    return eng.do(lambda e: e.tensor_tensor(out, a, b, op), *waits, inc=inc)


def ts(k, eng, out, a, s1, s2, op0, op1, *waits, inc=True):
    if op1 is None:
        return eng.do(lambda e: e.tensor_scalar(out, a, s1, None, op0), *waits, inc=inc)
    return eng.do(lambda e: e.tensor_scalar(out, a, s1, s2, op0, op1), *waits, inc=inc)


def stt(k, out, a, s, b, op0, op1, *waits, inc=True):
    return k.dve.do(lambda e: e.scalar_tensor_tensor(out=out, in0=a, scalar=s, in1=b, op0=op0, op1=op1), *waits,
                    inc=inc)


def red(k, out, a, op, *waits, inc=True):
    return k.dve.do(lambda e: e.tensor_reduce(out, a, AX, op), *waits, inc=inc)


def cp(k, eng, out, a, *waits, inc=True):
    if eng is k.act:
        return act(k, out, a, ACT.Copy, *waits, inc=inc)
    return eng.do(lambda e: e.tensor_copy(out, a), *waits, inc=inc)


def stats(k, i, x_ready):
    n = k.n_stats
    k.n_stats += 1
    st = k.st6[:, 6 * (n % 4):6 * (n % 4) + 6]
    a = k.dve.do(lambda e: e.bn_stats(st, k.X[:, i * 128:(i + 1) * 128]), x_ready, (k.s_aggr, n - 3))
    k.dve.do(lambda e: e.bn_aggr(k.MV[:, 2 * i:2 * i + 2], st), a, inc=k.s_aggr)


def modulation(k, t_const, t_mods):
    M = views(k.T, MODS)
    o = width(MODS)
    e1, e2 = k.T[:, o:o + 64], k.T[:, o + 64:o + 128]
    sT = k.sT[:, :]
    d2 = None
    for l in range(4):
        c = M[f"c{l}"]
        s = slice(16 * l, 16 * l + 16)
        a = act(k, e1[:, s], c, ACT.Exp, t_mods, scale=-1.0)
        a = ts(k, k.dve, e1[:, s], e1[:, s], 1.0, None, ALU.add, None, a)
        a = k.dve.do(lambda e, s=s: e.reciprocal(e2[:, s], e1[:, s]), a)
        a = tt(k, k.dve, sT[:, s], c, e2[:, s], ALU.mult, a)
        ps = k.bank[l]
        for j in range(6):
            m = mm(k, ps[:, 16 * j:16 * j + 16], M[f"w{l}"][:, 128 * j:128 * j + 128], sT[:, s], a,
                   inc=(j == 5))
        d = cp(k, k.dve, k.modT[:, 96 * l:96 * l + 96], ps[:, 0:96], m)
        for j in (1, 4):
            v = k.modT[:, 96 * l + 16 * j:96 * l + 16 * j + 16]
            ts(k, k.dve, v, v, 1.0, None, ALU.add, None, d)
        for j in (2, 5):
            v = k.modT[:, 96 * l + 16 * j:96 * l + 16 * j + 16]
            d2 = gate_floor(k, v, k.T[:, o + 128:o + 144], k.T[:, o + 144:o + 160], d, d2)
        if l != 1:
            i = {0: 0, 2: 1, 3: 2}[l]
            d3 = cp(k, k.dve, k.wgb[:, 128 * i:128 * i + 128], M[f"w{l}"][:, 640:768], t_mods)
    k.mod_tok = d3
    k.phase_end = [d3]


def gate_floor(k, v, a, b, *waits):
    w = ts(k, k.dve, a, v, 0.0, 2.0, ALU.is_ge, ALU.mult, *waits)
    w = ts(k, k.dve, a, a, -1.0, None, ALU.add, None, w)
    w2 = stt(k, b, v, -1.0, v, ALU.mult, ALU.max, *waits)
    w2 = ts(k, k.dve, b, b, 0.25, None, ALU.max, None, w2)
    return tt(k, k.dve, v, a, b, ALU.mult, w, w2)


def gate_rows(k, l, region):
    i = {0: 0, 2: 1, 3: 2}[l]
    scr = [region.get(128) for _ in range(2)]
    s_row, s_rows = sems(k, f"g{l}", "row", "rows")
    for h in range(4):
        ps = k.bank[7 - h % 2]
        for j in range(4):
            b = 4 * h + j
            s = scr[b % 2]
            col = k.sT[:, 16 * l + b:16 * l + b + 1]
            c = ts(k, k.dve, s, k.C["ones"], col, None, ALU.mult, None, k.mod_tok, *k.phase_end, (s_row, b - 1))
            mm(k, ps[:, 128 * j:128 * j + 128], s, k.wgb[:, 128 * i:128 * i + 128], c, (s_rows, h - 1),
               inc=s_row)
        cp(k, k.dve, k.gbbc[:, 512 * h:512 * h + 512], ps[:, :], (s_row, 4 * h + 4), inc=s_rows)
    n = region.at
    a, b = region.get(2048), region.get(2048)
    region.at = n
    return gate_floor(k, k.gbbc[:, :], a, b, (s_rows, 4))


def layernorm(k, l, sub, region):
    var = k.MV[:, :].rearrange("p (t c) -> p t c", c=2)[:, :, 1]
    mean = k.MV[:, :].rearrange("p (t c) -> p t c", c=2)[:, :, 0]
    rstd = k.rs[:, 0:32]
    v1 = k.rs[:, 32:64]
    a = ts(k, k.dve, v1, var, 1e-5, None, ALU.add, None, (k.s_aggr, k.n_stats), *k.phase_end)
    a = act(k, v1, v1, ACT.Sqrt, a)
    a = k.dve.do(lambda e: e.reciprocal(rstd, v1), a)
    n0 = region.at
    xn = [region.get(128) for _ in range(8)]
    region.at = n0
    s_c = 96 * l + 48 * sub
    (s_turned,) = sems(k, f"n{l}{sub}", "turned")
    h0 = 16 * k.norms
    for c in range(NB // 2):
        ps = k.bank[c % 4]
        for j in range(4):
            i = 4 * c + j
            x = xn[i % 8]
            d = ts(k, k.dve, x, k.X[:, i * 128:(i + 1) * 128], mean[:, i:i + 1], rstd[:, i:i + 1],
                   ALU.subtract, ALU.mult, a, (s_turned, i - 7))
            tr(k, ps[:, 128 * j:128 * j + 128], x, d, (k.s_h, h0 + 2 * (c - 3) if c > 3 else 0), inc=s_turned)
        for b in (2 * c, 2 * c + 1):
            act(k, k.HT[:, b * 256:(b + 1) * 256], ps[:, (b % 2) * 256:(b % 2) * 256 + 256],
                ACT.Identity, (s_turned, 4 * c + 4), scale=k.modT[:, s_c + 16 + b:s_c + 17 + b],
                bias=k.modT[:, s_c + b:s_c + b + 1], inc=k.s_h)
    k.norms += 1
    k.phase_end = [(k.s_h, 16 * k.norms)]


def enter(k, *more):
    for e in (k.pe, k.dve, k.act, k.pool):
        for t in list(k.phase_end) + list(more):
            e.wait(t)


def attention(k, l, layer, w, t_w):
    nG, HG, W = {"l0": (8, 8, 65), "l1": (1, 16, 9), "l3": (1, 16, 9)}[layer]
    big = layer == "l0"
    d = W - 1
    CH = HG * d // 128
    scale = d ** -0.5
    per = 2 * HG // 4
    groups, units = NB * nG, NB * nG * per
    (s_ones, s_half, s_masked, s_shift, s_sshift, s_exps, s_sexp, s_turn, s_even, s_odd, s_values, s_o, s_div, s_side,
     s_free, s_out, s_y, s_yread, s_x) = sems(
         k, layer + "a", "ones", "half", "masked", "shift", "sshift", "exps", "sexp", "turn", "even", "odd", "values",
         "o", "div", "side", "free", "out", "y", "yread", "x")
    R = Region(k.T, TW)
    many = lambda n, w_: [R.get(w_) for _ in range(n)]
    qT = many(2, 1024)
    kT = many(2, 256 if big else 1024)
    va = many(3, 2 * W if big else 2 * HG * 32)
    OT = None if big else many(2, 128)
    Sm = None if layer == "l3" else many(3, 1024)
    Pr = Sm if layer == "l1" else many(3, 1024)
    PT = many(2, 1024)
    mxs, ngs, ess, dens, rins, tks = (many(4, 4) for _ in range(6))
    ot = many(2, 2 * CH * 128)
    oT = many(2, CH * 256)
    yT = R.get(256)
    lats = many(2, 256)
    nsink = R.get(64)
    b_ = k.bank
    if layer == "l3":
        Sb, Tb, Ob, side, acc = b_[0:4], b_[4:6], b_[6], b_[7], b_[7]
    else:
        Sb, Tb, Ob, side, acc = b_[0:3], b_[3:5], b_[5], b_[6], b_[7]
    h0 = 16 * (k.norms - 1)

    def place(i):
        n, r = divmod(i, per)
        qt, s4 = divmod(r, HG // 4)
        return n, qt, s4, 2 if (layer == "l3" or qt == 1) else 1

    def turns(i):
        n, r = divmod(i, per)
        if layer == "l3":
            return 2 * i
        return n * (per + per // 2) + r + max(0, r - per // 2)

    parts = {"l0": ("q0", "q1", "kv"), "l1": ("lat", "q0", "q1", "k0", "k1", "v"),
             "l3": ("q0", "q1", "k0", "k1", "v")}[layer]
    late = 4 if big else 5
    before, after = {}, {}
    for n in range(groups):
        for p, part in enumerate(parts):
            at = max(0, n * per - (4 if big else 7) + p)
            before.setdefault(at, []).append((part, n))
        at = n * per + per - 1 + late
        for c2 in range((CH + 1) // 2):
            after.setdefault(at + c2, []).append((f"end{c2}", n))
        at += 1 + (CH + 1) // 2
        after.setdefault(at, []).append(("out", n))
        if n % nG == nG - 1:
            after.setdefault(at + 1, []).append(("x", n))
    order = []
    for i in range(units + late + 5):
        first = [("scores", i)] if i < units else []
        if not big and 4 <= i < units + 4:
            first.append(("o_turn", i - 4))
        if 2 <= i < units + 2:
            first.append(("turn", i - 2))
        order += before.get(i, []) + first if i == 0 else first + before.get(i, [])
        if i < units:
            order.append(("exps", i))
        if 3 <= i < units + 3:
            order.append(("values", i - 3))
        order += after.get(i, [])
    in_side = ("lat", "q0", "q1", "k0", "k1", "kv", "v", "end0", "end1", "o_turn")
    if acc is side:
        in_side += ("out", "x")
    uses = {step: u for u, step in enumerate(s for s in order if s[0] in in_side)}

    def side_filled(step, n):
        return (s_side, uses[step, n] + 1) if n >= 0 else None

    def side_taken(step, n):
        return (s_free, uses[step, n] + 1) if n >= 0 else None

    def side_before(step, n):
        return (s_free, uses[step, n])

    def q_or_k(part, n, wt, bias, x, x_ready, dst):
        j = int(part[1])
        for c in range(2):
            mm(k, side[:, 256 * c:256 * c + 256], wt[:, 128 * (2 * j + c):128 * (2 * j + c) + 128], x,
               side_before(part, n), x_ready, inc=s_side if c == 1 else None)
        eng = k.act if part in ("q0", "k1") else k.dve
        waits = [side_filled(part, n), (s_half, 2 * per * (n - 1))]
        o = dst[:, 512 * j:512 * j + 512]
        if bias is None:
            return cp(k, eng, o, side[:, :], *waits, inc=s_free)
        for c in range(2):
            s = slice(256 * c, 256 * c + 256)
            bb = bias[:, 2 * j + c:2 * j + c + 1]
            inc = s_free if c == 1 else False
            if eng is k.act:
                act(k, o[:, s], side[:, s], ACT.Identity, *waits, bias=bb, inc=inc)
            else:
                ts(k, eng, o[:, s], side[:, s], bb, None, ALU.add, None, *waits, inc=inc)

    def project(part, n):
        b, g = divmod(n, nG)
        x, x_ready = k.HT[:, b * 256:(b + 1) * 256], (k.s_h, h0 + b + 1)
        q, kt, v, lat = qT[n % 2], kT[n % 2], va[n % 3], lats[n % 2]
        v_free = (s_values, per * (n - 2))
        if part == "lat":
            mm(k, side[0:96, 0:256], w["wlat"], x, side_before(part, n), x_ready, inc=s_side)
            act(k, lat[0:96, :], side[0:96, 0:256], ACT.Copy, side_filled(part, n), side_filled("v", n - 2),
                inc=s_free)
            return
        if layer == "l1":
            x, x_ready = lat[0:96, :], side_taken("lat", n)
            wq, wk, bq, bk, wv = w["wq96"][0:96, :], w["wk96"][0:96, :], None, None, w["wv96"][0:96, :]
        elif layer == "l3":
            wq, wk, bq, bk, wv = w["q3"], w["k3"], w["bq3"], w["bk3"], w["v3"]
        else:
            wq, bq = w["wq"][:, 512 * g:512 * g + 512], w["bq"][:, 4 * g:4 * g + 4]
        if part[0] == "q":
            return q_or_k(part, n, wq, bq, x, x_ready, q)
        if part in ("k0", "k1"):
            return q_or_k(part, n, wk, bk, x, x_ready, kt)
        if part == "kv":
            mm(k, side[:, 0:256], w["wk"][:, 128 * g:128 * g + 128], x, side_before(part, n), x_ready)
            for j in range(2):
                mm(k, side[:, 256 + 64 * j:320 + 64 * j], x[:, 128 * j:128 * j + 128],
                   w["wv"][:, 64 * g:64 * g + 64], inc=s_side if j == 1 else None)
            ts(k, k.dve, kt, side[:, 0:256], w["bk"][:, g:g + 1], None, ALU.add, None, side_filled(part, n),
               (s_half, 2 * per * (n - 1)), inc=False)
            bv = w["bv"][:, 64 * g:64 * g + 64].unsqueeze(1).broadcast_to([P, 2, 64])
            tt(k, k.dve, v.rearrange("p (t w) -> p t w", t=2)[:, :, 0:64],
               side[:, 256:384].rearrange("p (t w) -> p t w", t=2), bv, ALU.add, v_free, inc=s_free)
            return
        for j in range(2):
            mm(k, side[:, 128 * j:128 * j + 128], x[:, 128 * j:128 * j + 128], wv, side_before(part, n), x_ready,
               inc=s_side if j == 1 else None)
        v4 = v.rearrange("p (t h w) -> p t h w", t=2, h=16)
        p4 = side[:, 0:256].rearrange("p (t h w) -> p t h w", t=2, h=16)
        for j in range(2):
            o, inc = v4[:, j, :, 0:8], s_free if j == 1 else False
            if layer == "l1":
                cp(k, k.dve, o, p4[:, j], side_filled(part, n), v_free, inc=inc)
            else:
                bv = w["bv3"].rearrange("p (h w) -> p h w", h=16)
                tt(k, k.dve, o, p4[:, j], bv, ALU.add, side_filled(part, n), v_free, inc=inc)

    def scores(i):
        n, qt, s4, nk = place(i)
        q, kt, w_ = qT[n % 2], kT[n % 2], 128 * nk
        for j in range(2):
            for p in range(2):
                half = 2 * i + p
                bk = Sb[half % len(Sb)]
                if big:
                    c, r, kk = 2 * s4 + j, slice(64 * p, 64 * p + 64), kT[n % 2][:, 0:w_]
                    ready = [side_taken(f"q{s4}", n), side_taken("kv", n)]
                else:
                    g = 2 * (s4 % 2) + p
                    c, r = 2 * (s4 // 2) + j, slice(32 * g, 32 * g + 32)
                    kk = kt[:, 256 * c:256 * c + w_]
                    ready = [side_taken(f"q{s4 // 2}", n), side_taken(f"k{s4 // 2}", n)]
                free = (s_exps, i - 1) if layer == "l3" else (s_masked, half - 2)
                mm(k, bk[:, w_ * j:w_ * j + w_], q[r, 256 * c + 128 * qt:256 * c + 128 * qt + 128], kk[r, :], free,
                   *ready, inc=s_half if j == 1 else None)

    def maximum(i):
        n, qt, s4, nk = place(i)
        w_, g = 128 * nk, n % nG
        mx, ng, tk = mxs[i % 4], ngs[i % 4], tks[i % 4]
        if layer == "l3":
            for p in range(2):
                t = red(k, mx[:, 2 * p:2 * p + 2], Sb[(2 * i + p) % 4][:, :].rearrange("p (h t) -> p h t", h=2),
                        ALU.max, (s_half, 2 * i + p + 1), (s_shift, i - 3))
        else:
            mask = k.C["mwin" if big else "mcaus"]
            mask = mask if nk == 2 else mask[:, 128:256]
            sm = Sm[i % 3]
            free = (s_exps, i - 2) if big else (s_turn, turns(i - 2) if i > 2 else 0)
            for p in range(2):
                bk = Sb[(2 * i + p) % 3]
                for j in range(2):
                    h = 2 * p + j
                    k.dve.do(lambda e, h=h, j=j, bk=bk: e.tensor_tensor_reduce(
                        sm[:, 256 * h:256 * h + w_], bk[:, j * w_:j * w_ + w_], mask, 1.0, -3.0e38, ALU.add, ALU.max,
                        mx[:, h:h + 1]), (s_half, 2 * i + p + 1), free, (s_shift, i - 3),
                        inc=s_masked if j == 1 else False)
            t = (s_masked, 2 * i + 2)
        if big:
            q0 = 8 * g + 4 * s4
            stt(k, ng, mx, -scale, nsink[:, q0:q0 + 4], ALU.mult, ALU.min, t, (s_exps, i - 3), inc=s_shift)
            tt(k, k.dve, tk, ng, w["sink"][:, q0:q0 + 4], ALU.add, (s_shift, i + 1), (s_sexp, i - 3), inc=s_sshift)
        else:
            ts(k, k.dve, ng, mx, -scale, None, ALU.mult, None, t, (s_exps, i - 3), inc=s_shift)

    def exps(i):
        n, qt, s4, nk = place(i)
        w_, pr = 128 * nk, Pr[i % 3]
        for h in range(4):
            if layer == "l3":
                src = Sb[(2 * i + h // 2) % 4][:, (h % 2) * w_:(h % 2) * w_ + w_]
            else:
                src = Sm[i % 3][:, 256 * h:256 * h + w_]
            act(k, pr[:, 256 * h:256 * h + w_], src, ACT.Exp, (s_shift, i + 1), (s_turn, turns(i - 2) if i > 2 else 0),
                bias=ngs[i % 4][:, h:h + 1], scale=scale, inc=s_exps if h == 3 else False)
        if big:
            act(k, ess[i % 4], tks[i % 4], ACT.Exp, (s_sshift, i + 1), (s_div, i - 3), inc=s_sexp)

    def turn(i):
        n, qt, s4, nk = place(i)
        for c in range(nk):
            t = turns(i) + c
            bk = Tb[t % 2]
            s_taken = (s_even, s_odd)[t % 2]
            for h in range(4):
                tr(k, bk[:, 128 * h:128 * h + 128], Pr[i % 3][:, 256 * h + 128 * c:256 * h + 128 * c + 128],
                   (s_exps, i + 1), (s_taken, t // 2), inc=s_turn if h == 3 else None)
            cp(k, (k.act, k.dve)[t % 2], PT[i % 2][:, 512 * c:512 * c + 512], bk[:, :], (s_turn, t + 1),
               (s_values, i - 1), inc=s_taken)

    def values(i):
        n, qt, s4, nk = place(i)
        v, pt = va[n % 3], PT[i % 2]
        v_ready = side_taken("kv" if big else "v", n)
        for a in range(4 if big else nk):
            for b in range(nk if big else 4):
                h, c = (a, b) if big else (b, a)
                t = turns(i) + c
                taken = ((s_even, s_odd)[t % 2], t // 2 + 1)
                x = pt[:, 512 * c + 128 * h:512 * c + 128 * h + 128]
                inc = s_values if (h == 3 and c == nk - 1) else None
                if big:
                    mm(k, Ob[:, W * h:W * h + W], x, v[:, c * W:(c + 1) * W], (s_div, i), taken, v_ready,
                       start=(c == 0), stop=(c == nk - 1), inc=inc)
                else:
                    hh = 32 * (16 * c + 4 * s4 + h)
                    mm(k, Ob[32 * h:32 * h + 32, 0:128], v[:, hh:hh + 32], x, (s_o, i), taken, v_ready,
                       start=(c == 0), stop=(c == nk - 1), inc=inc)
        if not big:
            cp(k, k.act, OT[i % 2], Ob[:, 0:128], (s_values, i + 1), side_filled("o_turn", i - 2), inc=s_o)

    def o_turn(i):
        tr(k, side[:, 0:128], OT[i % 2], (s_o, i + 1), side_before("o_turn", i), inc=s_side)

    def divide(i):
        n, qt, s4, nk = place(i)
        den, rin = dens[i % 4], rins[i % 4]
        if big:
            o3 = Ob[:, 0:4 * W].rearrange("p (h w) -> p h w", h=4)
            t = tt(k, k.dve, den, o3[:, :, d], ess[i % 4], ALU.add, (s_values, i + 1), (s_sexp, i + 1), (s_div, i - 3))
            t = k.dve.do(lambda e: e.reciprocal(rin, den), t)
        else:
            o3 = side[:, 0:128].rearrange("p (h w) -> p h w", h=4)
            t = k.dve.do(lambda e: e.reciprocal(rin, o3[:, :, d]), side_filled("o_turn", i), side_taken("o_turn", i - 4))
        c0 = qt * CH * 128 + s4 * 4 * d
        o = ot[n % 2][:, c0:c0 + 4 * d].rearrange("p (h w) -> p h w", h=4)
        tt(k, k.dve, o, o3[:, :, 0:d], rin.unsqueeze(2).broadcast_to([P, 4, d]), ALU.mult, t,
           side_filled(f"end{(CH - 1) // 2}", n - 2), inc=s_div if big else s_free)

    def out_filled(n):
        return side_filled("out", n) if acc is side else (s_out, n + 1)

    def out_taken(n):
        return side_taken("out", n) if acc is side else (s_y, n // nG + 1)

    def y_turned(n):
        return side_filled("x", n) if acc is side else (s_yread, n // nG + 1)

    def end(step, n):
        c2 = int(step[3])
        cs = list(range(2 * c2, min(2 * c2 + 2, CH)))
        last = (n + 1) * per - 1
        rows = (s_div, last + 1) if big else side_taken("o_turn", last)
        for j, c in enumerate(cs):
            for q in range(2):
                tr(k, side[:, 256 * j + 128 * q:256 * j + 128 * q + 128],
                   ot[n % 2][:, (q * CH + c) * 128:(q * CH + c + 1) * 128], side_before(step, n), rows,
                   inc=s_side if (j == len(cs) - 1 and q == 1) else None)
        w_ = 256 * len(cs)
        cp(k, (k.act, k.dve)[c2], oT[n % 2][:, 512 * c2:512 * c2 + w_], side[:, 0:w_], side_filled(step, n),
           out_filled(n - 2), inc=s_free)

    def out(n):
        b, g = divmod(n, nG)
        free = side_before("out", n) if acc is side else (s_x, b)
        for c in range(CH):
            mm(k, acc[:, 0:256], w["wo"][:, (g * CH + c) * 128:(g * CH + c + 1) * 128],
               oT[n % 2][:, 256 * c:256 * c + 256], free, side_taken(f"end{c // 2}", n), start=(g == 0 and c == 0),
               stop=(g == nG - 1 and c == CH - 1), inc=(s_side if acc is side else s_out) if c == CH - 1 else None)
        if g == nG - 1:
            ga = k.modT[:, 96 * l + 32 + b:96 * l + 33 + b]
            ts(k, k.dve, yT, acc[:, 0:256], w["bo"], ga, ALU.add, ALU.mult, out_filled(n), y_turned(n - nG),
               inc=s_free if acc is side else s_y)

    def to_x(n):
        b = n // nG
        for j in range(2):
            tr(k, acc[:, 128 * j:128 * j + 128], yT[:, 128 * j:128 * j + 128], out_taken(n),
               side_before("x", n) if acc is side else None,
               inc=(s_side if acc is side else s_yread) if j == 1 else None)
        x = k.X[:, b * 256:b * 256 + 256]
        tt(k, k.dve, x, x, acc[:, 0:256], ALU.add, y_turned(n), inc=s_free if acc is side else s_x)
        summed = side_taken("x", n) if acc is side else (s_x, b + 1)
        stats(k, 2 * b, summed)
        stats(k, 2 * b + 1, summed)

    enter(k, t_w)
    for v in va:
        k.pool.do(lambda e, v=v: e.memset(v, 1.0), inc=s_ones)
    if big:
        t = ts(k, k.dve, nsink, w["sink"], -1.0, None, ALU.mult, None)
        k.dve.wait(t)
    k.dve.wait((s_ones, len(va)))
    run = {"scores": lambda i: (scores(i), maximum(i)), "exps": exps, "turn": turn,
           "values": lambda i: (values(i), divide(i)) if big else values(i),
           "o_turn": lambda i: (o_turn(i), divide(i)), "out": out, "x": to_x}
    for step, n in order:
        if step in run:
            run[step](n)
        elif step[0:3] == "end":
            end(step, n)
        else:
            project(step, n)
    k.phase_end = [(k.s_aggr, k.n_stats)]


def v3(ap, n):
    return ap.rearrange("p (t e) -> p t e", e=n)


def bc(ap, n):
    return ap.unsqueeze(len(ap.shape)).broadcast_to(list(ap.shape) + [n])


def chain(k):
    last = [None]

    def step(fn, *waits):
        last[0] = k.dve.do(fn, last[0], *waits)
        return last[0]
    return step


def rank(k, step, vals, n, C, out):
    C4 = C.rearrange("p (t e j) -> p t e j", e=n, j=n)
    for e in range(n):
        if e:
            k.dve.do(lambda q, e=e: q.tensor_tensor(C4[:, :, e, 0:e], vals[:, :, 0:e],
                                                   vals[:, :, e:e + 1].broadcast_to([P, NT, e]), ALU.is_ge))
        step(lambda q, e=e: q.tensor_tensor(C4[:, :, e, e:n], vals[:, :, e:n],
                                            vals[:, :, e:e + 1].broadcast_to([P, NT, n - e]), ALU.is_gt))
    return step(lambda q: q.tensor_reduce(out, C4, AX, ALU.add))


def scores_tok(k, wg, n, t_w):
    for i in range(NT):
        m = mm(k, k.bank[4][:, n * i:n * i + n], k.HT[:, 128 * i:128 * i + 128], wg, t_w, *k.phase_end,
               inc=True if i == NT - 1 else None)
    return m


def gate_groups(k, l, w, t_w, r):
    nc_ = 17 if l == 0 else 16
    comb = v3(r.get(NT * nc_), nc_)
    n0 = r.at
    s, m, g, gr, rk, wt, den, C = (r.get(x) for x in (512, 512, 128, 128, 512, 512, 32, 8192))
    x = scores_tok(k, w["gk"] if l == 0 else w["wg"], 16, t_w)
    step = chain(k)
    a = act(k, s, k.bank[4][:, 0:512], ACT.Exp, x, scale=-1.0)
    s3, m3, g3, gr3, w3_, rk3 = v3(s, 16), v3(m, 16), v3(g, 4), v3(gr, 4), v3(wt, 16), v3(rk, 16)
    step(lambda q: q.tensor_scalar(s, s, 1.0, None, ALU.add), a)
    step(lambda q: q.reciprocal(s, s))
    q4 = s.rearrange("p (x f) -> p x f", f=4)
    if l == 0:
        gb = w["gb"].unsqueeze(1).broadcast_to([P, NT, 16])
        step(lambda q: q.tensor_tensor(s3, s3, gb, ALU.add))
        t0, t1, t2 = rk[:, 0:128], rk[:, 128:256], rk[:, 256:384]
        T = lambda o, a_, b_, op: step(lambda q: q.tensor_tensor(o, a_, b_, op))
        T(t0, q4[:, :, 0], q4[:, :, 1], ALU.max)
        T(t1, q4[:, :, 2], q4[:, :, 3], ALU.max)
        T(g, t0, t1, ALU.max)
        T(t0, t0, t1, ALU.min)
        T(t1, q4[:, :, 0], q4[:, :, 1], ALU.min)
        T(t2, q4[:, :, 2], q4[:, :, 3], ALU.min)
        T(t1, t1, t2, ALU.max)
        T(t0, t0, t1, ALU.max)
        T(g, g, t0, ALU.add)
    else:
        step(lambda q: q.tensor_reduce(g, q4, AX, ALU.max))
    rank(k, step, g3, 4, C[:, 0:512], gr3)
    step(lambda q: q.tensor_scalar(gr, gr, 2.0, None, ALU.is_lt))
    m4 = m.rearrange("p (x f) -> p x f", f=4)
    step(lambda q: q.tensor_tensor(m4, q4, bc(gr, 4), ALU.mult))
    if l == 2:
        step(lambda q: q.tensor_scalar(gr, gr, -1.0, None, ALU.add))
        step(lambda q: q.tensor_tensor(m4, m4, bc(gr, 4), ALU.add))
    rank(k, step, m3, 16, C, rk3)
    step(lambda q: q.tensor_scalar(rk, rk, 4.0, None, ALU.is_lt))
    step(lambda q: q.tensor_tensor(wt, m, rk, ALU.mult))
    step(lambda q: q.tensor_reduce(den, w3_, AX, ALU.add))
    if l == 0:
        step(lambda q: q.tensor_scalar(den, den, 1e-20, None, ALU.add))
    step(lambda q: q.reciprocal(den, den))
    step(lambda q: q.tensor_scalar(den, den, 2.5, None, ALU.mult))
    t = step(lambda q: q.tensor_tensor(comb[:, :, 0:16], w3_, bc(den, 16), ALU.mult))
    if l == 0:
        t = step(lambda q: q.memset(comb[:, :, 16:17], 1.0))
    r.at = n0
    return comb, t


def gate_top(k, w, t_w, r):
    comb = v3(r.get(NT * 8), 8)
    n0 = r.at
    S, Y, A, B, Gm = (r.get(256) for _ in range(5))
    sg, kk, t, cd, ct, pr, thr, mx, need = (r.get(8) for _ in range(9))
    c8 = r.get(8)
    e_t = lambda ap: ap.rearrange("p (t e) -> p e t", e=8)
    over = lambda ap: ap.unsqueeze(1).broadcast_to([P, NT, 8])
    x = scores_tok(k, w["wg"], 8, t_w)
    step = chain(k)
    step(lambda q: q.tensor_copy(S, k.bank[4][:, 0:256]), x)
    banks = [k.bank[5], k.bank[6]]
    n = [0]

    def total(src, ones="ones"):
        bk = banks[n[0] % 2]
        n[0] += 1
        m = mm(k, bk[:, 0:8], k.C[ones], src, (k.dve.sem, k.dve.n), inc=True)
        return bk[:, 0:8], m

    def count(src3, against, op):
        step(lambda q: q.tensor_tensor(v3(A, 8), src3, over(against), op))
        step(lambda q: q.tensor_reduce(c8, e_t(A), AX, ALU.add))
        return total(c8)

    step(lambda q: q.memset(t, 0.0))
    c, m = count(v3(S, 8), t, ALU.is_ge)
    step(lambda q: q.tensor_scalar(pr, c, 511.5, None, ALU.is_ge), m)
    step(lambda q: q.tensor_scalar(sg, pr, 2.0, -1.0, ALU.mult, ALU.add))
    step(lambda q: q.tensor_scalar(kk, pr, 512.0 - 3585.0, 3585.0, ALU.mult, ALU.add))
    step(lambda q: q.tensor_tensor(v3(Y, 8), v3(S, 8), over(sg), ALU.mult))
    ti, ci, pi = t.bitcast(I32), cd.bitcast(I32), pr.bitcast(I32)
    for bit in range(30, -1, -1):
        step(lambda q, bit=bit: q.tensor_scalar(ci, ti, 1 << bit, None, ALU.bitwise_or))
        c, m = count(v3(Y, 8), cd, ALU.is_ge)
        step(lambda q, c=c: q.tensor_tensor(pi, c, kk, ALU.is_ge), m)
        step(lambda q: q.copy_predicated(t, pi, cd))
    step(lambda q: q.tensor_tensor(thr, t, sg, ALU.mult))
    c, m = count(v3(S, 8), thr, ALU.is_gt)
    step(lambda q: q.tensor_scalar(need, c, -1.0, 512.0, ALU.mult, ALU.add), m)
    step(lambda q: q.tensor_tensor(v3(A, 8), v3(S, 8), over(thr), ALU.is_equal))
    m1 = mm(k, banks[0][:, 0:256], k.C["tri"], A, (k.dve.sem, k.dve.n), inc=True)
    m2 = mm(k, banks[1][:, 0:256], k.C["ones"], A, inc=True)
    step(lambda q: q.tensor_copy(B, banks[0][:, 0:256]), m1)
    step(lambda q: q.tensor_copy(Gm, banks[1][:, 0:256]), m2)
    z = 1
    src, dst = Gm, r.get(256)
    while z < NT:
        step(lambda q, s=src, d=dst, z=z: q.tensor_copy(d[:, 0:8 * z], s[:, 0:8 * z]))
        step(lambda q, s=src, d=dst, z=z: q.tensor_tensor(d[:, 8 * z:256], s[:, 8 * z:256], s[:, 0:256 - 8 * z], ALU.add))
        src, dst = dst, src
        z *= 2
    step(lambda q: q.tensor_tensor(B[:, 8:256], B[:, 8:256], src[:, 0:248], ALU.add))
    step(lambda q: q.tensor_tensor(v3(B, 8), v3(B, 8), over(need), ALU.is_lt))
    step(lambda q: q.tensor_tensor(B, B, A, ALU.mult))
    step(lambda q: q.tensor_tensor(v3(A, 8), v3(S, 8), over(thr), ALU.is_gt))
    sel = step(lambda q: q.tensor_tensor(B, B, A, ALU.add))
    a = step(lambda q: q.tensor_reduce(mx, e_t(S), AX, ALU.max))
    m = tr(k, banks[0][0:8, 0:128], mx, a, inc=True)
    step(lambda q: q.tensor_reduce(thr[0:8, 0:1], banks[0][0:8, 0:128], AX, ALU.max), m)
    step(lambda q: q.tensor_scalar(Y[0:8, 0:8], k.C["ident"][0:8, 0:8], thr[0:8, 0:1], None, ALU.mult))
    m = mm(k, banks[1][:, 0:8], k.C["ones"][0:8, :], Y[0:8, 0:8], (k.dve.sem, k.dve.n), inc=True)
    step(lambda q: q.tensor_copy(mx, banks[1][:, 0:8]), m)
    d = step(lambda q: q.tensor_tensor(v3(A, 8), v3(S, 8), over(mx), ALU.subtract))
    a = act(k, A, A, ACT.Exp, d)
    step(lambda q: q.tensor_tensor(A, A, B, ALU.mult), a)
    step(lambda q: q.tensor_reduce(c8, e_t(A), AX, ALU.add))
    c, m = total(c8)
    step(lambda q: q.reciprocal(need, c), m)
    t_ = step(lambda q: q.tensor_tensor(comb, v3(A, 8), over(need), ALU.mult))
    r.at = n0
    return comb, t_


def moe(k, l, t_w, t_gb, r):
    w = views(k.W1 if l == 3 else k.W2, {0: L0F, 2: L2F, 3: L3F}[l])
    if l == 3:
        comb, t_c = gate_top(k, w, t_w, r)
    else:
        comb, t_c = gate_groups(k, l, w, t_w, r)
    s_silu, s_hidden, s_down, s_sum, s_tox, s_ct, s_ctp = sems(k, f"f{l}", "silu", "hidden", "down", "sum", "tox",
                                                               "ct", "ctp")
    sg = [r.get(512) for _ in range(3)]
    h = [r.get(512) for _ in range(3)]
    acc = [r.get(512) for _ in range(2)]
    ym = [r.get(512) for _ in range(2)]
    if l == 0:
        yb, E = [(k.bank[4], k.bank[5]), (k.bank[6], k.bank[7])], 9
    else:
        yb, E = [(k.bank[4],), (k.bank[5],), (k.bank[6],)], 16
    enter(k, t_gb, t_c, t_w)
    if l == 2:
        cT = r.get(4096)
        for g in range(8):
            bk = k.bank[4 + g % 2]
            for j in range(4):
                tr(k, bk[0:16, 128 * j:128 * j + 128], comb[:, 4 * g + j, :], (s_ct, g - 1),
                   inc=s_ctp if j == 3 else None)
            cp(k, k.dve, cT[0:16, 512 * g:512 * g + 512], bk[0:16, :], (s_ctp, g + 1), inc=s_ct)

    last = [None] * 4

    def up(u):
        B, e = divmod(u, E)
        g_, u_ = k.bank[2 * (u % 2)], k.bank[2 * (u % 2) + 1]
        x = k.HT[:, 512 * B:512 * B + 512]
        if l == 0 and e == 8:
            w1, w3 = w["sw1"], w["sw3"]
        else:
            w1, w3 = w["w1"][:, 128 * e:128 * e + 128], w["w3"][:, 128 * e:128 * e + 128]
        m1 = mm(k, g_[:, :], w1, x, (s_silu, u - 1), inc=True)
        m2 = mm(k, u_[:, :], w3, x, (s_hidden, u - 1), inc=True)
        a, hh = sg[u % 3], h[u % 3]
        act(k, a, g_[:, :], ACT.Silu, m1, (s_hidden, u - 2), bias=(w["b1"][:, e:e + 1] if l == 2 else 0.0),
            inc=s_silu)
        if l == 2:
            stt(k, hh, u_[:, :], w["b3"][:, e:e + 1], a, ALU.add, ALU.mult, (s_silu, u + 1), m2, (s_down, u - 2),
                inc=s_hidden)
        else:
            tt(k, k.dve, hh, u_[:, :], a, ALU.mult, (s_silu, u + 1), m2, (s_down, u - 2), inc=s_hidden)

    def down(u):
        B, e = divmod(u, E)
        hh, A = h[u % 3], acc[B % 2]
        v = u + (B + 1 if l == 2 else 0)
        if l == 2 and e == 0:
            y = yb[(v - 1) % 3][0]
            for j in range(4):
                i = 4 * B + j
                m = mm(k, y[:, 128 * j:128 * j + 128], cT[0:16, 128 * i:128 * i + 128], w["b2"][0:16, :],
                       (s_sum, v - 3), (s_ct, 8), inc=True if j == 3 else None)
            cp(k, k.dve, A, y[:, :], m, (s_tox, B - 1), inc=s_sum)
            last[:] = [(s_sum, v)] * 4
        ys = yb[v % len(yb)]
        two = l == 0 and e < 8
        for j in range(4):
            if two:
                o, rhs = ys[j // 2][:, 256 * (j % 2):256 * (j % 2) + 256], w["w2"][:, 256 * e:256 * e + 256]
            else:
                o, rhs = ys[0][:, 128 * j:128 * j + 128], (w["sw2"] if l == 0 else w["w2"][:, 128 * e:128 * e + 128])
            m = mm(k, o, hh[:, 128 * j:128 * j + 128], rhs, (s_sum, v - len(yb) + 1), (s_hidden, u + 1),
                   inc=s_down if j == 3 else (True if two and j == 1 else None))
            if two and j == 1:
                m_lo = m
        m = (s_down, u + 1)
        for q in range(2 if two else 1):
            for j in range(4):
                i = 4 * B + j
                if l == 0:
                    c = comb[:, i, 2 * e + q:2 * e + q + 1] if e < 8 else comb[:, i, 16:17]
                else:
                    c = comb[:, i, e:e + 1] if l == 2 else comb[:, i, e // 2:e // 2 + 1]
                a = A[:, 128 * j:128 * j + 128]
                if two:
                    src, mw = ys[j // 2][:, 256 * (j % 2) + 128 * q:256 * (j % 2) + 128 * q + 128], m_lo if j < 2 else m
                else:
                    src, mw = ys[0][:, 128 * j:128 * j + 128], m
                end = j == 3 and q == (1 if two else 0)
                if e == 0 and q == 0 and l != 2:
                    t = ts(k, k.dve, a, src, c, None, ALU.mult, None, mw, (s_tox, B - 1), inc=s_sum if end else True)
                else:
                    t = stt(k, a, src, c, a, ALU.mult, ALU.add, mw, last[j], inc=s_sum if end else True)
                last[j] = (s_sum, v + 1) if end else t
        if e == E - 1:
            y2 = ym[B % 2]
            for hb in range(2):
                b = 2 * B + hb
                g = k.gbbc[:, 128 * b:128 * b + 128].unsqueeze(1).broadcast_to([P, 2, 128])
                o = y2[:, 256 * hb:256 * hb + 256]
                p = tt(k, k.pool, o.rearrange("p (t d) -> p t d", t=2),
                       A[:, 256 * hb:256 * hb + 256].rearrange("p (t d) -> p t d", t=2), g, ALU.mult,
                       (s_sum, v + 1), (s_tox, B - 1))
                x = k.X[:, 256 * b:256 * b + 256]
                p = tt(k, k.pool, x, x, o, ALU.add, p, inc=s_tox if hb else True)
                p = (s_tox, B + 1) if hb else p
                stats(k, 2 * b, p)
                stats(k, 2 * b + 1, p)

    for u in range(8 * E + 1):
        if u < 8 * E:
            up(u)
        if u >= 1:
            down(u - 1)
    k.phase_end = [(k.s_aggr, k.n_stats)]


def back_to_x(k, yT, ready, B, bank, bank_free, s_turned, s_sum):
    for j in range(4):
        tr(k, bank[:, 128 * j:128 * j + 128], yT[:, 128 * j:128 * j + 128], ready, bank_free,
           inc=s_turned if j == 3 else None)
    x = k.X[:, 512 * B:512 * B + 512]
    tt(k, k.dve, x, x, bank[:, :], ALU.add, (s_turned, B + 1), inc=s_sum)


def soft_moe(k, t_w):
    w = views(k.W1, L1F)
    r = Region(k.T, TW)
    mxn = r.get(1024)
    yt = r.get(2048)
    small = [r.get(64) for _ in range(6)]
    n1 = r.at
    htok = r.get(4096)
    L = [r.get(2048) for _ in range(2)]
    E = [r.get(2048) for _ in range(2)]
    (s_turned, s_htok_a, s_htok_d, s_logits, s_biased, s_max, s_slot, s_shift, s_exps, s_inv, s_soft,
     s_gather) = sems(k, "s1", "turned", "htok_a", "htok_d", "logits", "biased", "max", "slot", "shift", "exps",
                      "inv", "soft", "gather")
    enter(k, t_w)
    bank = k.bank
    for g in range(8):
        p = bank[g % 4]
        for j in range(4):
            i = 4 * g + j
            tr(k, p[:, 128 * j:128 * j + 128], k.HT[:, 128 * i:128 * i + 128],
               ((s_htok_d, s_htok_a)[g % 2], g // 2 - 1), inc=s_turned if j == 3 else None)
        cp(k, (k.dve, k.act)[g % 2], htok[:, 512 * g:512 * g + 512], p[:, :], (s_turned, g + 1),
           inc=(s_htok_d, s_htok_a)[g % 2])

    def logits(i):
        l, e, mx = L[i % 2], E[i % 2], small[i % 2]
        for j in range(4):
            n = 4 * i + j
            mm(k, bank[j][:, :], k.HT[:, 128 * i:128 * i + 128], w["phi"][:, 512 * j:512 * j + 512],
               (s_biased, n - 3), (s_htok_d, 4), (s_htok_a, 4), inc=s_logits)
            tt(k, k.dve, l[:, 512 * j:512 * j + 512], bank[j][:, :], w["phib"][:, 512 * j:512 * j + 512],
               ALU.add, (s_logits, n + 1), (s_slot, i - 1), (s_shift, i - 1), inc=s_biased)
        l3, e3 = l.rearrange("p (n q) -> p n q", q=32), e.rearrange("p (n q) -> p n q", q=32)
        red(k, mx, l3, ALU.max, (s_biased, 4 * i + 4), (s_shift, i - 1), inc=s_max)
        red(k, mxn[:, 32 * i:32 * i + 32], l.rearrange("p (n q) -> p q n", q=32), ALU.max, (s_biased, 4 * i + 4),
            inc=s_slot)
        tt(k, k.pool, e3, l3, bc(mx, 32), ALU.subtract, (s_max, i + 1), (s_gather, i - 1), inc=s_shift)
        act(k, e, e, ACT.Exp, (s_shift, i + 1), inc=s_exps)

    def dispatch(i):
        e, s, rv = E[i % 2], small[2 + i % 2], small[4 + i % 2]
        e3 = e.rearrange("p (n q) -> p n q", q=32)
        t = red(k, s, e3, ALU.add, (s_exps, i + 1), (s_inv, i - 1))
        k.dve.do(lambda q: q.reciprocal(rv, s), t, (s_soft, i - 1), inc=s_inv)
        tt(k, k.pool, e3, e3, bc(rv, 32), ALU.mult, (s_inv, i + 1), inc=s_soft)
        for j in range(4):
            mm(k, bank[4 + j][:, :], htok[:, 128 * i:128 * i + 128], e[:, 512 * j:512 * j + 512], (s_soft, i + 1),
               start=(i == 0), stop=(i == NT - 1), inc=s_gather if j == 3 else None)

    for i in range(NT + 1):
        if i < NT:
            logits(i)
        if i >= 1:
            dispatch(i - 1)
    m_x = (s_gather, NT)
    k.phase_end = [m_x]
    enter(k)
    r.at = n1
    eb = r.get(2048)
    xt, xs, xs2, xt2 = (r.get(2048) for _ in range(4))
    mv, sd, st = r.get(32), r.get(16), [r.get(6) for _ in range(16)]
    t_eb = load(k, "eb", eb, *k.phase_end)
    for j in range(4):
        t = ts(k, k.dve, xt[:, 512 * j:512 * j + 512], bank[4 + j][:, :], -33000.0, 65000.0, ALU.max, ALU.min, m_x)
    for s in range(16):
        m = tr(k, bank[s // 4][:, 128 * (s % 4):128 * (s % 4) + 128], xt[:, 128 * s:128 * s + 128], t, inc=(s % 4 == 3))
        if s % 4 == 3:
            a = cp(k, k.dve, xs[:, 512 * (s // 4):512 * (s // 4) + 512], bank[s // 4][:, :], m)
    for s in range(16):
        a2 = k.dve.do(lambda q, s=s: q.bn_stats(st[s], xs[:, 128 * s:128 * s + 128]), a)
    for s in range(16):
        a3 = k.dve.do(lambda q, s=s: q.bn_aggr(mv[:, 2 * s:2 * s + 2], st[s]), a2)
    mv2 = mv.rearrange("p (t c) -> p t c", c=2)
    t = ts(k, k.dve, sd, mv2[:, :, 1], 1e-5, None, ALU.add, None, a3)
    t = act(k, sd, sd, ACT.Sqrt, t)
    t = k.dve.do(lambda q: q.reciprocal(sd, sd), t)
    for s in range(16):
        t2 = ts(k, k.dve, xs2[:, 128 * s:128 * s + 128], xs[:, 128 * s:128 * s + 128], mv[:, 2 * s:2 * s + 1],
                sd[:, s:s + 1], ALU.subtract, ALU.mult, t)
    t = act(k, xs, xs2, ACT.Tanh, t2)
    for s in range(16):
        m = tr(k, bank[s // 4][:, 128 * (s % 4):128 * (s % 4) + 128], xs[:, 128 * s:128 * s + 128], t, a,
               inc=(s % 4 == 3))
        if s % 4 == 3:
            c = cp(k, k.dve, xt2[:, 512 * (s // 4):512 * (s // 4) + 512], bank[s // 4][:, :], m)
    for s in range(16):
        o = bank[4 + s // 4]
        for j in range(4):
            n = 4 * s + j
            m = mm(k, o[32 * j:32 * j + 32, 128 * (s % 4):128 * (s % 4) + 128], xt2[:, 32 * n:32 * n + 32],
                   w["ew"][:, 128 * n:128 * n + 128], c, inc=(s % 4 == 3 and j == 3))
        if s % 4 == 3:
            q = s // 4
            t_y = tt(k, k.dve, yt[:, 512 * q:512 * q + 512], o[:, :], eb[:, 512 * q:512 * q + 512], ALU.add, m, t_eb)
    k.phase_end = [t_y]
    enter(k)
    r.at = n1
    (s_turned, s_mT, s_sel, s_mb, s_logits, s_shift, s_exps, s_total, s_inv, s_soft, s_comb, s_gate, s_yt,
     s_x) = sems(k, "s3", "turned", "mT", "sel", "mb", "logits", "shift", "exps", "total", "inv", "soft", "comb",
                 "gate", "yt", "x")
    ET = [r.get(8192), w["ew"]]
    dl = [r.get(512) for _ in range(2)]
    mT = r.get(512)
    mb, rc, yo = ([r.get(512) for _ in range(2)] for _ in range(3))
    turn = bank[7]

    def begin(B):
        for j in range(4):
            i = 4 * B + j
            tr(k, turn[0:32, 128 * j:128 * j + 128], mxn[:, 32 * i:32 * i + 32], (s_mb, B), (s_x, B - 1),
               inc=s_turned if j == 3 else None)
        cp(k, k.dve, mT[0:32, :], turn[0:32, :], (s_turned, B + 1), (s_sel, B), inc=s_mT)
        mm(k, turn[:, :], k.C["sel32"][0:32, :], mT[0:32, :], (s_mT, B + 1), inc=s_sel)
        cp(k, k.act, mb[B % 2], turn[:, :], (s_sel, B + 1), (s_shift, 16 * (B - 1)), inc=s_mb)

    def expo(B, s):
        n = 16 * B + s
        l, d = bank[n % 3], dl[n % 2]
        mm(k, l[:, :], w["phi"][:, 128 * s:128 * s + 128], k.HT[:, 512 * B:512 * B + 512], (s_shift, n - 2),
           inc=s_logits)
        tt(k, k.dve, d, l[:, :], mb[B % 2], ALU.subtract, (s_logits, n + 1), (s_mb, B + 1), (s_exps, n - 1),
           inc=s_shift)
        act(k, ET[B % 2][:, 512 * s:512 * s + 512], d, ACT.Exp, (s_shift, n + 1), (s_comb, B - 1),
            bias=w["phic"][:, s:s + 1], inc=s_exps)

    def total(B, s):
        mm(k, bank[3 + B % 2][:, :], k.C["same32"], ET[B % 2][:, 512 * s:512 * s + 512], (s_exps, 16 * B + s + 1),
           (s_inv, B - 1), start=(s == 0), stop=(s == 15), inc=s_total if s == 15 else None)
        if s == 15:
            k.dve.do(lambda e: e.reciprocal(rc[B % 2], bank[3 + B % 2][:, :]), (s_total, B + 1),
                     (s_soft, 16 * (B - 1)), inc=s_inv)

    def combine(B, s):
        e = ET[B % 2][:, 512 * s:512 * s + 512]
        y = bank[5 + B % 2]
        tt(k, k.dve, e, e, rc[B % 2], ALU.mult, (s_inv, B + 1), inc=s_soft)
        mm(k, y[:, :], yt[:, 128 * s:128 * s + 128], e, (s_soft, 16 * B + s + 1), (s_gate, B - 1), start=(s == 0),
           stop=(s == 15), inc=s_comb if s == 15 else None)
        if s == 15:
            for h in range(2):
                g = 96 + 80 + 2 * B + h
                ts(k, k.dve, yo[B % 2][:, 256 * h:256 * h + 256], y[:, 256 * h:256 * h + 256],
                   k.modT[:, g:g + 1], None, ALU.mult, None, (s_comb, B + 1), (s_yt, B - 1),
                   inc=s_gate if h else True)
            k.pe.wait((s_x, B))
            back_to_x(k, yo[B % 2], (s_gate, B + 1), B, turn, (s_mb, min(B + 2, 8)), s_yt, s_x)
            for j in range(4):
                stats(k, 4 * B + j, (s_x, B + 1))

    for B in range(9):
        if B < 8:
            begin(B)
        for s in range(17):
            if B < 8 and s < 16:
                expo(B, s)
            if B < 8 and s >= 1:
                total(B, s - 1)
            if B >= 1 and s < 16:
                combine(B - 1, s)
    k.phase_end = [(k.s_aggr, k.n_stats)]


def rwkv(k, w, *t_w):
    r, r1 = Region(k.T, TW), Region(k.W1, width(L1F))
    s_zero, s_proj, s_ra, s_rd, s_mix, s_decay, s_lev, s_prod, s_merge, s_off, s_ym, s_yo, s_st = sems(
        k, "r1", "zero", "proj", "ra", "rd", "mix", "decay", "lev", "prod", "merge", "off", "ym", "yo", "st")
    LORA, LORA4, MIX, TDA, TDB, KP, RP, VP, GP = 0, 1, 2, 7, 8, 9, 10, 11, 12

    def filled(B, i):
        return (s_proj, 13 * B + i + 1)

    def taken(B, i):
        if i < MIX:
            return (s_ra, 7 * B + i + 1)
        if i < TDA:
            return (s_rd, 6 * B + i - MIX + 1)
        if i < GP:
            return (s_ra, 7 * B + i - TDA + 3)
        return (s_rd, 6 * B + 6)

    st = [r.get(6) for _ in range(8)]
    yall, gall = r1.get(4096), r1.get(4096)
    mvy, sd = r.get(128), r.get(64)
    U = lambda: r.get(512)
    U2 = lambda: [r.get(512) for _ in range(2)]
    dxa, xm, lor, lor4, tmp = U2(), U(), U(), U(), U2()
    xin = [U() for _ in range(5)]
    wA, dd, kk, rr, vv = U(), U2(), U2(), U2(), U2()
    Pq, Qq, Rr, Kr, TT = U(), U(), U2(), U2(), U2()
    AT = [U(), U()]
    off = [[r1.get(256) for _ in range(2)] for _ in range(2)]
    gt = [r1.get(512) for _ in range(2)]
    enter(k, *t_w)
    for s in Rr + Kr:
        k.pool.do(lambda e, s=s: e.memset(s, 0.0), inc=s_zero)
    zero = (s_zero, 4)
    lev = [k.C["lev"][:, 128 * i:128 * i + 128] for i in range(8)]

    def proj(B, i, *parts):
        u = 13 * B + i
        bk = k.bank[4 + u % 3]
        for j, (rows, c0, c1, a, b) in enumerate(parts):
            mm(k, bk[0:rows, c0:c1], a, b, taken(*divmod(u - 3, 13)), inc=s_proj if j == len(parts) - 1 else None)
        return bk

    def front(B):
        x = k.HT[:, 512 * B:512 * B + 512]
        x3 = x.rearrange("p (b t) -> p b t", b=2)
        dx = dxa[B % 2]
        d3 = dx.rearrange("p (b t) -> p b t", b=2)
        tt(k, k.pool, d3[:, :, 1:256], x3[:, :, 0:255], x3[:, :, 1:256], ALU.subtract, taken(B - 2, MIX + 4))
        a = ts(k, k.pool, d3[:, :, 0:1], x3[:, :, 0:1], -1.0, None, ALU.mult, None)
        t = stt(k, xm, dx, w["miux"], x, ALU.mult, ALU.add, a, filled(B - 1, LORA4))
        k.pe.wait(t)
        p = proj(B, LORA, (128, 0, 512, w["A"][:, 0:128], xm))
        act(k, lor, p[:, :], ACT.Tanh, filled(B, LORA), filled(B - 1, MIX + 4), inc=s_ra)
        p = proj(B, LORA4, (32, 0, 512, w["A"][:, 128:160], xm))
        act(k, lor4[0:32, :], p[0:32, :], ACT.Tanh, filled(B, LORA4), inc=s_ra)
        for f in range(5):
            k.pe.wait(taken(B, LORA if f < 4 else LORA4))
            if f < 4:
                p = proj(B, MIX + f, (128, 0, 512, w["B"][:, 128 * f:128 * f + 128], lor))
            else:
                p = proj(B, MIX + f, (128, 0, 512, w["B"][0:32, 512:640], lor4[0:32, :]))
            n, tm = 5 * B + f, tmp[(5 * B + f) % 2]
            stt(k, tm, p[:, :], w["lam"][:, f:f + 1], dx, ALU.add, ALU.mult, filled(B, MIX + f), (s_mix, n - 1),
                inc=s_rd)
            tt(k, k.pool, xin[f], tm, x, ALU.add, taken(B, MIX + f), filled(B - 1, (TDA, KP, VP, RP, GP)[f]), inc=s_mix)
        xw, xk, xv, xr, xg = xin
        mixed = lambda f: (s_mix, 5 * B + f + 1)
        k.pe.wait(mixed(0))
        p = proj(B, TDA, (64, 0, 512, w["tdA"], xw))
        act(k, wA[0:64, :], p[0:64, :], ACT.Tanh, filled(B, TDA), filled(B - 1, TDB), inc=s_ra)
        k.pe.wait(taken(B, TDA))
        p = proj(B, TDB, (128, 0, 512, w["tdB"][0:64, :], wA[0:64, :]))
        d = dd[B % 2]
        act(k, d, p[:, :], ACT.Exp, filled(B, TDB), (s_lev, B - 1), bias=w["tdmiu"], inc=s_ra)
        act(k, d, d, ACT.Exp, taken(B, TDB), scale=-1.0, inc=s_decay)
        k.pe.wait(mixed(1))
        p = proj(B, KP, (128, 0, 512, w["WkT"], xk))
        cp(k, k.act, kk[B % 2], p[:, :], filled(B, KP), (s_lev, B - 1), inc=s_ra)
        k.pe.wait(mixed(3))
        p = proj(B, RP, (128, 0, 512, w["WrT"], xr))
        cp(k, k.act, rr[B % 2], p[:, :], filled(B, RP), (s_lev, B - 1), (s_prod, 18 * (B - 2) + 2), inc=s_ra)
        k.pe.wait(mixed(2))
        p = proj(B, VP, *[(128, 128 * j, 128 * j + 128, xv[:, 128 * j:128 * j + 128], w["WvT"]) for j in range(4)])
        cp(k, k.act, vv[B % 2], p[:, :], filled(B, VP), (s_ym, B - 1), inc=s_ra)
        k.pe.wait(mixed(4))
        p = proj(B, GP, *[(128, 128 * j, 128 * j + 128, xg[:, 128 * j:128 * j + 128], w["WgT"]) for j in range(4)])
        g1, g2 = gt
        t = act(k, g1, p[:, :], ACT.Exp, filled(B, GP), taken(B - 1, GP), scale=-1.0)
        t = ts(k, k.dve, g1, g1, 1.0, None, ALU.add, None, t)
        t = k.dve.do(lambda e: e.reciprocal(g2, g1), t)
        tt(k, k.dve, gall[:, 512 * B:512 * B + 512], p[:, :], g2, ALU.mult, t, inc=s_rd)

    def pairs(B):
        d, kq, rq, v = dd[B % 2], kk[B % 2], rr[B % 2], vv[B % 2]
        tP = k.pool.do(lambda e: e.memset(Pq, 1.0), (s_lev, B))
        tQ = k.pool.do(lambda e: e.memset(Qq, 1.0), (s_lev, B))
        T_, tT = d, (s_decay, B + 1)
        k_ready, r_ready = taken(B, KP), taken(B, RP)

        def multiplied(i, hd):
            return (s_prod, 18 * B + 2 * i + hd + 1)

        def merged(b, i, hd):
            return (s_merge, 16 * b + 2 * i + hd + 1)

        def merge(i):
            for hd in range(2):
                o3 = AT[hd].rearrange("p (t s) -> p t s", t=4)
                b3 = k.bank[hd + 2 * ((9 * B + i) % 2)].rearrange("p (t s) -> p t s", t=4)
                mk = lev[i].unsqueeze(1).broadcast_to([P, 4, 128])
                if i == 0:
                    tt(k, k.dve, o3, b3, mk, ALU.mult, multiplied(i, hd), (s_ym, B), inc=s_merge)
                else:
                    k.dve.do(lambda e, o3=o3, b3=b3, mk=mk: e.copy_predicated(o3, mk.bitcast(I32), b3),
                             multiplied(i, hd), merged(B, i - 1, hd), inc=s_merge)

        for i in range(9):
            n, h = 9 * B + i, 1 << max(0, i - 1)
            R, Kx = Rr[i % 2], Kr[i % 2]
            back = multiplied(i - 2, 1) if i > 1 else (s_prod, 18 * B)
            if i == 0:
                ra, rt = rq, r_ready
                kt = ts(k, k.dve, Kx, kq, w["u"], None, ALU.mult, None, k_ready, back, zero)
            else:
                hv = lambda ap: ap.rearrange("p (n two h) -> p n two h", two=2, h=h)
                Rh, Kh, Ph, Qh, rh, kh = (hv(ap) for ap in (R, Kx, Pq, Qq, rq, kq))
                t1 = tt(k, k.dve, Rh[:, :, 1, :], rh[:, :, 1, :], Ph[:, :, 1, :], ALU.mult, tP, r_ready, back, zero)
                t2 = tt(k, k.dve, Kh[:, :, 0, :], kh[:, :, 0, :], Qh[:, :, 0, :], ALU.mult, tQ, k_ready, back, zero,
                        inc=s_lev if i == 8 else True)
                ra, rt, kt = R, t1, (s_lev, B + 1) if i == 8 else t2
                if i < 8:
                    T3 = T_[:, 0:512 // h].rearrange("p (n two) -> p n two", two=2)
                    nb = 256 // h
                    tP = tt(k, k.dve, Ph[:, :, 1, :], Ph[:, :, 1, :], T3[:, :, 0:1].broadcast_to([P, nb, h]),
                            ALU.mult, t1, tT)
                    tQ = tt(k, k.dve, Qh[:, :, 0, :], Qh[:, :, 0, :], T3[:, :, 1:2].broadcast_to([P, nb, h]),
                            ALU.mult, t2, tT)
                    T_ = TT[i % 2]
                    tT = tt(k, k.dve, T_[:, 0:nb], T3[:, :, 0], T3[:, :, 1], ALU.mult, tT)
            for hd in range(2):
                q = slice(64 * hd, 64 * hd + 64)
                bk = k.bank[hd + 2 * (n % 2)]
                free = (s_off, B) if i == 1 else merged(B - 1, 7, hd) if i == 0 else merged(B, i - 2, hd)
                cols = [(128 * j, 128 * j, 128 * j) for j in range(4)] if i < 8 else [(0, 0, 128), (128, 256, 384)]
                for j, (o, a, b) in enumerate(cols):
                    mm(k, bk[:, o:o + 128], Kx[q, a:a + 128], ra[q, b:b + 128], rt, kt, free,
                       inc=s_prod if j == len(cols) - 1 else None)
            if i >= 1:
                merge(i - 1)
        for hd in range(2):
            cp(k, k.act, off[hd][B % 2], k.bank[hd + 2 * (n % 2)][:, 0:256], multiplied(8, hd), (s_ym, B - 1),
               inc=s_off if hd else True)
        y = k.bank[7]
        for hd in range(2):
            for j in range(4):
                o = y[:, 128 * j + 64 * hd:128 * j + 64 * hd + 64]
                vs = lambda q: v[:, 128 * q + 64 * hd:128 * q + 64 * hd + 64]
                mm(k, o, AT[hd][:, 128 * j:128 * j + 128], vs(j), merged(B, 7, 1), taken(B, VP), (s_yo, B),
                   stop=(j % 2 == 0))
                if j % 2:
                    b = j // 2
                    mm(k, o, off[hd][B % 2][:, 128 * b:128 * b + 128], vs(j - 1), (s_off, B + 1), start=False,
                       inc=s_ym if j == 3 and hd == 1 else None)
        cp(k, k.act, yall[:, 512 * B:512 * B + 512], y[:, :], (s_ym, B + 1), inc=s_yo)
        for q in range(8):
            c, n = 512 * B + 64 * q, 8 * B + q
            a = k.dve.do(lambda e, q=q, c=c: e.bn_stats(st[q], yall[:, c:c + 64]), (s_yo, B + 1), (s_st, n - 7))
            k.dve.do(lambda e, q=q, n=n: e.bn_aggr(mvy[:, 2 * n:2 * n + 2], st[q]), a, inc=s_st)

    for B in range(9):
        if B < 8:
            front(B)
        if B >= 1:
            pairs(B - 1)
    mv2 = mvy.rearrange("p (t c) -> p t c", c=2)
    t = ts(k, k.dve, sd, mv2[:, :, 1], 2e-5, None, ALU.add, None, (s_st, 64))
    t = act(k, sd, sd, ACT.Sqrt, t)
    t_sd = k.dve.do(lambda e: e.reciprocal(sd, sd), t)
    k.phase_end = [t_sd]
    enter(k)
    ynT, oo = xin[0:2], xin[2:4]
    s_turned, s_yn, s_out, s_gated, s_yt, s_x = sems(k, "r2", "turned", "yn", "out", "gated", "yt", "x")
    for B in range(8):
        y = yall[:, 512 * B:512 * B + 512]
        for q in range(8):
            c, n = y[:, 64 * q:64 * q + 64], 8 * B + q
            t = ts(k, k.dve, c, c, mvy[:, 2 * n:2 * n + 1], sd[:, n:n + 1], ALU.subtract, ALU.mult, t_sd)
        y4 = y.rearrange("p (t c) -> p t c", t=4)
        t = tt(k, k.dve, y4, y4, w["gam"].unsqueeze(1).broadcast_to([P, 4, 128]), ALU.mult, t)
        t = tt(k, k.dve, y4, y4, w["bet"].unsqueeze(1).broadcast_to([P, 4, 128]), ALU.add, t)
        t = tt(k, k.dve, y, y, gall[:, 512 * B:512 * B + 512], ALU.mult, t)
        p, q_, yn, o = k.bank[B % 2], k.bank[2 + B % 2], ynT[B % 2], oo[B % 2]
        for j in range(4):
            tr(k, p[:, 128 * j:128 * j + 128], y[:, 128 * j:128 * j + 128], t, (s_yn, B - 1),
               inc=s_turned if j == 3 else None)
        cp(k, k.act, yn, p[:, :], (s_turned, B + 1), (s_out, B - 1), inc=s_yn)
        mm(k, q_[:, :], w["WoT"], yn, (s_yn, B + 1), (s_gated, B - 1), inc=s_out)
        for h in range(2):
            g = 192 + 32 + 2 * B + h
            act(k, o[:, 256 * h:256 * h + 256], q_[:, 256 * h:256 * h + 256], ACT.Copy, (s_out, B + 1), (s_yt, B - 1),
                scale=k.modT[:, g:g + 1], inc=s_gated if h else False)
        back_to_x(k, o, (s_gated, B + 1), B, k.bank[7], (s_x, B), s_yt, s_x)
        for j in range(4):
            stats(k, 4 * B + j, (s_x, B + 1))
    k.phase_end = [(k.s_aggr, k.n_stats)]


def program(nc, dram, out, phases):
    ctx = ExitStack()
    with ctx:
        k = setup(nc, ctx, dram, out)
        t_const = load(k, "const", k.C_tile)
        t_mods = load(k, "mods", k.T)
        k.sp.q.append(("do", lambda e: e.dma_start(k.X[:, :], dram["x"][:, :]).then_inc(k.dsem["x"], 16), None))
        t_x = (k.dsem["x"], 16)
        t_l0a = load(k, "l0a", k.W1)
        t_l0f = load(k, "l0f", k.W2)
        t_sm = load(k, "sm", k.W3)
        sm = views(k.W3, SM)
        for i in range(NT):
            stats(k, i, t_x)
        for e in (k.pe, k.dve, k.act, k.pool):
            e.wait(t_const)
        modulation(k, t_const, t_mods)
        first, last = phases
        t_w1, t_w2 = t_l0a, t_l0f

        def region():
            return Region(k.T, TW)

        if first <= 0 <= last:
            layernorm(k, 0, 0, region())
            attention(k, 0, "l0", views(k.W1, L0A), t_l0a)
        t_l1f = load(k, "l1f", k.W1, t_l0a, *k.phase_end)
        if first <= 1 <= last:
            r = region()
            gb = gate_rows(k, 0, r)
            layernorm(k, 0, 1, r)
            moe(k, 0, t_l0f, gb, r)
        t_l2f = load(k, "l2f", k.W2, t_l0f, *k.phase_end)
        if first <= 2 <= last:
            layernorm(k, 1, 0, region())
            w = dict(sm, wo=sm["wproj"], bo=sm["bproj"])
            attention(k, 1, "l1", w, t_sm)
        if first <= 3 <= last:
            layernorm(k, 1, 1, region())
            soft_moe(k, t_l1f)
        if first <= 4 <= last:
            layernorm(k, 2, 0, region())
            rwkv(k, sm, t_sm, t_l1f)
        t_l3f = load(k, "l3f", k.W1, t_l1f, *k.phase_end)
        if first <= 5 <= last:
            r = region()
            gb = gate_rows(k, 2, r)
            layernorm(k, 2, 1, r)
            moe(k, 2, t_l2f, gb, r)
        if first <= 6 <= last:
            layernorm(k, 3, 0, region())
            w = dict(sm, wo=sm["o3"], bo=sm["bo3"])
            attention(k, 3, "l3", w, t_sm)
        if first <= 7 <= last:
            r = region()
            gb = gate_rows(k, 3, r)
            layernorm(k, 3, 1, r)
            moe(k, 3, t_l3f, gb, r)
        for t in k.phase_end:
            k.sp.wait(t)
        k.sp.q.append(("do", lambda e: e.dma_start(
            out.rearrange("b (t p) d -> p (b t) d", p=128),
            k.X[:, :].rearrange("p (i d) -> p i d", d=128)).then_inc(k.dsem["out"], 16), None))
        for t in (t_l1f, t_l2f, t_l3f, (k.dsem["out"], 16)):
            k.sp.wait(t)

        block = ctx.enter_context(nc.Block())

        @block.sync
        def _(e):
            k.sp.flush(e)

        @block.tensor
        def _(e):
            k.pe.flush(e)

        @block.vector
        def _(e):
            k.dve.flush(e)

        @block.scalar
        def _(e):
            k.act.flush(e)

        @block.gpsimd
        def _(e):
            k.pool.flush(e)




def _constants():
    p = np.arange(128)
    q, kk = p[:, None], np.arange(128)[None, :]
    neg = np.float32(NEG)
    caus = np.where(kk <= q, 0, neg)
    old = np.where(kk > q, 0, neg)
    lev = [(p[:, None] == p[None, :])]
    h = 1
    while h < 128:
        s, t = p[:, None], p[None, :]
        lev.append((s // (2 * h) == t // (2 * h)) & ((s // h) % 2 == 0) & ((t // h) % 2 == 1))
        h *= 2
    sel = np.zeros((128, 128))
    sel[:32] = (p[None, :] % 32) == np.arange(32)[:, None]
    return {
        "ident": np.eye(128), "mwin": np.concatenate([old, caus], 1),
        "mcaus": np.concatenate([np.zeros((128, 128)), caus], 1), "ones": np.ones((128, 128)),
        "tri": (p[:, None] < p[None, :]), "same32": (p[:, None] % 32) == (p[None, :] % 32),
        "sel32": sel, "lev": np.concatenate(lev, 1),
    }


def _pack(spec, parts):
    out = np.zeros((128, width(spec)), np.float32)
    at = 0
    for n, w in spec:
        a = np.asarray(parts[n])
        if a.ndim == 1:
            a = a[:, None] if w == 1 else a[None, :]
        assert a.shape[1] == w and a.shape[0] <= 128, (n, a.shape, w)
        out[:a.shape[0], at:at + w] = a
        at += w
    return out


def _rows(a):
    return np.broadcast_to(np.asarray(a).reshape(1, -1), (128, np.asarray(a).size))


def _put(rows, at, a):
    out = np.zeros((rows, a.shape[1]), a.dtype)
    out[at:at + a.shape[0]] = a
    return out


def _spread(a):
    out = np.zeros((a.shape[0], 2, 2, 2, 2, 32), a.dtype)
    out[..., :8] = a.reshape(-1, 2, 2, 2, 2, 8).transpose(0, 1, 4, 2, 3, 5)
    return out.reshape(a.shape[0], 512)


def _layouts(i):
    A = {n: np.asarray(v) for n, v in i.items()}
    cat = np.concatenate
    g = {}
    g["const"] = _constants()
    g["mods"] = {}
    for l in range(4):
        g["mods"][f"c{l}"] = A[f"L{l}_c"].T
        g["mods"][f"w{l}"] = A[f"L{l}_wmod"]
    turn0 = lambda a: a.reshape(8, 2, 2, 2, 64, -1).transpose(0, 1, 3, 2, 4, 5).reshape(4096, -1)
    wk = A["L0_attn_Wk"].reshape(8, 64, 128)
    bk = A["L0_attn_bk"].reshape(8, 64)
    g["l0a"] = {
        "wq": turn0(A["L0_attn_Wq"]).T, "wo": A["L0_attn_Wo"].T.reshape(32, 128, 128).transpose(1, 0, 2).reshape(128, 4096),
        "wk": cat([wk, wk], 1).reshape(1024, 128).T, "wv": A["L0_attn_Wv"].T,
        "bq": turn0(A["L0_attn_bq"]).reshape(32, 128).T, "bk": cat([bk, bk], 1).T, "bv": _rows(A["L0_attn_bv"]),
        "bo": A["L0_attn_bo"], "sink": _rows(A["L0_attn_sinks"]),
    }
    wd = A["L0_ffn_w_down"]
    w2 = np.zeros((128, 8, 2, 128), np.float32)
    w2[0:64, :, 0] = wd[0::2].transpose(1, 0, 2)
    w2[64:128, :, 1] = wd[1::2].transpose(1, 0, 2)
    up = lambda a: a.transpose(1, 0, 2).reshape(128, -1)
    g["l0f"] = {
        "gk": A["L0_ffn_gate_kernel"], "gb": _rows(A["L0_ffn_gate_bias"]), "w1": up(A["L0_ffn_w_gate"]),
        "w3": up(A["L0_ffn_w_up"]), "w2": w2.reshape(128, 2048), "sw1": A["L0_ffn_sw_gate"],
        "sw3": A["L0_ffn_sw_up"], "sw2": A["L0_ffn_sw_down"],
    }
    pb = A["L1_ffn_phi_b"]
    g["l1f"] = {
        "phi": A["L1_ffn_phi_w"].T, "phib": _rows(pb), "phic": pb.reshape(16, 128).T, "ew": up(A["L1_ffn_expert_w"]),
    }
    eb = A["L1_ffn_expert_b"].reshape(16, 4, 1, 128)
    g["eb"] = {"eb": np.broadcast_to(eb, (16, 4, 32, 128)).reshape(16, 128, 128).transpose(1, 0, 2).reshape(128, 2048)}
    Bl = A["L2_attn_B_lora"]
    col = lambda n: A[n].reshape(-1)
    g["sm"] = {
        "wlat": cat([A["L1_attn_wq_lat"], A["L1_attn_wk_lat"], A["L1_attn_wv_lat"]], 1),
        "wq96": _spread(_put(96, 0, A["L1_attn_wq_heads"])), "wk96": _spread(_put(96, 32, A["L1_attn_wk_heads"])),
        "wv96": _put(96, 64, A["L1_attn_wv_heads"]), "wproj": A["L1_attn_w_proj"], "bproj": A["L1_attn_b_proj"],
        "miux": col("L2_attn_miu_x"), "lam": A["L2_attn_lambda_"].reshape(5, 128).T, "A": A["L2_attn_A_lora"],
        "B": cat([_put(128, 32 * f if f < 4 else 0, Bl[f]) for f in range(5)], 1),
        "tdmiu": col("L2_attn_td_miu"), "tdA": A["L2_attn_td_A"], "tdB": A["L2_attn_td_B"], "u": col("L2_attn_u"),
        "WrT": A["L2_attn_Wr"].T, "WkT": A["L2_attn_Wk"].T, "WvT": A["L2_attn_Wv"].T, "WgT": A["L2_attn_Wg"].T,
        "WoT": A["L2_attn_Wo"].T, "gam": _rows(A["L2_attn_gn_gamma"]), "bet": _rows(A["L2_attn_gn_beta"]),
        "q3": _spread(A["L3_attn_Wq"].T), "k3": _spread(A["L3_attn_Wk"].T), "v3": A["L3_attn_Wv"].T, "o3": A["L3_attn_Wo"].T,
        "bq3": _spread(A["L3_attn_bq"][None]).reshape(4, 128).T, "bk3": _spread(A["L3_attn_bk"][None]).reshape(4, 128).T, "bv3": _rows(A["L3_attn_bv"]), "bo3": A["L3_attn_bo"],
    }
    tw = lambda a: a.transpose(2, 0, 1).reshape(128, -1)
    g["l2f"] = {
        "wg": A["L2_ffn_Wg"].T, "w1": tw(A["L2_ffn_W1"]), "b1": A["L2_ffn_b1"].T, "w3": tw(A["L2_ffn_W3"]),
        "b3": A["L2_ffn_b3"].T, "w2": tw(A["L2_ffn_W2"]), "b2": A["L2_ffn_b2"],
    }
    w2 = A["L3_ffn_W2"].reshape(8, 128, 2, 128)
    g["l3f"] = {
        "wg": A["L3_ffn_Wg"].T, "w1": tw(A["L3_ffn_W1"]), "w3": tw(A["L3_ffn_W3"]),
        "w2": w2.transpose(3, 0, 2, 1).reshape(128, 2048),
    }
    out = {n: _pack(PACKS[n], g[n]) for n in PACKS}
    out["x"] = A["L0_attn_x"].reshape(32, 128, 128).transpose(1, 0, 2).reshape(128, 4096)
    return out


def kernel(**inputs):
    import concourse.bacc as _bacc
    from concourse.bass_utils import run_bass_kernel_spmd as _run

    nc = _bacc.Bacc("TRN2", target_bir_lowering=False, num_devices=1)
    arrays, dram = {}, {}
    for name, a in _layouts(inputs).items():
        a = np.ascontiguousarray(a)
        arrays[f"in_{name}_dram"] = a
        dram[name] = nc.dram_tensor(f"in_{name}_dram", a.shape, F32, kind="ExternalInput").ap()
    out = nc.dram_tensor("out_0_dram", (NB, 256, 128), F32, kind="ExternalOutput").ap()
    program(nc, dram, out, PHASES)
    r = _run(nc, [arrays], core_ids=[0])
    return r.results[0]["out_0_dram"]
```

```python
from contextlib import ExitStack

import numpy as np

import concourse.bass as bass
from concourse import mybir

F32 = mybir.dt.float32
I32 = mybir.dt.int32
F32R = mybir.dt.float32r
ALU = mybir.AluOpType
ACT = mybir.ActivationFunctionType
AX = mybir.AxisListType.X
P = 128
NB = 16
NT = 32
PHASES = (0, 7)
NEG = -1e30
TW = 12060

CONST = [("ident", 128), ("mwin", 256), ("mcaus", 256), ("ones", 128), ("tri", 128),
         ("same32", 128), ("sel32", 128), ("lev", 8 * 128), ("split", 4)]
MODS = [(f"{n}{l}", w) for l in range(4) for n, w in (("c", 16), ("w", 768))]
L0A = [("wq", 4096), ("wo", 4096), ("wk", 1024), ("wv", 512), ("bq", 32), ("bk", 8),
       ("bv", 512), ("bo", 1), ("sink", 64)]
L0F = [("gk", 16), ("gb", 16), ("w1", 1024), ("w3", 1024), ("w2", 2048), ("sw1", 128),
       ("sw3", 128), ("sw2", 128)]
L1F = [("phi", 2048), ("phib", 2048), ("phic", 16), ("ew", 8192)]
EB = [("eb", 2048)]
SM = [("wlat", 96), ("wq96", 512), ("wk96", 512), ("wv96", 128), ("wproj", 512), ("bproj", 1),
      ("miux", 1), ("lam", 5), ("A", 160), ("B", 640), ("tdmiu", 1), ("tdA", 64), ("tdB", 128),
      ("u", 1), ("WrT", 128), ("WkT", 128), ("WvT", 128), ("WgT", 128), ("WoT", 128),
      ("gam", 128), ("bet", 128),
      ("q3", 512), ("k3", 512), ("v3", 128), ("o3", 512), ("bq3", 4), ("bk3", 4), ("bv3", 128),
      ("bo3", 1)]
L2F = [("wg", 16), ("w1", 2048), ("b1", 16), ("w3", 2048), ("b3", 16), ("w2", 2048), ("b2", 128)]
L3F = [("wg", 8), ("w1", 2048), ("w3", 2048), ("w2", 2048)]
PACKS = {"const": CONST, "mods": MODS, "l0a": L0A, "l0f": L0F, "l1f": L1F, "eb": EB, "sm": SM,
         "l2f": L2F, "l3f": L3F}


def width(spec):
    return sum(w for _, w in spec)


class Eng:

    def __init__(self, sem):
        self.q, self.sem, self.n = [], sem, 0

    def wait(self, *waits):
        for w in waits:
            if w is not None and w[1] > 0:
                self.q.append(("wait", *w))

    def do(self, fn, *waits, inc=True):
        self.wait(*waits)
        if inc is True:
            self.n += 1
            self.q.append(("do", fn, self.sem))
            return (self.sem, self.n)
        self.q.append(("do", fn, inc or None))

    def flush(self, eng):
        for kind, a, b in self.q:
            if kind == "wait":
                eng.wait_ge(a, b)
            else:
                r = a(eng)
                if b is not None:
                    r.then_inc(b, 1)


class Region:

    def __init__(self, ap, width_):
        self.ap, self.w, self.at = ap, width_, 0

    def get(self, n):
        a = self.at
        self.at += n
        assert self.at <= self.w, (self.at, self.w)
        return self.ap[:, a:a + n]


def views(tile, spec, at=0):
    out = {}
    for n, w in spec:
        out[n] = tile[:, at:at + w]
        at += w
    return out


class K:
    pass


def sems(k, phase, *names):
    return [n and k.ctx.enter_context(k.nc.semaphore(f"{phase}_{n}")) for n in names]


def setup(nc, ctx, dram, out):
    k = K()
    k.nc, k.ctx, k.dram, k.out = nc, ctx, dram, out
    sem = lambda n: ctx.enter_context(nc.semaphore(n))
    k.pe, k.dve, k.act, k.pool, k.sp = (Eng(sem(f"s_{n}")) for n in ("pe", "dve", "act", "pool", "sp"))
    k.dsem = {n: sem(f"d_{n}") for n in list(PACKS) + ["x", "out", "sm2"]}
    sb = lambda n, w: ctx.enter_context(nc.sbuf_tensor(n, [P, w], F32))
    k.X = sb("X", 4096)
    k.HT = sb("HT", 4096)
    k.W1 = sb("W1", width(L1F))
    k.W2 = sb("W2", width(L2F))
    k.W3 = sb("W3", width(SM))
    k.C_tile = sb("C", width(CONST))
    k.C = views(k.C_tile, CONST)
    k.modT = sb("modT", 4 * 96)
    k.gbbc = sb("gbbc", 2048)
    k.MV = sb("MV", 64)
    k.rs = sb("rs", 64)
    k.T = sb("T", TW)
    k.QK = ctx.enter_context(nc.sbuf_tensor("QK", [P, 4096], F32R))
    k.st6 = sb("st6", 24)
    k.s_aggr, k.s_h, k.s_turned = sem("s_aggr"), sem("s_h"), sem("s_turned")
    k.s_gate = [sem(f"s_gate_{n}") for n in ("diag", "row", "rows")]
    k.n_stats, k.norms, k.gates = 0, 0, 0
    k.bank = [ctx.enter_context(nc.psum_tensor(f"ps{i}", [P, 512], F32)) for i in range(8)]
    k.phase_end = []
    return k


def load(k, name, tile, *waits):
    w = width(PACKS[name])
    src = k.dram[name]
    for wt in waits:
        k.sp.wait(wt)
    k.sp.q.append(("do", lambda e: e.dma_start(tile[:, 0:w], src[:, :]).then_inc(k.dsem[name], 16), None))
    return (k.dsem[name], 16)


def mm(k, out, lhsT, rhs, *waits, start=True, stop=True, inc=None):
    return k.pe.do(lambda e: e.matmul(out, lhsT, rhs, start=start, stop=stop), *waits, inc=inc)


def tr(k, out, in_, *waits, inc=None):
    return k.pe.do(lambda e: e.transpose(out, in_, k.C["ident"]), *waits, inc=inc)


def act(k, out, in_, f, *waits, bias=0.0, scale=1.0, inc=True):
    return k.act.do(lambda e: e.activation(out, in_, f, bias=bias, scale=scale), *waits, inc=inc)


def tt(k, eng, out, a, b, op, *waits, inc=True):
    return eng.do(lambda e: e.tensor_tensor(out, a, b, op), *waits, inc=inc)


def ts(k, eng, out, a, s1, s2, op0, op1, *waits, inc=True):
    if op1 is None:
        return eng.do(lambda e: e.tensor_scalar(out, a, s1, None, op0), *waits, inc=inc)
    return eng.do(lambda e: e.tensor_scalar(out, a, s1, s2, op0, op1), *waits, inc=inc)


def stt(k, out, a, s, b, op0, op1, *waits, inc=True):
    return k.dve.do(lambda e: e.scalar_tensor_tensor(out=out, in0=a, scalar=s, in1=b, op0=op0, op1=op1), *waits,
                    inc=inc)


def red(k, out, a, op, *waits, inc=True):
    return k.dve.do(lambda e: e.tensor_reduce(out, a, AX, op), *waits, inc=inc)


def cp(k, eng, out, a, *waits, inc=True):
    if eng is k.act:
        return act(k, out, a, ACT.Copy, *waits, inc=inc)
    return eng.do(lambda e: e.tensor_copy(out, a), *waits, inc=inc)


def stats(k, i, x_ready):
    n = k.n_stats
    k.n_stats += 1
    st = k.st6[:, 6 * (n % 4):6 * (n % 4) + 6]
    a = k.dve.do(lambda e: e.bn_stats(st, k.X[:, i * 128:(i + 1) * 128]), x_ready, (k.s_aggr, n - 3))
    k.dve.do(lambda e: e.bn_aggr(k.MV[:, 2 * i:2 * i + 2], st), a, inc=k.s_aggr)


def modulation(k, t_const, t_mods):
    M = views(k.T, MODS)
    r = Region(k.T, TW)
    r.at = width(MODS)
    e1, e2, sT, a, b = r.get(64), r.get(64), r.get(64), r.get(128), r.get(128)
    for l in range(4):
        t = act(k, e1[:, 16 * l:16 * l + 16], M[f"c{l}"], ACT.Exp, t_mods, scale=-1.0)
    t = ts(k, k.dve, e1, e1, 1.0, None, ALU.add, None, t)
    t = k.dve.do(lambda e: e.reciprocal(e2, e1), t)
    for l in range(4):
        s = slice(16 * l, 16 * l + 16)
        t_s = tt(k, k.dve, sT[:, s], M[f"c{l}"], e2[:, s], ALU.mult, t, t_mods)
    for l in range(4):
        for j in range(6):
            m = mm(k, k.bank[l][:, 16 * j:16 * j + 16], M[f"w{l}"][:, 128 * j:128 * j + 128],
                   sT[:, 16 * l:16 * l + 16], t_s, inc=(j == 5))
        t = cp(k, k.dve, k.modT[:, 96 * l:96 * l + 96], k.bank[l][:, 0:96], m)
    v = k.modT[:, :].rearrange("p (l h j b) -> p (l h) j b", h=2, j=3, l=4)
    t1 = ts(k, k.dve, v[:, :, 1, :], v[:, :, 1, :], 1.0, None, ALU.add, None, t)
    g = v[:, :, 2, :]
    a, b = (x.rearrange("p (l b) -> p l b", l=8) for x in (a, b))
    s = ts(k, k.dve, a, g, 0.0, 2.0, ALU.is_ge, ALU.mult, t)
    s = ts(k, k.dve, a, a, -1.0, None, ALU.add, None, s)
    x = stt(k, b, g, -1.0, g, ALU.mult, ALU.max, t)
    x = ts(k, k.dve, b, b, 0.25, None, ALU.max, None, x)
    k.t_mod = tt(k, k.dve, g, a, b, ALU.mult, s, x, t1)
    k.phase_end = [k.t_mod]


def gate_rows(k, l, region):
    (s_diag, s_row, s_rows), g = k.s_gate, 4 * k.gates
    k.gates += 1
    n = region.at
    scr = [region.get(512) for _ in range(2)]
    region.at = n
    gb = k.modT[:, 96 * l + 80:96 * l + 96]
    for h in range(4):
        s, ps = scr[h % 2], k.bank[7 - h % 2]
        tt(k, k.dve, s.rearrange("p (b d) -> p b d", b=4), k.C["ident"].unsqueeze(1).broadcast_to([P, 4, 128]),
           gb[:, 4 * h:4 * h + 4].unsqueeze(2).broadcast_to([P, 4, 128]), ALU.mult, k.t_mod, *k.phase_end,
           (s_row, g + h - 1), inc=s_diag)
        mm(k, ps[:, :], k.C["ones"], s, (s_diag, g + h + 1), (s_rows, g + h - 1), inc=s_row)
        cp(k, k.act, k.gbbc[:, 512 * h:512 * h + 512], ps[:, :], (s_row, g + h + 1), inc=s_rows)
    return (s_rows, g + 4)


def layernorm(k, l, sub, region):
    var = k.MV[:, :].rearrange("p (t c) -> p t c", c=2)[:, :, 1]
    mean = k.MV[:, :].rearrange("p (t c) -> p t c", c=2)[:, :, 0]
    rstd = k.rs[:, 0:32]
    v1 = k.rs[:, 32:64]
    a = ts(k, k.dve, v1, var, 1e-5, None, ALU.add, None, (k.s_aggr, k.n_stats), *k.phase_end)
    a = act(k, v1, v1, ACT.Sqrt, a)
    a = k.dve.do(lambda e: e.reciprocal(rstd, v1), a)
    n0 = region.at
    xn = [region.get(128) for _ in range(8)]
    region.at = n0
    s_c = 96 * l + 48 * sub
    s_turned, t0, h0 = k.s_turned, 32 * k.norms, 16 * k.norms
    for c in range(NB // 2):
        ps = k.bank[c % 4]
        for j in range(4):
            i = 4 * c + j
            x = xn[i % 8]
            d = ts(k, k.dve, x, k.X[:, i * 128:(i + 1) * 128], mean[:, i:i + 1], rstd[:, i:i + 1],
                   ALU.subtract, ALU.mult, a, (s_turned, t0 + i - 7 if i > 7 else 0))
            tr(k, ps[:, 128 * j:128 * j + 128], x, d, (k.s_h, h0 + 2 * (c - 3) if c > 3 else 0), inc=s_turned)
        for b in (2 * c, 2 * c + 1):
            act(k, k.HT[:, b * 256:(b + 1) * 256], ps[:, (b % 2) * 256:(b % 2) * 256 + 256],
                ACT.Identity, (s_turned, t0 + 4 * c + 4), scale=k.modT[:, s_c + 16 + b:s_c + 17 + b],
                bias=k.modT[:, s_c + b:s_c + b + 1], inc=k.s_h)
    k.norms += 1
    k.phase_end = [(k.s_h, 16 * k.norms)]


def enter(k, *more):
    for e in (k.pe, k.dve, k.act, k.pool):
        for t in list(k.phase_end) + list(more):
            e.wait(t)


def attention(k, l, layer, w, t_w):
    nG, HG, d = {"l0": (8, 8, 64), "l1": (1, 16, 8), "l3": (1, 16, 8)}[layer]
    big = layer == "l0"
    CH = 4
    scale = d ** -0.5
    per = 2 * HG // 4
    groups, units = NB * nG, NB * nG * per
    (s_zero, s_half, s_masked, s_shift, s_sshift, s_exps, s_sexp, s_inv, s_diag, s_turn, s_even, s_odd, s_values, s_o,
     s_side, s_free, s_high, s_low, s_out, s_y, s_yread, s_x) = sems(
         k, layer + "a", "zero", "half", None if layer == "l3" else "masked", "shift", big and "sshift" or None, "exps",
         big and "sexp" or None, "inv", "diag", "turn", "even", "odd", "values", "o", "side", "free",
         None if big else "high", None if big else "low",
         *((None,) * 4 if layer == "l3" else ("out", "y", "yread", "x")))
    R = Region(k.T, TW)
    many = lambda n, w_: [R.get(w_) for _ in range(n)]
    if big:
        qT, kT = many(2, 1024), many(2, 256)
    else:
        qT, kT = ([k.QK[:, 1024 * i:1024 * i + 1024] for i in j] for j in ((0, 1), (2, 3)))
    nv = 3 if big else 2
    va = many(nv, 128 if big else 2 * HG * 32)
    diag = [k.gbbc[:, 512 * i:512 * i + 512] for i in range(3)]
    Sm = None if layer == "l3" else many(3, 1024)
    Pr = Sm if layer == "l1" else many(3, 1024)
    PT = [k.W3[:, 1024 * i:1024 * i + 1024] for i in range(2)] if big else many(2, 1024)
    mxs, ngs, ess, dens, rins, tks = (many(4, 4) for _ in range(6))
    oT = many(2, CH * 256)
    yT = R.get(256)
    lats = many(2, 256) if layer == "l1" else [None, None]
    nsink = R.get(64)
    whole = None if big else many(2, 512)
    b_ = k.bank
    if layer == "l3":
        Sb, Tb, Ob, side, acc = b_[0:4], b_[4:6], b_[6], b_[7], b_[7]
    else:
        Sb, Tb, Ob, side, acc = b_[0:3], b_[3:5], b_[5], b_[6], b_[7]
    h0 = 16 * (k.norms - 1)

    def place(i):
        n, r = divmod(i, per)
        qt, s4 = divmod(r, HG // 4)
        return n, qt, s4, 2 if (layer == "l3" or qt == 1) else 1

    def turns(i):
        n, r = divmod(i, per)
        if layer == "l3":
            return 2 * i
        return n * (per + per // 2) + r + max(0, r - per // 2)

    parts = {"l0": ("q0", "q1", "kv"), "l1": ("lat", "q0", "q1", "k0", "k1", "v"),
             "l3": ("q0", "q1", "k0", "k1", "v")}[layer]
    late = 4
    before, after = {}, {}
    for n in range(groups):
        for p, part in enumerate(parts):
            at = max(0, n * per - (4 if big else 7) + p)
            before.setdefault(at, []).append((part, n))
            if not big and part in ("q0", "q1", "k0", "k1"):
                (before if at == 0 else after).setdefault(at, []).append(("low " + part, n))
        at = n * per + per - 1 + late
        after.setdefault(at, []).append(("out", n))
        if n % nG == nG - 1:
            after.setdefault(at + 1, []).append(("x", n))
    order = []
    for i in range(units + late + 5):
        first = [("scores", i)] if i < units else []
        if 1 <= i < units + 1:
            first.append(("weigh", i - 1))
        if 2 <= i < units + 2:
            first.append(("turn", i - 2))
        order += before.get(i, []) + first if i == 0 else first + before.get(i, [])
        if i < units:
            order.append(("exps", i))
        if 3 <= i < units + 3:
            order.append(("values", i - 3))
        order += after.get(i, [])
    in_side = ("lat", "q0", "q1", "k0", "k1", "kv", "v")
    if acc is side:
        in_side += ("out", "x")
    uses = {step: u for u, step in enumerate(s for s in order if s[0] in in_side)}

    def side_filled(step, n):
        return (s_side, uses[step, n] + 1) if n >= 0 else None

    def side_taken(step, n):
        return (s_free, uses[step, n] + 1) if n >= 0 else None

    def side_before(step, n):
        return (s_free, uses[step, n])

    def q_or_k(part, n, wt, bias, x, x_ready, dst):
        j = int(part[1])
        k.pe.wait(side_before(part, n), x_ready)
        for c in range(2):
            mm(k, side[:, 256 * c:256 * c + 256], wt[:, 128 * (2 * j + c):128 * (2 * j + c) + 128], x, inc=s_side if c == 1 else None)
        if not big:
            m = part_no(part, n)
            t = whole[m % 2]
            for c in range(2):
                o, i = t[:, 256 * c:256 * c + 256], side[:, 256 * c:256 * c + 256]
                waits, inc = [side_filled(part, n), (s_low, m - 1)], s_free if c == 1 else False
                if bias is None:
                    cp(k, k.dve, o, i, *waits, inc=inc)
                else:
                    ts(k, k.dve, o, i, bias[:, 2 * j + c:2 * j + c + 1], None, ALU.add, None, *waits, inc=inc)
            sign = k.C["split"][:, 0:1] if part[0] == "q" else k.C["split"][:, 2:3]
            act(k, dst[:, 512 * j:512 * j + 512], t, ACT.Copy, side_taken(part, n),
                (s_half, 2 * per * (n - 1)), scale=sign, inc=s_high)
            return
        eng = k.act if part == "q0" else k.dve
        o = dst[:, 512 * j:512 * j + 512]
        for c in range(2):
            waits, inc = [side_filled(part, n), (s_half, 2 * per * (n - 1))], s_free if c == 1 else False
            s = slice(256 * c, 256 * c + 256)
            bb = bias[:, 2 * j + c:2 * j + c + 1]
            if eng is k.act:
                act(k, o[:, s], side[:, s], ACT.Identity, *waits, bias=bb, inc=inc)
            else:
                ts(k, eng, o[:, s], side[:, s], bb, None, ALU.add, None, *waits, inc=inc)

    def part_no(part, n):
        return 4 * n + ("q0", "q1", "k0", "k1").index(part)

    def low(part, n):
        m, j = part_no(part, n), int(part[1])
        dst = (qT if part[0] == "q" else kT)[n % 2][:, 512 * j:512 * j + 512]
        mask = k.C["split"][:, 1:2] if part[0] == "q" else k.C["split"][:, 3:4]
        k.dve.do(lambda e: e.scalar_tensor_tensor(out=dst, in0=whole[m % 2], scalar=mask, in1=dst.bitcast(F32),
                                                  op0=ALU.mult, op1=ALU.subtract), (s_high, m + 1), inc=s_low)

    def project(part, n):
        b, g = divmod(n, nG)
        x, x_ready = k.HT[:, b * 256:(b + 1) * 256], (k.s_h, h0 + b + 1)
        q, kt, v, lat = qT[n % 2], kT[n % 2], va[n % nv], lats[n % 2]
        v_free = (s_values, per * (n + 1 - nv))
        if part == "lat":
            mm(k, side[0:96, 0:256], w["wlat"], x, side_before(part, n), x_ready, inc=s_side)
            act(k, lat[0:96, :], side[0:96, 0:256], ACT.Copy, side_filled(part, n), side_filled("v", n - 2),
                inc=s_free)
            return
        if layer == "l1":
            x, x_ready = lat[0:96, :], side_taken("lat", n)
            wq, wk, bq, bk, wv = w["wq96"][0:96, :], w["wk96"][0:96, :], None, None, w["wv96"][0:96, :]
        elif layer == "l3":
            wq, wk, bq, bk, wv = w["q3"], w["k3"], w["bq3"], w["bk3"], w["v3"]
        else:
            wq, bq = w["wq"][:, 512 * g:512 * g + 512], w["bq"][:, 4 * g:4 * g + 4]
        if part[0] == "q":
            return q_or_k(part, n, wq, bq, x, x_ready, q)
        if part in ("k0", "k1"):
            return q_or_k(part, n, wk, bk, x, x_ready, kt)
        if part == "kv":
            mm(k, side[:, 0:256], w["wk"][:, 128 * g:128 * g + 128], x, side_before(part, n), x_ready)
            for j in range(2):
                mm(k, side[:, 256 + 64 * j:320 + 64 * j], x[:, 128 * j:128 * j + 128],
                   w["wv"][:, 64 * g:64 * g + 64], inc=s_side if j == 1 else None)
            ts(k, k.dve, kt, side[:, 0:256], w["bk"][:, g:g + 1], None, ALU.add, None, side_filled(part, n),
               (s_half, 2 * per * (n - 1)), inc=False)
            bv = w["bv"][:, 64 * g:64 * g + 64].unsqueeze(1).broadcast_to([P, 2, 64])
            tt(k, k.dve, v.rearrange("p (t w) -> p t w", t=2),
               side[:, 256:384].rearrange("p (t w) -> p t w", t=2), bv, ALU.add, v_free, inc=s_free)
            return
        for j in range(2):
            mm(k, side[:, 128 * j:128 * j + 128], x[:, 128 * j:128 * j + 128], wv, side_before(part, n), x_ready,
               inc=s_side if j == 1 else None)
        v4 = v.rearrange("p (t h w) -> p t h w", t=2, h=16)
        p4 = side[:, 0:256].rearrange("p (t h w) -> p t h w", t=2, h=16)
        for j in range(2):
            o, inc = v4[:, j, :, 0:8], s_free if j == 1 else False
            if layer == "l1":
                cp(k, k.dve, o, p4[:, j], side_filled(part, n), v_free, inc=inc)
            else:
                bv = w["bv3"].rearrange("p (h w) -> p h w", h=16)
                tt(k, k.dve, o, p4[:, j], bv, ALU.add, side_filled(part, n), v_free, inc=inc)

    def scores(i):
        n, qt, s4, nk = place(i)
        q, kt, w_ = qT[n % 2], kT[n % 2], 128 * nk
        if big:
            k.pe.wait(side_taken(f"q{s4}", n), side_taken("kv", n))
        else:
            k.pe.wait((s_low, part_no(f"q{s4 // 2}", n) + 1), (s_low, part_no(f"k{s4 // 2}", n) + 1))
        for j in range(2):
            for p in range(2):
                half = 2 * i + p
                bk = Sb[half % len(Sb)]
                if big:
                    c, r, kk = 2 * s4 + j, slice(64 * p, 64 * p + 64), kt[:, 0:w_]
                else:
                    g = 2 * (s4 % 2) + p
                    c, r = 2 * (s4 // 2) + j, slice(32 * g, 32 * g + 32)
                    kk = kt[:, 256 * c:256 * c + w_]
                if j == 0:
                    k.pe.wait((s_exps, i - 1) if layer == "l3" else (s_masked, half - 2))
                mm(k, bk[:, w_ * j:w_ * j + w_], q[r, 256 * c + 128 * qt:256 * c + 128 * qt + 128], kk[r, :],
                   inc=s_half if j == 1 else None)

    def maximum(i):
        n, qt, s4, nk = place(i)
        w_, g = 128 * nk, n % nG
        mx, ng, tk = mxs[i % 4], ngs[i % 4], tks[i % 4]
        if layer == "l3":
            for p in range(2):
                t = red(k, mx[:, 2 * p:2 * p + 2], Sb[(2 * i + p) % 4][:, :].rearrange("p (h t) -> p h t", h=2),
                        ALU.max, (s_half, 2 * i + p + 1), (s_shift, i - 3))
        else:
            mask = k.C["mwin" if big else "mcaus"]
            mask = mask if nk == 2 else mask[:, 128:256]
            sm = Sm[i % 3]
            k.dve.wait((s_exps, i - 2) if big else (s_turn, turns(i - 2) if i > 2 else 0), (s_shift, i - 3))
            for p in range(2):
                bk = Sb[(2 * i + p) % 3]
                k.dve.wait((s_half, 2 * i + p + 1))
                for j in range(2):
                    h = 2 * p + j
                    k.dve.do(lambda e, h=h, j=j, bk=bk: e.tensor_tensor_reduce(
                        sm[:, 256 * h:256 * h + w_], bk[:, j * w_:j * w_ + w_], mask, 1.0, -3.0e38, ALU.add, ALU.max,
                        mx[:, h:h + 1]), inc=s_masked if j == 1 else False)
            t = (s_masked, 2 * i + 2)
        if big:
            q0 = 8 * g + 4 * s4
            stt(k, ng, mx, -scale, nsink[:, q0:q0 + 4], ALU.mult, ALU.min, t, (s_exps, i - 3), inc=s_shift)
            tt(k, k.dve, tk, ng, w["sink"][:, q0:q0 + 4], ALU.add, (s_shift, i + 1), (s_sexp, i - 3), inc=s_sshift)
        else:
            ts(k, k.dve, ng, mx, -scale, None, ALU.mult, None, t, (s_exps, i - 3), inc=s_shift)

    def exps(i):
        n, qt, s4, nk = place(i)
        w_, pr = 128 * nk, Pr[i % 3]
        k.act.wait((s_shift, i + 1), (s_turn, turns(i - 2) if i > 2 else 0), (s_inv, i - 3))
        for h in range(4):
            if layer == "l3":
                src = Sb[(2 * i + h // 2) % 4][:, (h % 2) * w_:(h % 2) * w_ + w_]
            else:
                src = Sm[i % 3][:, 256 * h:256 * h + w_]
            k.act.do(lambda e, h=h, src=src: e.activation(
                pr[:, 256 * h:256 * h + w_], src, ACT.Exp, bias=ngs[i % 4][:, h:h + 1], scale=scale,
                accum_out=dens[i % 4][:, h:h + 1]), inc=s_exps if h == 3 else False)
        if big:
            act(k, ess[i % 4], tks[i % 4], ACT.Exp, (s_sshift, i + 1), (s_inv, i - 3), inc=s_sexp)

    def weigh(i):
        den, rin = dens[i % 4], rins[i % 4]
        if big:
            t = tt(k, k.dve, den, den, ess[i % 4], ALU.add, (s_exps, i + 1), (s_sexp, i + 1))
        else:
            t = (s_exps, i + 1)
        k.dve.do(lambda e: e.reciprocal(rin, den), t, (s_diag, i - 3), inc=s_inv)
        tt(k, k.pool, diag[i % 3].rearrange("p (h q) -> p h q", h=4), k.C["ident"].unsqueeze(1).broadcast_to([P, 4, 128]),
           rin.unsqueeze(2).broadcast_to([P, 4, 128]), ALU.mult, (s_inv, i + 1), (s_turn, turns(i - 2) if i > 2 else 0),
           inc=s_diag)

    def turn(i):
        n, qt, s4, nk = place(i)
        for c in range(nk):
            t = turns(i) + c
            bk = Tb[t % 2]
            s_taken = (s_even, s_odd)[t % 2]
            k.pe.wait((s_diag, i + 1), (s_taken, t // 2))
            for h in range(4):
                mm(k, bk[:, 128 * h:128 * h + 128], Pr[i % 3][:, 256 * h + 128 * c:256 * h + 128 * c + 128],
                   diag[i % 3][:, 128 * h:128 * h + 128], inc=s_turn if h == 3 else None)
            cp(k, (k.act, k.dve)[t % 2], PT[i % 2][:, 512 * c:512 * c + 512], bk[:, :], (s_turn, t + 1),
               (s_values, i - 1), inc=s_taken)

    def values(i):
        n, qt, s4, nk = place(i)
        v, pt = va[n % nv], PT[i % 2]
        k.pe.wait(side_taken("kv" if big else "v", n), (s_o, i))
        for c in range(nk):
            t = turns(i) + c
            k.pe.wait(((s_even, s_odd)[t % 2], t // 2 + 1))
            if big:
                x = pt[:, 512 * c:512 * c + 512].rearrange("p (a r q) -> p r a q", a=2, r=2)
                tiles = [(Ob[64 * r:64 * r + 64, 0:256], v[:, 64 * c:64 * c + 64], x[:, r]) for r in range(2)]
            else:
                tiles = [(Ob[32 * h:32 * h + 32, 0:128], v[:, 32 * (16 * c + 4 * s4 + h):32 * (16 * c + 4 * s4 + h) + 32],
                          pt[:, 512 * c + 128 * h:512 * c + 128 * h + 128]) for h in range(4)]
            for j, (o, a, b) in enumerate(tiles):
                mm(k, o, a, b, start=(c == 0), stop=(c == nk - 1),
                   inc=s_values if (c == nk - 1 and j == len(tiles) - 1) else None)
        o3 = oT[n % 2].rearrange("p (c q) -> p c q", c=4)[:, :, 128 * qt:128 * qt + 128]
        if big:
            cp(k, k.dve, o3[:, 2 * s4:2 * s4 + 2, :], Ob[:, 0:256].rearrange("p (a q) -> p a q", a=2),
               (s_values, i + 1), out_filled(n - 2), inc=s_o)
        else:
            cp(k, k.dve, o3[:, s4, :], Ob[:, 0:128], (s_values, i + 1), out_filled(n - 2), inc=s_o)

    def out_filled(n):
        return side_filled("out", n) if acc is side else (s_out, n + 1)

    def out_taken(n):
        return side_taken("out", n) if acc is side else (s_y, n // nG + 1)

    def y_turned(n):
        return side_filled("x", n) if acc is side else (s_yread, n // nG + 1)

    def out(n):
        b, g = divmod(n, nG)
        free = side_before("out", n) if acc is side else (s_x, b)
        k.pe.wait(free, (s_o, (n + 1) * per))
        for c in range(CH):
            mm(k, acc[:, 0:256], w["wo"][:, (g * CH + c) * 128:(g * CH + c + 1) * 128],
               oT[n % 2][:, 256 * c:256 * c + 256], start=(g == 0 and c == 0),
               stop=(g == nG - 1 and c == CH - 1), inc=(s_side if acc is side else s_out) if c == CH - 1 else None)
        if g == nG - 1:
            ga = k.modT[:, 96 * l + 32 + b:96 * l + 33 + b]
            ts(k, k.dve, yT, acc[:, 0:256], w["bo"], ga, ALU.add, ALU.mult, out_filled(n), y_turned(n - nG),
               inc=s_free if acc is side else s_y)

    def to_x(n):
        b = n // nG
        for j in range(2):
            tr(k, acc[:, 128 * j:128 * j + 128], yT[:, 128 * j:128 * j + 128], out_taken(n),
               side_before("x", n) if acc is side else None,
               inc=(s_side if acc is side else s_yread) if j == 1 else None)
        x = k.X[:, b * 256:b * 256 + 256]
        tt(k, k.dve, x, x, acc[:, 0:256], ALU.add, y_turned(n), inc=s_free if acc is side else s_x)
        summed = side_taken("x", n) if acc is side else (s_x, b + 1)
        stats(k, 2 * b, summed)
        stats(k, 2 * b + 1, summed)

    enter(k, t_w)
    for v in va:
        k.pool.do(lambda e, v=v: e.memset(v, 0.0), inc=s_zero)
    if big:
        t = ts(k, k.dve, nsink, w["sink"], -1.0, None, ALU.mult, None)
        k.dve.wait(t)
    k.dve.wait((s_zero, nv))
    run = {"scores": lambda i: (scores(i), maximum(i)), "exps": exps, "weigh": weigh, "turn": turn,
           "values": values, "out": out, "x": to_x}
    for step, n in order:
        if step[0:4] == "low ":
            low(step[4:], n)
        elif step in run:
            run[step](n)
        else:
            project(step, n)
    k.phase_end = [(k.s_aggr, k.n_stats)]


def v3(ap, n):
    return ap.rearrange("p (t e) -> p t e", e=n)


def bc(ap, n):
    return ap.unsqueeze(len(ap.shape)).broadcast_to(list(ap.shape) + [n])


def chain(k):
    last = [None]

    def step(fn, *waits):
        last[0] = k.dve.do(fn, last[0], *waits)
        return last[0]
    return step


def rank(k, step, vals, n, C, out):
    C4 = C.rearrange("p (t e j) -> p t e j", e=n, j=n)
    for e in range(n):
        if e:
            k.dve.do(lambda q, e=e: q.tensor_tensor(C4[:, :, e, 0:e], vals[:, :, 0:e],
                                                   vals[:, :, e:e + 1].broadcast_to([P, NT, e]), ALU.is_ge))
        step(lambda q, e=e: q.tensor_tensor(C4[:, :, e, e:n], vals[:, :, e:n],
                                            vals[:, :, e:e + 1].broadcast_to([P, NT, n - e]), ALU.is_gt))
    return step(lambda q: q.tensor_reduce(out, C4, AX, ALU.add))


def scores_tok(k, wg, n, t_w):
    for i in range(NT):
        m = mm(k, k.bank[4][:, n * i:n * i + n], k.HT[:, 128 * i:128 * i + 128], wg, t_w, *k.phase_end,
               inc=True if i == NT - 1 else None)
    return m


def gate_groups(k, l, w, t_w, r):
    nc_ = 17 if l == 0 else 16
    comb = v3(r.get(NT * nc_), nc_)
    n0 = r.at
    s, m, g, gr, rk, wt, den, C = (r.get(x) for x in (512, 512, 128, 128, 512, 512, 32, 8192))
    x = scores_tok(k, w["gk"] if l == 0 else w["wg"], 16, t_w)
    step = chain(k)
    a = act(k, s, k.bank[4][:, 0:512], ACT.Exp, x, scale=-1.0)
    s3, m3, g3, gr3, w3_, rk3 = v3(s, 16), v3(m, 16), v3(g, 4), v3(gr, 4), v3(wt, 16), v3(rk, 16)
    step(lambda q: q.tensor_scalar(s, s, 1.0, None, ALU.add), a)
    step(lambda q: q.reciprocal(s, s))
    q4 = s.rearrange("p (x f) -> p x f", f=4)
    if l == 0:
        gb = w["gb"].unsqueeze(1).broadcast_to([P, NT, 16])
        step(lambda q: q.tensor_tensor(s3, s3, gb, ALU.add))
        t0, t1, t2 = rk[:, 0:128], rk[:, 128:256], rk[:, 256:384]
        T = lambda o, a_, b_, op: step(lambda q: q.tensor_tensor(o, a_, b_, op))
        T(t0, q4[:, :, 0], q4[:, :, 1], ALU.max)
        T(t1, q4[:, :, 2], q4[:, :, 3], ALU.max)
        T(g, t0, t1, ALU.max)
        T(t0, t0, t1, ALU.min)
        T(t1, q4[:, :, 0], q4[:, :, 1], ALU.min)
        T(t2, q4[:, :, 2], q4[:, :, 3], ALU.min)
        T(t1, t1, t2, ALU.max)
        T(t0, t0, t1, ALU.max)
        T(g, g, t0, ALU.add)
    else:
        step(lambda q: q.tensor_reduce(g, q4, AX, ALU.max))
    rank(k, step, g3, 4, C[:, 0:512], gr3)
    step(lambda q: q.tensor_scalar(gr, gr, 2.0, None, ALU.is_lt))
    m4 = m.rearrange("p (x f) -> p x f", f=4)
    step(lambda q: q.tensor_tensor(m4, q4, bc(gr, 4), ALU.mult))
    if l == 2:
        step(lambda q: q.tensor_scalar(gr, gr, -1.0, None, ALU.add))
        step(lambda q: q.tensor_tensor(m4, m4, bc(gr, 4), ALU.add))
    rank(k, step, m3, 16, C, rk3)
    step(lambda q: q.tensor_scalar(rk, rk, 4.0, None, ALU.is_lt))
    step(lambda q: q.tensor_tensor(wt, m, rk, ALU.mult))
    step(lambda q: q.tensor_reduce(den, w3_, AX, ALU.add))
    if l == 0:
        step(lambda q: q.tensor_scalar(den, den, 1e-20, None, ALU.add))
    step(lambda q: q.reciprocal(den, den))
    step(lambda q: q.tensor_scalar(den, den, 2.5, None, ALU.mult))
    t = step(lambda q: q.tensor_tensor(comb[:, :, 0:16], w3_, bc(den, 16), ALU.mult))
    if l == 0:
        t = step(lambda q: q.memset(comb[:, :, 16:17], 1.0))
    r.at = n0
    return comb, t


def gate_top(k, w, t_w, r):
    comb = v3(r.get(NT * 8), 8)
    n0 = r.at
    S, Y, A, B, Gm = (r.get(256) for _ in range(5))
    sg, kk, t, cd, ct, pr, thr, mx, need = (r.get(8) for _ in range(9))
    c8 = r.get(8)
    e_t = lambda ap: ap.rearrange("p (t e) -> p e t", e=8)
    over = lambda ap: ap.unsqueeze(1).broadcast_to([P, NT, 8])
    x = scores_tok(k, w["wg"], 8, t_w)
    step = chain(k)
    step(lambda q: q.tensor_copy(S, k.bank[4][:, 0:256]), x)
    banks = [k.bank[5], k.bank[6]]
    n = [0]

    def total(src, ones="ones"):
        bk = banks[n[0] % 2]
        n[0] += 1
        m = mm(k, bk[:, 0:8], k.C[ones], src, (k.dve.sem, k.dve.n), inc=True)
        return bk[:, 0:8], m

    def count(src3, against, op):
        step(lambda q: q.tensor_tensor(v3(A, 8), src3, over(against), op))
        step(lambda q: q.tensor_reduce(c8, e_t(A), AX, ALU.add))
        return total(c8)

    step(lambda q: q.memset(t, 0.0))
    c, m = count(v3(S, 8), t, ALU.is_ge)
    step(lambda q: q.tensor_scalar(pr, c, 511.5, None, ALU.is_ge), m)
    step(lambda q: q.tensor_scalar(sg, pr, 2.0, -1.0, ALU.mult, ALU.add))
    step(lambda q: q.tensor_scalar(kk, pr, 512.0 - 3585.0, 3585.0, ALU.mult, ALU.add))
    step(lambda q: q.tensor_tensor(v3(Y, 8), v3(S, 8), over(sg), ALU.mult))
    ti, ci, pi = t.bitcast(I32), cd.bitcast(I32), pr.bitcast(I32)
    for bit in range(30, -1, -1):
        step(lambda q, bit=bit: q.tensor_scalar(ci, ti, 1 << bit, None, ALU.bitwise_or))
        c, m = count(v3(Y, 8), cd, ALU.is_ge)
        step(lambda q, c=c: q.tensor_tensor(pi, c, kk, ALU.is_ge), m)
        step(lambda q: q.copy_predicated(t, pi, cd))
    step(lambda q: q.tensor_tensor(thr, t, sg, ALU.mult))
    c, m = count(v3(S, 8), thr, ALU.is_gt)
    step(lambda q: q.tensor_scalar(need, c, -1.0, 512.0, ALU.mult, ALU.add), m)
    step(lambda q: q.tensor_tensor(v3(A, 8), v3(S, 8), over(thr), ALU.is_equal))
    m1 = mm(k, banks[0][:, 0:256], k.C["tri"], A, (k.dve.sem, k.dve.n), inc=True)
    m2 = mm(k, banks[1][:, 0:256], k.C["ones"], A, inc=True)
    step(lambda q: q.tensor_copy(B, banks[0][:, 0:256]), m1)
    step(lambda q: q.tensor_copy(Gm, banks[1][:, 0:256]), m2)
    z = 1
    src, dst = Gm, r.get(256)
    while z < NT:
        step(lambda q, s=src, d=dst, z=z: q.tensor_copy(d[:, 0:8 * z], s[:, 0:8 * z]))
        step(lambda q, s=src, d=dst, z=z: q.tensor_tensor(d[:, 8 * z:256], s[:, 8 * z:256], s[:, 0:256 - 8 * z], ALU.add))
        src, dst = dst, src
        z *= 2
    step(lambda q: q.tensor_tensor(B[:, 8:256], B[:, 8:256], src[:, 0:248], ALU.add))
    step(lambda q: q.tensor_tensor(v3(B, 8), v3(B, 8), over(need), ALU.is_lt))
    step(lambda q: q.tensor_tensor(B, B, A, ALU.mult))
    step(lambda q: q.tensor_tensor(v3(A, 8), v3(S, 8), over(thr), ALU.is_gt))
    sel = step(lambda q: q.tensor_tensor(B, B, A, ALU.add))
    a = step(lambda q: q.tensor_reduce(mx, e_t(S), AX, ALU.max))
    m = tr(k, banks[0][0:8, 0:128], mx, a, inc=True)
    step(lambda q: q.tensor_reduce(thr[0:8, 0:1], banks[0][0:8, 0:128], AX, ALU.max), m)
    step(lambda q: q.tensor_scalar(Y[0:8, 0:8], k.C["ident"][0:8, 0:8], thr[0:8, 0:1], None, ALU.mult))
    m = mm(k, banks[1][:, 0:8], k.C["ones"][0:8, :], Y[0:8, 0:8], (k.dve.sem, k.dve.n), inc=True)
    step(lambda q: q.tensor_copy(mx, banks[1][:, 0:8]), m)
    d = step(lambda q: q.tensor_tensor(v3(A, 8), v3(S, 8), over(mx), ALU.subtract))
    a = act(k, A, A, ACT.Exp, d)
    step(lambda q: q.tensor_tensor(A, A, B, ALU.mult), a)
    step(lambda q: q.tensor_reduce(c8, e_t(A), AX, ALU.add))
    c, m = total(c8)
    step(lambda q: q.reciprocal(need, c), m)
    t_ = step(lambda q: q.tensor_tensor(comb, v3(A, 8), over(need), ALU.mult))
    r.at = n0
    return comb, t_


def moe(k, l, t_w, t_gb, r):
    w = views(k.W1 if l == 3 else k.W2, {0: L0F, 2: L2F, 3: L3F}[l])
    if l == 3:
        comb, t_c = gate_top(k, w, t_w, r)
    else:
        comb, t_c = gate_groups(k, l, w, t_w, r)
    s_silu, s_hidden, s_down, s_sum, s_tox, s_ct, s_ctp = sems(k, f"f{l}", "silu", "hidden", "down", "sum", "tox",
                                                               "ct", "ctp")
    sg = [r.get(512) for _ in range(3)]
    h = [r.get(512) for _ in range(3)]
    acc = [r.get(512) for _ in range(2)]
    ym = [r.get(512) for _ in range(2)]
    if l == 0:
        yb, E = [(k.bank[4], k.bank[5]), (k.bank[6], k.bank[7])], 9
    else:
        yb, E = [(k.bank[4],), (k.bank[5],), (k.bank[6],)], 16
    enter(k, t_gb, t_c, t_w)
    if l == 2:
        cT = r.get(4096)
        for g in range(8):
            bk = k.bank[4 + g % 2]
            for j in range(4):
                tr(k, bk[0:16, 128 * j:128 * j + 128], comb[:, 4 * g + j, :], (s_ct, g - 1),
                   inc=s_ctp if j == 3 else None)
            cp(k, k.dve, cT[0:16, 512 * g:512 * g + 512], bk[0:16, :], (s_ctp, g + 1), inc=s_ct)

    last = [None] * 4

    def up(u):
        B, e = divmod(u, E)
        g_, u_ = k.bank[2 * (u % 2)], k.bank[2 * (u % 2) + 1]
        x = k.HT[:, 512 * B:512 * B + 512]
        if l == 0 and e == 8:
            w1, w3 = w["sw1"], w["sw3"]
        else:
            w1, w3 = w["w1"][:, 128 * e:128 * e + 128], w["w3"][:, 128 * e:128 * e + 128]
        m1 = mm(k, g_[:, :], w1, x, (s_silu, u - 1), inc=True)
        m2 = mm(k, u_[:, :], w3, x, (s_hidden, u - 1), inc=True)
        a, hh = sg[u % 3], h[u % 3]
        act(k, a, g_[:, :], ACT.Silu, m1, (s_hidden, u - 2), bias=(w["b1"][:, e:e + 1] if l == 2 else 0.0),
            inc=s_silu)
        if l == 2:
            stt(k, hh, u_[:, :], w["b3"][:, e:e + 1], a, ALU.add, ALU.mult, (s_silu, u + 1), m2, (s_down, u - 2),
                inc=s_hidden)
        else:
            tt(k, k.dve, hh, u_[:, :], a, ALU.mult, (s_silu, u + 1), m2, (s_down, u - 2), inc=s_hidden)

    def down(u):
        B, e = divmod(u, E)
        hh, A = h[u % 3], acc[B % 2]
        v = u + (B + 1 if l == 2 else 0)
        if l == 2 and e == 0:
            y = yb[(v - 1) % 3][0]
            for j in range(4):
                i = 4 * B + j
                m = mm(k, y[:, 128 * j:128 * j + 128], cT[0:16, 128 * i:128 * i + 128], w["b2"][0:16, :],
                       (s_sum, v - 3), (s_ct, 8), inc=True if j == 3 else None)
            cp(k, k.dve, A, y[:, :], m, (s_tox, B - 1), inc=s_sum)
            last[:] = [(s_sum, v)] * 4
        ys = yb[v % len(yb)]
        two = l == 0 and e < 8
        for j in range(4):
            if two:
                o, rhs = ys[j // 2][:, 256 * (j % 2):256 * (j % 2) + 256], w["w2"][:, 256 * e:256 * e + 256]
            else:
                o, rhs = ys[0][:, 128 * j:128 * j + 128], (w["sw2"] if l == 0 else w["w2"][:, 128 * e:128 * e + 128])
            m = mm(k, o, hh[:, 128 * j:128 * j + 128], rhs, (s_sum, v - len(yb) + 1), (s_hidden, u + 1),
                   inc=s_down if j == 3 else (True if two and j == 1 else None))
            if two and j == 1:
                m_lo = m
        m = (s_down, u + 1)
        for q in range(2 if two else 1):
            for j in range(4):
                i = 4 * B + j
                if l == 0:
                    c = comb[:, i, 2 * e + q:2 * e + q + 1] if e < 8 else comb[:, i, 16:17]
                else:
                    c = comb[:, i, e:e + 1] if l == 2 else comb[:, i, e // 2:e // 2 + 1]
                a = A[:, 128 * j:128 * j + 128]
                if two:
                    src, mw = ys[j // 2][:, 256 * (j % 2) + 128 * q:256 * (j % 2) + 128 * q + 128], m_lo if j < 2 else m
                else:
                    src, mw = ys[0][:, 128 * j:128 * j + 128], m
                end = j == 3 and q == (1 if two else 0)
                if e == 0 and q == 0 and l != 2:
                    t = ts(k, k.dve, a, src, c, None, ALU.mult, None, mw, (s_tox, B - 1), inc=s_sum if end else True)
                else:
                    t = stt(k, a, src, c, a, ALU.mult, ALU.add, mw, last[j], inc=s_sum if end else True)
                last[j] = (s_sum, v + 1) if end else t
        if e == E - 1:
            y2 = ym[B % 2]
            for hb in range(2):
                b = 2 * B + hb
                g = k.gbbc[:, 128 * b:128 * b + 128].unsqueeze(1).broadcast_to([P, 2, 128])
                o = y2[:, 256 * hb:256 * hb + 256]
                p = tt(k, k.pool, o.rearrange("p (t d) -> p t d", t=2),
                       A[:, 256 * hb:256 * hb + 256].rearrange("p (t d) -> p t d", t=2), g, ALU.mult,
                       (s_sum, v + 1), (s_tox, B - 1))
                x = k.X[:, 256 * b:256 * b + 256]
                p = tt(k, k.pool, x, x, o, ALU.add, p, inc=s_tox if hb else True)
                p = (s_tox, B + 1) if hb else p
                stats(k, 2 * b, p)
                stats(k, 2 * b + 1, p)

    for u in range(8 * E + 1):
        if u < 8 * E:
            up(u)
        if u >= 1:
            down(u - 1)
    k.phase_end = [(k.s_aggr, k.n_stats)]


def back_to_x(k, yT, ready, B, bank, bank_free, s_turned, s_sum):
    for j in range(4):
        tr(k, bank[:, 128 * j:128 * j + 128], yT[:, 128 * j:128 * j + 128], ready, bank_free,
           inc=s_turned if j == 3 else None)
    x = k.X[:, 512 * B:512 * B + 512]
    tt(k, k.dve, x, x, bank[:, :], ALU.add, (s_turned, B + 1), inc=s_sum)


def soft_moe(k, *t_w):
    w = views(k.W1, L1F)
    r = Region(k.T, TW)
    rg = Region(k.gbbc, 2048)
    mxn = rg.get(1024)
    yt = r.get(2048)
    small = [rg.get(64) for _ in range(6)]
    n1 = r.at
    htok = k.W2[:, 0:4096]
    L = [r.get(2048) for _ in range(2)]
    E = [r.get(2048) for _ in range(2)] + [yt, k.W2[:, 4096:6144]]
    (s_turned, s_htok_a, s_htok_d, s_logits, s_taken, s_max, s_slot, s_shift, s_exps, s_inv, s_soft,
     s_gather) = sems(k, "s1", "turned", "htok_a", "htok_d", "logits", "taken", "max", "slot", "shift", "exps",
                      "inv", "soft", "gather")
    enter(k, *t_w)
    bank = k.bank
    for g in range(8):
        p = bank[g % 4]
        for j in range(4):
            i = 4 * g + j
            tr(k, p[:, 128 * j:128 * j + 128], k.HT[:, 128 * i:128 * i + 128],
               ((s_htok_d, s_htok_a)[g % 2], g // 2 - 1), inc=s_turned if j == 3 else None)
        cp(k, (k.dve, k.act)[g % 2], htok[:, 512 * g:512 * g + 512], p[:, :], (s_turned, g + 1),
           inc=(s_htok_d, s_htok_a)[g % 2])

    bias, eighths = k.QK[0:16, 0:2048], k.QK[0:16, 2048:2176]
    act(k, bias, w["phib"][0:16, :], ACT.Copy, scale=k.C["split"][0:16, 0:1])
    t = act(k, eighths, k.C["ones"][0:16, :], ACT.Copy, scale=0.125)
    t_bias = k.dve.do(lambda e: e.scalar_tensor_tensor(
        out=bias, in0=w["phib"][0:16, :], scalar=k.C["split"][0:16, 1:2], in1=bias.bitcast(F32), op0=ALU.mult,
        op1=ALU.subtract), t)

    def logits(i):
        l, e, mx = L[i % 2], E[i % 4], small[i % 2]
        for j in range(4):
            n = 4 * i + j
            mm(k, bank[j][:, :], k.HT[:, 128 * i:128 * i + 128], w["phi"][:, 512 * j:512 * j + 512],
               (s_taken, n - 3), (s_htok_d, 4), (s_htok_a, 4), stop=False)
            mm(k, bank[j][:, :], eighths, bias[:, 512 * j:512 * j + 512], t_bias, start=False, inc=s_logits)
            cp(k, k.act, l[:, 512 * j:512 * j + 512], bank[j][:, :], (s_logits, n + 1), (s_slot, i - 1),
               (s_shift, i - 1), inc=s_taken)
        l3, e3 = l.rearrange("p (n q) -> p n q", q=32), e.rearrange("p (n q) -> p n q", q=32)
        red(k, mx, l3, ALU.max, (s_taken, 4 * i + 4), (s_shift, i - 1), inc=s_max)
        tt(k, k.pool, e3, l3, bc(mx, 32), ALU.subtract, (s_max, i + 1), (s_gather, i - 3), inc=s_shift)

    def exps(i):
        act(k, E[i % 4], E[i % 4], ACT.Exp, (s_shift, i + 1), inc=s_exps)

    def slot_max(i):
        red(k, mxn[:, 32 * i:32 * i + 32], L[i % 2].rearrange("p (n q) -> p q n", q=32), ALU.max,
            (s_taken, 4 * i + 4), inc=s_slot)

    def softmax(i):
        e, s, rv = E[i % 4], small[2 + i % 2], small[4 + i % 2]
        e3 = e.rearrange("p (n q) -> p n q", q=32)
        t = red(k, s, e3, ALU.add, (s_exps, i + 1), (s_inv, i - 1))
        k.dve.do(lambda q: q.reciprocal(rv, s), t, (s_soft, i - 1), inc=s_inv)
        tt(k, k.pool, e3, e3, bc(rv, 32), ALU.mult, (s_inv, i + 1), inc=s_soft)

    def dispatch(i):
        e = E[i % 4]
        for j in range(4):
            mm(k, bank[4 + j][:, :], htok[:, 128 * i:128 * i + 128], e[:, 512 * j:512 * j + 512], (s_soft, i + 1),
               start=(i == 0), stop=(i == NT - 1), inc=s_gather if j == 3 else None)

    for i in range(NT + 3):
        if i < NT:
            logits(i)
        if 1 <= i <= NT:
            exps(i - 1)
            softmax(i - 1)
        if i < NT:
            slot_max(i)
        if i >= 3:
            dispatch(i - 3)
    m_x = (s_gather, NT)
    k.phase_end = [m_x]
    enter(k)
    r.at = n1
    rw = Region(k.W2, width(L2F))
    eb, xt, xs2 = (rw.get(2048) for _ in range(3))
    xs, xt2 = (r.get(2048) for _ in range(2))
    mv, sd, st = r.get(32), r.get(16), [r.get(6) for _ in range(16)]
    t_eb = load(k, "eb", eb, *k.phase_end)
    for j in range(4):
        t = ts(k, k.dve, xt[:, 512 * j:512 * j + 512], bank[4 + j][:, :], -33000.0, 65000.0, ALU.max, ALU.min, m_x)
    for s in range(16):
        m = tr(k, bank[s // 4][:, 128 * (s % 4):128 * (s % 4) + 128], xt[:, 128 * s:128 * s + 128], t, inc=(s % 4 == 3))
        if s % 4 == 3:
            a = cp(k, k.dve, xs[:, 512 * (s // 4):512 * (s // 4) + 512], bank[s // 4][:, :], m)
    for s in range(16):
        a2 = k.dve.do(lambda q, s=s: q.bn_stats(st[s], xs[:, 128 * s:128 * s + 128]), a)
    for s in range(16):
        a3 = k.dve.do(lambda q, s=s: q.bn_aggr(mv[:, 2 * s:2 * s + 2], st[s]), a2)
    mv2 = mv.rearrange("p (t c) -> p t c", c=2)
    t = ts(k, k.dve, sd, mv2[:, :, 1], 1e-5, None, ALU.add, None, a3)
    t = act(k, sd, sd, ACT.Sqrt, t)
    t = k.dve.do(lambda q: q.reciprocal(sd, sd), t)
    for s in range(16):
        t2 = ts(k, k.dve, xs2[:, 128 * s:128 * s + 128], xs[:, 128 * s:128 * s + 128], mv[:, 2 * s:2 * s + 1],
                sd[:, s:s + 1], ALU.subtract, ALU.mult, t)
    t = act(k, xs, xs2, ACT.Tanh, t2)
    for s in range(16):
        m = tr(k, bank[s // 4][:, 128 * (s % 4):128 * (s % 4) + 128], xs[:, 128 * s:128 * s + 128], t, a,
               inc=(s % 4 == 3))
        if s % 4 == 3:
            c = cp(k, k.dve, xt2[:, 512 * (s // 4):512 * (s // 4) + 512], bank[s // 4][:, :], m)
    for s in range(16):
        o = bank[4 + s // 4]
        for j in range(4):
            n = 4 * s + j
            m = mm(k, o[32 * j:32 * j + 32, 128 * (s % 4):128 * (s % 4) + 128], xt2[:, 32 * n:32 * n + 32],
                   w["ew"][:, 128 * n:128 * n + 128], c, inc=(s % 4 == 3 and j == 3))
        if s % 4 == 3:
            q = s // 4
            t_y = tt(k, k.dve, yt[:, 512 * q:512 * q + 512], o[:, :], eb[:, 512 * q:512 * q + 512], ALU.add, m, t_eb)
    k.phase_end = [t_y]
    enter(k)
    r.at = n1
    (s_turned, s_mT, s_sel, s_mb, s_logits, s_shift, s_exps, s_total, s_inv, s_soft, s_comb, s_gate, s_yt,
     s_x) = sems(k, "s3", "turned", "mT", "sel", "mb", "logits", "shift", "exps", "total", "inv", "soft", "comb",
                 "gate", "yt", "x")
    ET = [r.get(8192), w["ew"]]
    rw.at = 0
    dl = [rw.get(512) for _ in range(2)]
    mT = rw.get(512)
    mb, rc, yo = ([rw.get(512) for _ in range(2)] for _ in range(3))
    turn = bank[7]

    def begin(B):
        for j in range(4):
            i = 4 * B + j
            tr(k, turn[0:32, 128 * j:128 * j + 128], mxn[:, 32 * i:32 * i + 32], (s_mb, B), (s_x, B - 1),
               inc=s_turned if j == 3 else None)
        cp(k, k.dve, mT[0:32, :], turn[0:32, :], (s_turned, B + 1), (s_sel, B), inc=s_mT)
        mm(k, turn[:, :], k.C["sel32"][0:32, :], mT[0:32, :], (s_mT, B + 1), inc=s_sel)
        cp(k, k.act, mb[B % 2], turn[:, :], (s_sel, B + 1), (s_shift, 16 * (B - 1)), inc=s_mb)

    def expo(B, s):
        n = 16 * B + s
        l, d = bank[n % 3], dl[n % 2]
        mm(k, l[:, :], w["phi"][:, 128 * s:128 * s + 128], k.HT[:, 512 * B:512 * B + 512], (s_shift, n - 2),
           inc=s_logits)
        tt(k, k.dve, d, l[:, :], mb[B % 2], ALU.subtract, (s_logits, n + 1), (s_mb, B + 1), (s_exps, n - 1),
           inc=s_shift)
        act(k, ET[B % 2][:, 512 * s:512 * s + 512], d, ACT.Exp, (s_shift, n + 1), (s_comb, B - 1),
            bias=w["phic"][:, s:s + 1], inc=s_exps)

    def total(B, s):
        mm(k, bank[3 + B % 2][:, :], k.C["same32"], ET[B % 2][:, 512 * s:512 * s + 512], (s_exps, 16 * B + s + 1),
           (s_inv, B - 1), start=(s == 0), stop=(s == 15), inc=s_total if s == 15 else None)
        if s == 15:
            k.dve.do(lambda e: e.reciprocal(rc[B % 2], bank[3 + B % 2][:, :]), (s_total, B + 1),
                     (s_soft, 16 * (B - 1)), inc=s_inv)

    def scale(B, s):
        e = ET[B % 2][:, 512 * s:512 * s + 512]
        tt(k, k.dve, e, e, rc[B % 2], ALU.mult, (s_inv, B + 1), inc=s_soft)

    def combine(B, s):
        e = ET[B % 2][:, 512 * s:512 * s + 512]
        y = bank[5 + B % 2]
        mm(k, y[:, :], yt[:, 128 * s:128 * s + 128], e, (s_soft, 16 * B + s + 1), (s_gate, B - 1), start=(s == 0),
           stop=(s == 15), inc=s_comb if s == 15 else None)
        if s == 15:
            for h in range(2):
                g = 96 + 80 + 2 * B + h
                ts(k, k.dve, yo[B % 2][:, 256 * h:256 * h + 256], y[:, 256 * h:256 * h + 256],
                   k.modT[:, g:g + 1], None, ALU.mult, None, (s_comb, B + 1), (s_yt, B - 1),
                   inc=s_gate if h else True)
            k.pe.wait((s_x, B))
            back_to_x(k, yo[B % 2], (s_gate, B + 1), B, turn, (s_mb, min(B + 2, 8)), s_yt, s_x)
            for j in range(4):
                stats(k, 4 * B + j, (s_x, B + 1))

    for B in range(9):
        if B < 8:
            begin(B)
        for s in range(18):
            if B < 8 and s < 16:
                expo(B, s)
            if B < 8 and s >= 2:
                total(B, s - 2)
            if B >= 1 and s < 16:
                scale(B - 1, s)
            if B >= 1 and 1 <= s < 17:
                combine(B - 1, s - 1)
    k.phase_end = [(k.s_aggr, k.n_stats)]


def rwkv(k, w, *t_w):
    r, r1 = Region(k.T, TW), Region(k.W1, width(L1F))
    s_zero, s_proj, s_ra, s_rd, s_mix, s_decay, s_lev, s_prod, s_merge, s_off, s_ym, s_yo, s_st = sems(
        k, "r1", "zero", "proj", "ra", "rd", "mix", "decay", "lev", "prod", "merge", "off", "ym", "yo", "st")
    LORA, LORA4, MIX, TDA, TDB, KP, RP, VP, GP = 0, 1, 2, 7, 8, 9, 10, 11, 12

    def filled(B, i):
        return (s_proj, 13 * B + i + 1)

    def taken(B, i):
        if i < MIX:
            return (s_ra, 7 * B + i + 1)
        if i < TDA:
            return (s_rd, 6 * B + i - MIX + 1)
        if i < GP:
            return (s_ra, 7 * B + i - TDA + 3)
        return (s_rd, 6 * B + 6)

    st = [r.get(6) for _ in range(8)]
    yall, gall = r1.get(4096), r1.get(4096)
    mvy, sd = r.get(128), r.get(64)
    U = lambda: r.get(512)
    U2 = lambda: [r.get(512) for _ in range(2)]
    rw = Region(k.W2, width(L2F))
    dxa, xm, lor, lor4, tmp = U2(), U(), U(), U(), U2()
    xin = [rw.get(512) for _ in range(5)]
    wA, dd, kk, rr, vv = r1.get(512), U2(), U2(), U2(), [rw.get(512) for _ in range(2)]
    Pq, Qq, Rr, Kr, TT = rw.get(512), rw.get(512), U2(), U2(), U2()
    AT = [r1.get(512), r1.get(512)]
    off = [[r1.get(256) for _ in range(2)] for _ in range(2)]
    gt = [r1.get(512) for _ in range(2)]
    enter(k, *t_w)
    for s in Rr + Kr:
        k.pool.do(lambda e, s=s: e.memset(s, 0.0), inc=s_zero)
    zero = (s_zero, 4)
    lev = [k.C["lev"][:, 128 * i:128 * i + 128] for i in range(8)]

    def proj(B, i, *parts):
        u = 13 * B + i
        bk = k.bank[4 + u % 3]
        for j, (rows, c0, c1, a, b) in enumerate(parts):
            mm(k, bk[0:rows, c0:c1], a, b, taken(*divmod(u - 3, 13)), inc=s_proj if j == len(parts) - 1 else None)
        return bk

    def front(B):
        x = k.HT[:, 512 * B:512 * B + 512]
        x3 = x.rearrange("p (b t) -> p b t", b=2)
        dx = dxa[B % 2]
        d3 = dx.rearrange("p (b t) -> p b t", b=2)
        tt(k, k.pool, d3[:, :, 1:256], x3[:, :, 0:255], x3[:, :, 1:256], ALU.subtract, taken(B - 2, MIX + 4))
        a = ts(k, k.pool, d3[:, :, 0:1], x3[:, :, 0:1], -1.0, None, ALU.mult, None)
        t = stt(k, xm, dx, w["miux"], x, ALU.mult, ALU.add, a, filled(B - 1, LORA4))
        k.pe.wait(t)
        yield
        p = proj(B, LORA, (128, 0, 512, w["A"][:, 0:128], xm))
        act(k, lor, p[:, :], ACT.Tanh, filled(B, LORA), filled(B - 1, MIX + 4), inc=s_ra)
        yield
        p = proj(B, LORA4, (32, 0, 512, w["A"][:, 128:160], xm))
        act(k, lor4[0:32, :], p[0:32, :], ACT.Tanh, filled(B, LORA4), inc=s_ra)
        for f in range(5):
            k.pe.wait(taken(B, LORA if f < 4 else LORA4))
            if f < 4:
                yield
                p = proj(B, MIX + f, (128, 0, 512, w["B"][:, 128 * f:128 * f + 128], lor))
            else:
                yield
                p = proj(B, MIX + f, (128, 0, 512, w["B"][0:32, 512:640], lor4[0:32, :]))
            n, tm = 5 * B + f, tmp[(5 * B + f) % 2]
            stt(k, tm, p[:, :], w["lam"][:, f:f + 1], dx, ALU.add, ALU.mult, filled(B, MIX + f), (s_mix, n - 1),
                inc=s_rd)
            tt(k, k.pool, xin[f], tm, x, ALU.add, taken(B, MIX + f), filled(B - 1, (TDA, KP, VP, RP, GP)[f]), inc=s_mix)
        xw, xk, xv, xr, xg = xin
        mixed = lambda f: (s_mix, 5 * B + f + 1)
        k.pe.wait(mixed(0))
        yield
        p = proj(B, TDA, (64, 0, 512, w["tdA"], xw))
        act(k, wA[0:64, :], p[0:64, :], ACT.Tanh, filled(B, TDA), filled(B - 1, TDB), inc=s_ra)
        k.pe.wait(taken(B, TDA))
        yield
        p = proj(B, TDB, (128, 0, 512, w["tdB"][0:64, :], wA[0:64, :]))
        d = dd[B % 2]
        act(k, d, p[:, :], ACT.Exp, filled(B, TDB), (s_lev, B - 1), bias=w["tdmiu"], inc=s_ra)
        act(k, d, d, ACT.Exp, taken(B, TDB), scale=-1.0, inc=s_decay)
        k.pe.wait(mixed(1))
        yield
        p = proj(B, KP, (128, 0, 512, w["WkT"], xk))
        cp(k, k.act, kk[B % 2], p[:, :], filled(B, KP), (s_lev, B - 1), inc=s_ra)
        k.pe.wait(mixed(3))
        yield
        p = proj(B, RP, (128, 0, 512, w["WrT"], xr))
        cp(k, k.act, rr[B % 2], p[:, :], filled(B, RP), (s_lev, B - 1), (s_prod, 18 * (B - 2) + 2), inc=s_ra)
        k.pe.wait(mixed(2))
        yield
        p = proj(B, VP, *[(128, 128 * j, 128 * j + 128, xv[:, 128 * j:128 * j + 128], w["WvT"]) for j in range(4)])
        cp(k, k.act, vv[B % 2], p[:, :], filled(B, VP), (s_ym, B - 1), inc=s_ra)
        k.pe.wait(mixed(4))
        yield
        p = proj(B, GP, *[(128, 128 * j, 128 * j + 128, xg[:, 128 * j:128 * j + 128], w["WgT"]) for j in range(4)])
        g1, g2 = gt
        t = act(k, g1, p[:, :], ACT.Exp, filled(B, GP), taken(B - 1, GP), scale=-1.0)
        t = ts(k, k.dve, g1, g1, 1.0, None, ALU.add, None, t)
        t = k.dve.do(lambda e: e.reciprocal(g2, g1), t)
        tt(k, k.dve, gall[:, 512 * B:512 * B + 512], p[:, :], g2, ALU.mult, t, inc=s_rd)

    def pairs(B):
        d, kq, rq, v = dd[B % 2], kk[B % 2], rr[B % 2], vv[B % 2]
        tP = k.pool.do(lambda e: e.memset(Pq, 1.0), (s_lev, B))
        tQ = k.pool.do(lambda e: e.memset(Qq, 1.0), (s_lev, B))
        T_, tT = d, (s_decay, B + 1)
        k_ready, r_ready = taken(B, KP), taken(B, RP)

        def multiplied(i, hd):
            return (s_prod, 18 * B + 2 * i + hd + 1)

        def merged(b, i, hd):
            return (s_merge, 16 * b + 2 * i + hd + 1)

        def merge(i):
            for hd in range(2):
                o3 = AT[hd].rearrange("p (t s) -> p t s", t=4)
                b3 = k.bank[hd + 2 * ((9 * B + i) % 2)].rearrange("p (t s) -> p t s", t=4)
                mk = lev[i].unsqueeze(1).broadcast_to([P, 4, 128])
                if i == 0:
                    tt(k, k.dve, o3, b3, mk, ALU.mult, multiplied(i, hd), (s_ym, B), inc=s_merge)
                else:
                    k.dve.do(lambda e, o3=o3, b3=b3, mk=mk: e.copy_predicated(o3, mk.bitcast(I32), b3),
                             multiplied(i, hd), merged(B, i - 1, hd), inc=s_merge)

        for i in range(9):
            n, h = 9 * B + i, 1 << max(0, i - 1)
            R, Kx = Rr[i % 2], Kr[i % 2]
            back = multiplied(i - 2, 1) if i > 1 else (s_prod, 18 * B)
            if i == 0:
                ra, rt = rq, r_ready
                kt = ts(k, k.dve, Kx, kq, w["u"], None, ALU.mult, None, k_ready, back, zero)
            else:
                hv = lambda ap: ap.rearrange("p (n two h) -> p n two h", two=2, h=h)
                Rh, Kh, Ph, Qh, rh, kh = (hv(ap) for ap in (R, Kx, Pq, Qq, rq, kq))
                t1 = tt(k, k.dve, Rh[:, :, 1, :], rh[:, :, 1, :], Ph[:, :, 1, :], ALU.mult, tP, r_ready, back, zero)
                t2 = tt(k, k.dve, Kh[:, :, 0, :], kh[:, :, 0, :], Qh[:, :, 0, :], ALU.mult, tQ, k_ready, back, zero,
                        inc=s_lev if i == 8 else True)
                ra, rt, kt = R, t1, (s_lev, B + 1) if i == 8 else t2
                if i < 8:
                    T3 = T_[:, 0:512 // h].rearrange("p (n two) -> p n two", two=2)
                    nb = 256 // h
                    tP = tt(k, k.dve, Ph[:, :, 1, :], Ph[:, :, 1, :], T3[:, :, 0:1].broadcast_to([P, nb, h]),
                            ALU.mult, t1, tT)
                    tQ = tt(k, k.dve, Qh[:, :, 0, :], Qh[:, :, 0, :], T3[:, :, 1:2].broadcast_to([P, nb, h]),
                            ALU.mult, t2, tT)
                    T_ = TT[i % 2]
                    tT = tt(k, k.dve, T_[:, 0:nb], T3[:, :, 0], T3[:, :, 1], ALU.mult, tT)
            for hd in range(2):
                q = slice(64 * hd, 64 * hd + 64)
                bk = k.bank[hd + 2 * (n % 2)]
                free = (s_off, B) if i == 1 else merged(B - 1, 7, hd) if i == 0 else merged(B, i - 2, hd)
                cols = [(128 * j, 128 * j, 128 * j) for j in range(4)] if i < 8 else [(0, 0, 128), (128, 256, 384)]
                for j, (o, a, b) in enumerate(cols):
                    mm(k, bk[:, o:o + 128], Kx[q, a:a + 128], ra[q, b:b + 128], rt, kt, free,
                       inc=s_prod if j == len(cols) - 1 else None)
            if i >= 1:
                merge(i - 1)
            yield
        for hd in range(2):
            cp(k, k.act, off[hd][B % 2], k.bank[hd + 2 * (n % 2)][:, 0:256], multiplied(8, hd), (s_ym, B - 1),
               inc=s_off if hd else True)
        y = k.bank[7]
        for hd in range(2):
            for j in range(4):
                o = y[:, 128 * j + 64 * hd:128 * j + 64 * hd + 64]
                vs = lambda q: v[:, 128 * q + 64 * hd:128 * q + 64 * hd + 64]
                mm(k, o, AT[hd][:, 128 * j:128 * j + 128], vs(j), merged(B, 7, 1), taken(B, VP), (s_yo, B),
                   stop=(j % 2 == 0))
                if j % 2:
                    b = j // 2
                    mm(k, o, off[hd][B % 2][:, 128 * b:128 * b + 128], vs(j - 1), (s_off, B + 1), start=False,
                       inc=s_ym if j == 3 and hd == 1 else None)
        cp(k, k.act, yall[:, 512 * B:512 * B + 512], y[:, :], (s_ym, B + 1), inc=s_yo)
        for q in range(8):
            c, n = 512 * B + 64 * q, 8 * B + q
            a = k.dve.do(lambda e, q=q, c=c: e.bn_stats(st[q], yall[:, c:c + 64]), (s_yo, B + 1), (s_st, n - 7))
            k.dve.do(lambda e, q=q, n=n: e.bn_aggr(mvy[:, 2 * n:2 * n + 2], st[q]), a, inc=s_st)

    for B in range(9):
        f = front(B) if B < 8 else iter(())
        p = pairs(B - 1) if B >= 1 else iter(())
        for j in range(14):
            next(f, None)
            if j % 3 != 2:
                next(p, None)
        for _ in f:
            pass
        for _ in p:
            pass
    mv2 = mvy.rearrange("p (t c) -> p t c", c=2)
    t = ts(k, k.dve, sd, mv2[:, :, 1], 2e-5, None, ALU.add, None, (s_st, 64))
    t = act(k, sd, sd, ACT.Sqrt, t)
    t_sd = k.dve.do(lambda e: e.reciprocal(sd, sd), t)
    k.phase_end = [t_sd]
    enter(k)
    ynT, oo = xin[0:2], xin[2:4]
    s_turned, s_yn, s_out, s_gated, s_yt, s_x = sems(k, "r2", "turned", "yn", "out", "gated", "yt", "x")
    for B in range(8):
        y = yall[:, 512 * B:512 * B + 512]
        for q in range(8):
            c, n = y[:, 64 * q:64 * q + 64], 8 * B + q
            t = ts(k, k.dve, c, c, mvy[:, 2 * n:2 * n + 1], sd[:, n:n + 1], ALU.subtract, ALU.mult, t_sd)
        y4 = y.rearrange("p (t c) -> p t c", t=4)
        t = tt(k, k.dve, y4, y4, w["gam"].unsqueeze(1).broadcast_to([P, 4, 128]), ALU.mult, t)
        t = tt(k, k.dve, y4, y4, w["bet"].unsqueeze(1).broadcast_to([P, 4, 128]), ALU.add, t)
        t = tt(k, k.dve, y, y, gall[:, 512 * B:512 * B + 512], ALU.mult, t)
        p, q_, yn, o = k.bank[B % 2], k.bank[2 + B % 2], ynT[B % 2], oo[B % 2]
        for j in range(4):
            tr(k, p[:, 128 * j:128 * j + 128], y[:, 128 * j:128 * j + 128], t, (s_yn, B - 1),
               inc=s_turned if j == 3 else None)
        cp(k, k.act, yn, p[:, :], (s_turned, B + 1), (s_out, B - 1), inc=s_yn)
        mm(k, q_[:, :], w["WoT"], yn, (s_yn, B + 1), (s_gated, B - 1), inc=s_out)
        for h in range(2):
            g = 192 + 32 + 2 * B + h
            act(k, o[:, 256 * h:256 * h + 256], q_[:, 256 * h:256 * h + 256], ACT.Copy, (s_out, B + 1), (s_yt, B - 1),
                scale=k.modT[:, g:g + 1], inc=s_gated if h else False)
        back_to_x(k, o, (s_gated, B + 1), B, k.bank[7], (s_x, B), s_yt, s_x)
        for j in range(4):
            stats(k, 4 * B + j, (s_x, B + 1))
    k.phase_end = [(k.s_aggr, k.n_stats)]


def program(nc, dram, out, phases):
    ctx = ExitStack()
    with ctx:
        k = setup(nc, ctx, dram, out)
        t_const = load(k, "const", k.C_tile)
        t_mods = load(k, "mods", k.T)
        k.sp.q.append(("do", lambda e: e.dma_start(k.X[:, :], dram["x"][:, :]).then_inc(k.dsem["x"], 16), None))
        t_x = (k.dsem["x"], 16)
        t_l0a = load(k, "l0a", k.W1)
        t_l0f = load(k, "l0f", k.W2)
        sm = views(k.W3, SM)
        for e in (k.pe, k.dve, k.act, k.pool):
            e.wait(t_const)
        modulation(k, t_const, t_mods)
        for i in range(NT):
            stats(k, i, t_x)
        first, last = phases
        t_w1, t_w2 = t_l0a, t_l0f

        def region():
            return Region(k.T, TW)

        if first <= 0 <= last:
            layernorm(k, 0, 0, region())
            attention(k, 0, "l0", views(k.W1, L0A), t_l0a)
        t_sm = load(k, "sm", k.W3, *k.phase_end)
        t_l1f = load(k, "l1f", k.W1, t_l0a)
        if first <= 1 <= last:
            r = region()
            gb = gate_rows(k, 0, r)
            layernorm(k, 0, 1, r)
            moe(k, 0, t_l0f, gb, r)
        if first <= 2 <= last:
            layernorm(k, 1, 0, region())
            w = dict(sm, wo=sm["wproj"], bo=sm["bproj"])
            attention(k, 1, "l1", w, t_sm)
        if first <= 3 <= last:
            layernorm(k, 1, 1, region())
            soft_moe(k, t_l1f, t_l0f)
        if first <= 4 <= last:
            layernorm(k, 2, 0, region())
            rwkv(k, sm, t_sm, t_l1f, t_l0f)
        t_l2f = load(k, "l2f", k.W2, t_l0f, *k.phase_end)
        t_l3f = load(k, "l3f", k.W1, t_l1f, *k.phase_end)
        if first <= 5 <= last:
            r = region()
            gb = gate_rows(k, 2, r)
            layernorm(k, 2, 1, r)
            moe(k, 2, t_l2f, gb, r)
        if first <= 6 <= last:
            layernorm(k, 3, 0, region())
            w = dict(sm, wo=sm["o3"], bo=sm["bo3"])
            attention(k, 3, "l3", w, t_sm)
        if first <= 7 <= last:
            r = region()
            gb = gate_rows(k, 3, r)
            layernorm(k, 3, 1, r)
            moe(k, 3, t_l3f, gb, r)
        for t in k.phase_end:
            k.sp.wait(t)
        k.sp.q.append(("do", lambda e: e.dma_start(
            out.rearrange("b (t p) d -> p (b t) d", p=128),
            k.X[:, :].rearrange("p (i d) -> p i d", d=128)).then_inc(k.dsem["out"], 16), None))
        for t in (t_l1f, t_l2f, t_l3f, (k.dsem["out"], 16)):
            k.sp.wait(t)

        block = ctx.enter_context(nc.Block())

        @block.sync
        def _(e):
            k.sp.flush(e)

        @block.tensor
        def _(e):
            k.pe.flush(e)

        @block.vector
        def _(e):
            k.dve.flush(e)

        @block.scalar
        def _(e):
            k.act.flush(e)

        @block.gpsimd
        def _(e):
            k.pool.flush(e)




def _constants():
    p = np.arange(128)
    q, kk = p[:, None], np.arange(128)[None, :]
    neg = np.float32(NEG)
    caus = np.where(kk <= q, 0, neg)
    old = np.where(kk > q, 0, neg)
    lev = [(p[:, None] == p[None, :])]
    h = 1
    while h < 128:
        s, t = p[:, None], p[None, :]
        lev.append((s // (2 * h) == t // (2 * h)) & ((s // h) % 2 == 0) & ((t // h) % 2 == 1))
        h *= 2
    sel = np.zeros((128, 128))
    sel[:32] = (p[None, :] % 32) == np.arange(32)[:, None]
    low = np.stack([(p // 8) % 2 == 1, (p // 16) % 2 == 1], 1)
    split = np.stack([2 * low[:, 0] - 1, low[:, 0], 2 * low[:, 1] - 1, low[:, 1]], 1)
    return {
        "ident": np.eye(128), "mwin": np.concatenate([old, caus], 1),
        "mcaus": np.concatenate([np.zeros((128, 128)), caus], 1), "ones": np.ones((128, 128)),
        "tri": (p[:, None] < p[None, :]), "same32": (p[:, None] % 32) == (p[None, :] % 32),
        "sel32": sel, "lev": np.concatenate(lev, 1), "split": split,
    }


def _pack(spec, parts):
    out = np.zeros((128, width(spec)), np.float32)
    at = 0
    for n, w in spec:
        a = np.asarray(parts[n])
        if a.ndim == 1:
            a = a[:, None] if w == 1 else a[None, :]
        assert a.shape[1] == w and a.shape[0] <= 128, (n, a.shape, w)
        out[:a.shape[0], at:at + w] = a
        at += w
    return out


def _rows(a):
    return np.broadcast_to(np.asarray(a).reshape(1, -1), (128, np.asarray(a).size))


def _put(rows, at, a):
    out = np.zeros((rows, a.shape[1]), a.dtype)
    out[at:at + a.shape[0]] = a
    return out


def _spread(a):
    x = a.reshape(-1, 2, 2, 2, 2, 1, 8).transpose(0, 1, 4, 2, 3, 5, 6)
    return np.broadcast_to(x, x.shape[:5] + (4, 8)).reshape(a.shape[0], 512)


def _spread_rows(a):
    out = np.zeros((4, 4, 32, a.shape[1]), a.dtype)
    out[:, :, :8] = a.reshape(4, 4, 8, -1)
    return out.reshape(4, 128, -1).transpose(1, 0, 2).reshape(128, -1)


def _layouts(i):
    A = {n: np.asarray(v) for n, v in i.items()}
    cat = np.concatenate
    g = {}
    g["const"] = _constants()
    g["mods"] = {}
    for l in range(4):
        g["mods"][f"c{l}"] = A[f"L{l}_c"].T
        g["mods"][f"w{l}"] = A[f"L{l}_wmod"]
    turn0 = lambda a: a.reshape(8, 2, 2, 2, 64, -1).transpose(0, 1, 3, 2, 4, 5).reshape(4096, -1)
    wk = A["L0_attn_Wk"].reshape(8, 64, 128)
    bk = A["L0_attn_bk"].reshape(8, 64)
    g["l0a"] = {
        "wq": turn0(A["L0_attn_Wq"]).T, "wo": A["L0_attn_Wo"].T.reshape(32, 128, 128).transpose(1, 0, 2).reshape(128, 4096),
        "wk": cat([wk, wk], 1).reshape(1024, 128).T, "wv": A["L0_attn_Wv"].T,
        "bq": turn0(A["L0_attn_bq"]).reshape(32, 128).T, "bk": cat([bk, bk], 1).T, "bv": _rows(A["L0_attn_bv"]),
        "bo": A["L0_attn_bo"], "sink": _rows(A["L0_attn_sinks"]),
    }
    wd = A["L0_ffn_w_down"]
    w2 = np.zeros((128, 8, 2, 128), np.float32)
    w2[0:64, :, 0] = wd[0::2].transpose(1, 0, 2)
    w2[64:128, :, 1] = wd[1::2].transpose(1, 0, 2)
    up = lambda a: a.transpose(1, 0, 2).reshape(128, -1)
    g["l0f"] = {
        "gk": A["L0_ffn_gate_kernel"], "gb": _rows(A["L0_ffn_gate_bias"]), "w1": up(A["L0_ffn_w_gate"]),
        "w3": up(A["L0_ffn_w_up"]), "w2": w2.reshape(128, 2048), "sw1": A["L0_ffn_sw_gate"],
        "sw3": A["L0_ffn_sw_up"], "sw2": A["L0_ffn_sw_down"],
    }
    pb = A["L1_ffn_phi_b"]
    g["l1f"] = {
        "phi": A["L1_ffn_phi_w"].T, "phib": _rows(pb), "phic": pb.reshape(16, 128).T, "ew": up(A["L1_ffn_expert_w"]),
    }
    eb = A["L1_ffn_expert_b"].reshape(16, 4, 1, 128)
    g["eb"] = {"eb": np.broadcast_to(eb, (16, 4, 32, 128)).reshape(16, 128, 128).transpose(1, 0, 2).reshape(128, 2048)}
    Bl = A["L2_attn_B_lora"]
    col = lambda n: A[n].reshape(-1)
    g["sm"] = {
        "wlat": cat([A["L1_attn_wq_lat"], A["L1_attn_wk_lat"], A["L1_attn_wv_lat"]], 1),
        "wq96": _spread(_put(96, 0, A["L1_attn_wq_heads"])), "wk96": _spread(_put(96, 32, A["L1_attn_wk_heads"])),
        "wv96": _put(96, 64, A["L1_attn_wv_heads"]), "wproj": _spread_rows(A["L1_attn_w_proj"]), "bproj": A["L1_attn_b_proj"],
        "miux": col("L2_attn_miu_x"), "lam": A["L2_attn_lambda_"].reshape(5, 128).T, "A": A["L2_attn_A_lora"],
        "B": cat([_put(128, 32 * f if f < 4 else 0, Bl[f]) for f in range(5)], 1),
        "tdmiu": col("L2_attn_td_miu"), "tdA": A["L2_attn_td_A"], "tdB": A["L2_attn_td_B"], "u": col("L2_attn_u"),
        "WrT": A["L2_attn_Wr"].T, "WkT": A["L2_attn_Wk"].T, "WvT": A["L2_attn_Wv"].T, "WgT": A["L2_attn_Wg"].T,
        "WoT": A["L2_attn_Wo"].T, "gam": _rows(A["L2_attn_gn_gamma"]), "bet": _rows(A["L2_attn_gn_beta"]),
        "q3": _spread(A["L3_attn_Wq"].T), "k3": _spread(A["L3_attn_Wk"].T), "v3": A["L3_attn_Wv"].T, "o3": _spread_rows(A["L3_attn_Wo"].T),
        "bq3": _spread(A["L3_attn_bq"][None]).reshape(4, 128).T, "bk3": _spread(A["L3_attn_bk"][None]).reshape(4, 128).T, "bv3": _rows(A["L3_attn_bv"]), "bo3": A["L3_attn_bo"],
    }
    tw = lambda a: a.transpose(2, 0, 1).reshape(128, -1)
    g["l2f"] = {
        "wg": A["L2_ffn_Wg"].T, "w1": tw(A["L2_ffn_W1"]), "b1": A["L2_ffn_b1"].T, "w3": tw(A["L2_ffn_W3"]),
        "b3": A["L2_ffn_b3"].T, "w2": tw(A["L2_ffn_W2"]), "b2": A["L2_ffn_b2"],
    }
    w2 = A["L3_ffn_W2"].reshape(8, 128, 2, 128)
    g["l3f"] = {
        "wg": A["L3_ffn_Wg"].T, "w1": tw(A["L3_ffn_W1"]), "w3": tw(A["L3_ffn_W3"]),
        "w2": w2.transpose(3, 0, 2, 1).reshape(128, 2048),
    }
    out = {n: _pack(PACKS[n], g[n]) for n in PACKS}
    out["x"] = A["L0_attn_x"].reshape(32, 128, 128).transpose(1, 0, 2).reshape(128, 4096)
    return out


def kernel(**inputs):
    import concourse.bacc as _bacc
    from concourse.bass_utils import run_bass_kernel_spmd as _run

    nc = _bacc.Bacc("TRN2", target_bir_lowering=False, num_devices=1)
    arrays, dram = {}, {}
    for name, a in _layouts(inputs).items():
        a = np.ascontiguousarray(a)
        arrays[f"in_{name}_dram"] = a
        dram[name] = nc.dram_tensor(f"in_{name}_dram", a.shape, F32, kind="ExternalInput").ap()
    out = nc.dram_tensor("out_0_dram", (NB, 256, 128), F32, kind="ExternalOutput").ap()
    program(nc, dram, out, PHASES)
    r = _run(nc, [arrays], core_ids=[0])
    return r.results[0]["out_0_dram"]
```
